# Optimizing a Trainium2 kernel written in Bass

```python
import numpy as np
import jax
import jax.numpy as jnp

def _softmax(x, axis=-1):
    return jax.nn.softmax(x, axis=axis)

def _gelu(x):
    return jax.nn.gelu(x, approximate=True)

def _silu(x):
    return jax.nn.silu(x)

def _sigmoid(x):
    return jax.nn.sigmoid(x)

def _layernorm(x, axis=-1, eps=1e-05):
    m = jnp.mean(x, axis=axis, keepdims=True)
    v = jnp.var(x, axis=axis, keepdims=True)
    return (x - m) / jnp.sqrt(v + eps)

def _scatter_add(tgt, idx, src, axis=0):
    return tgt.at[idx].add(src)

def _segment_sum(src, seg, n):
    return jax.ops.segment_sum(src, seg, n)
kernel_name = 'mk_gnn_preln_d4_gnn_r8_5e9af0'

def setup_inputs(seed: int=0):
    np.random.seed(seed)
    _w = jnp.asarray

    def _rec_inputs():
        import jax
        import jax.numpy as jnp
        _gk = jax.random.key(seed)
        x = -0.000202 + 1 * jax.random.normal(jax.random.fold_in(_gk, 1), (12500, 64), jnp.float32)
        src = jax.random.randint(jax.random.fold_in(_gk, 2), (200000,), 0, 12500, jnp.int32)
        dst = jax.random.randint(jax.random.fold_in(_gk, 3), (200000,), 0, 12500, jnp.int32)
        _o = jnp.argsort(dst, stable=True)
        src = src[_o]
        dst = dst[_o]
        edge_attr_32 = 0.000189758 + 1.00013 * jax.random.normal(jax.random.fold_in(_gk, 12), (200000, 32), jnp.float32)
        return (x, src, dst, edge_attr_32)
    x, src, dst, edge_attr_32 = _rec_inputs()

    def _L0_gnn_setup():
        import jax, jax.numpy as jnp
        import numpy as np
        N_NODES = 12500
        N_EDGES = 156250
        D_IN = 64
        H = 8
        HD = 8
        NEG_SLOPE = 0.2
        key = jax.random.key(seed)
        k1, k2, k3, k4, k5 = jax.random.split(key, 5)
        x = jax.random.normal(k1, (N_NODES, D_IN), dtype=jnp.float32)
        edge_indices = jax.random.randint(k2, (2, N_EDGES), 0, N_NODES)
        w_scale = np.sqrt(6.0 / (D_IN + HD)).astype(np.float32)
        a_scale = np.sqrt(6.0 / (2 * HD + 1)).astype(np.float32)
        W = jax.random.uniform(k3, (H * HD, D_IN), jnp.float32, -w_scale, w_scale)
        src_attn = jax.random.uniform(k4, (1, H, HD), jnp.float32, -a_scale, a_scale)
        dst_attn = jax.random.uniform(k5, (1, H, HD), jnp.float32, -a_scale, a_scale)
        return {'x': x, 'edge_indices': edge_indices, 'W': W, 'src_attn': src_attn, 'dst_attn': dst_attn}
    _L0_gnn_all = _L0_gnn_setup()
    _L0_gnn_in = {k: v for k, v in _L0_gnn_all.items() if k in ('W', 'src_attn', 'dst_attn')}
    del _L0_gnn_all

    def _L1_gnn_setup():
        import jax, jax.numpy as jnp
        import numpy as np
        N_NODES = 12500
        N_EDGES = 125000
        D = 64
        H = 128
        key = jax.random.key(seed)
        ks = jax.random.split(key, 12)
        x = jax.random.normal(ks[0], (N_NODES, D), dtype=jnp.float32)
        start = jax.random.randint(ks[1], (N_EDGES,), 0, N_NODES)
        end = jax.random.randint(ks[2], (N_EDGES,), 0, N_NODES)

        def w(k, fan_in, shape):
            return jax.random.normal(k, shape, dtype=jnp.float32) / jnp.sqrt(jnp.float32(fan_in))
        We1 = w(ks[3], 2 * D, (2 * D, H))
        be1 = jnp.zeros((H,), jnp.float32)
        We2 = w(ks[4], H, (H, 1))
        be2 = jnp.zeros((1,), jnp.float32)
        Wn1 = w(ks[5], 3 * D, (3 * D, H))
        bn1 = jnp.zeros((H,), jnp.float32)
        Wn2 = w(ks[6], H, (H, D))
        bn2 = jnp.zeros((D,), jnp.float32)
        return {'x': x, 'start': start, 'end': end, 'We1': We1, 'be1': be1, 'We2': We2, 'be2': be2, 'Wn1': Wn1, 'bn1': bn1, 'Wn2': Wn2, 'bn2': bn2}
    _L1_gnn_all = _L1_gnn_setup()
    _L1_gnn_in = {k: v for k, v in _L1_gnn_all.items() if k in ('We1', 'be1', 'We2', 'be2', 'Wn1', 'bn1', 'Wn2', 'bn2')}
    del _L1_gnn_all

    def _L2_gnn_setup():
        import jax, jax.numpy as jnp
        import numpy as np
        N = 6250
        E = 200000
        DIN = 64
        DH = 64
        DOUT = 64
        DE = 32

        def _segment_softmax(alpha, dst, n):
            m = jax.ops.segment_max(alpha, dst, num_segments=n)
            m = jnp.where(jnp.isfinite(m), m, 0.0)
            ex = jnp.exp(alpha - m[dst])
            s = jax.ops.segment_sum(ex, dst, num_segments=n)
            return ex / (s[dst] + 1e-16)

        def _transformer_conv(x, src, dst, edge_attr, Wq, bq, Wk, bk, Wv, bv, We, Ws, bs):
            d = Wq.shape[1]
            q = x @ Wq + bq
            k = x @ Wk + bk
            v = x @ Wv + bv
            e = edge_attr @ We
            k_j = k[src] + e
            alpha = jnp.sum(q[dst] * k_j, axis=-1) / jnp.sqrt(jnp.float32(d))
            a = _segment_softmax(alpha, dst, x.shape[0])
            msg = (v[src] + e) * a[:, None]
            agg = jax.ops.segment_sum(msg, dst, num_segments=x.shape[0])
            return agg + (x @ Ws + bs)
        key = jax.random.key(seed)
        ks = jax.random.split(key, 32)

        def w(k, i, o):
            return (jax.random.normal(k, (i, o), jnp.float32) / np.sqrt(i)).astype(jnp.float32)
        inp = {'x': jax.random.normal(ks[0], (N, DIN), jnp.float32), 'edge_index': jax.random.randint(ks[1], (2, E), 0, N, dtype=jnp.int32), 'flepe': jax.random.normal(ks[2], (E, DE), jnp.float32), 'Wq1': w(ks[3], DIN, DH), 'bq1': jnp.zeros((DH,), jnp.float32), 'Wk1': w(ks[4], DIN, DH), 'bk1': jnp.zeros((DH,), jnp.float32), 'Wv1': w(ks[5], DIN, DH), 'bv1': jnp.zeros((DH,), jnp.float32), 'We1': w(ks[6], DE, DH), 'Ws1': w(ks[7], DIN, DH), 'bs1': jnp.zeros((DH,), jnp.float32), 'Wq2': w(ks[8], DH, DOUT), 'bq2': jnp.zeros((DOUT,), jnp.float32), 'Wk2': w(ks[9], DH, DOUT), 'bk2': jnp.zeros((DOUT,), jnp.float32), 'Wv2': w(ks[10], DH, DOUT), 'bv2': jnp.zeros((DOUT,), jnp.float32), 'We2': w(ks[11], DE, DOUT), 'Ws2': w(ks[12], DH, DOUT), 'bs2': jnp.zeros((DOUT,), jnp.float32)}
        return inp
    _L2_gnn_all = _L2_gnn_setup()
    _L2_gnn_in = {k: v for k, v in _L2_gnn_all.items() if k in ('Wq1', 'bq1', 'Wk1', 'bk1', 'Wv1', 'bv1', 'We1', 'Ws1', 'bs1', 'Wq2', 'bq2', 'Wk2', 'bk2', 'Wv2', 'bv2', 'We2', 'Ws2', 'bs2')}
    del _L2_gnn_all

    def _L3_gnn_setup():
        import jax, jax.numpy as jnp
        import numpy as np
        N_NODES = 12500
        N_EDGES = 200000
        D = 64
        key = jax.random.key(seed)
        k1, k2, k3, k4 = jax.random.split(key, 4)
        x = jax.random.normal(k1, (N_NODES, D), dtype=jnp.float32)
        edge_index = jax.random.randint(k2, (2, N_EDGES), 0, N_NODES, dtype=jnp.int64)
        W = jax.random.normal(k3, (D, D), dtype=jnp.float32) * (1.0 / np.sqrt(D))
        b = jax.random.normal(k4, (D,), dtype=jnp.float32) * 0.01
        return {'x': x, 'edge_index': edge_index, 'W': W, 'b': b}
    _L3_gnn_all = _L3_gnn_setup()
    _L3_gnn_in = {k: v for k, v in _L3_gnn_all.items() if k in ('W', 'b')}
    del _L3_gnn_all
    return {'x': x, 'src': src, 'dst': dst, 'edge_attr_32': edge_attr_32, 'L0_gnn_W': _L0_gnn_in['W'], 'L0_gnn_src_attn': _L0_gnn_in['src_attn'], 'L0_gnn_dst_attn': _L0_gnn_in['dst_attn'], 'L1_gnn_We1': _L1_gnn_in['We1'], 'L1_gnn_be1': _L1_gnn_in['be1'], 'L1_gnn_We2': _L1_gnn_in['We2'], 'L1_gnn_be2': _L1_gnn_in['be2'], 'L1_gnn_Wn1': _L1_gnn_in['Wn1'], 'L1_gnn_bn1': _L1_gnn_in['bn1'], 'L1_gnn_Wn2': _L1_gnn_in['Wn2'], 'L1_gnn_bn2': _L1_gnn_in['bn2'], 'L2_gnn_Wq1': _L2_gnn_in['Wq1'], 'L2_gnn_bq1': _L2_gnn_in['bq1'], 'L2_gnn_Wk1': _L2_gnn_in['Wk1'], 'L2_gnn_bk1': _L2_gnn_in['bk1'], 'L2_gnn_Wv1': _L2_gnn_in['Wv1'], 'L2_gnn_bv1': _L2_gnn_in['bv1'], 'L2_gnn_We1': _L2_gnn_in['We1'], 'L2_gnn_Ws1': _L2_gnn_in['Ws1'], 'L2_gnn_bs1': _L2_gnn_in['bs1'], 'L2_gnn_Wq2': _L2_gnn_in['Wq2'], 'L2_gnn_bq2': _L2_gnn_in['bq2'], 'L2_gnn_Wk2': _L2_gnn_in['Wk2'], 'L2_gnn_bk2': _L2_gnn_in['bk2'], 'L2_gnn_Wv2': _L2_gnn_in['Wv2'], 'L2_gnn_bv2': _L2_gnn_in['bv2'], 'L2_gnn_We2': _L2_gnn_in['We2'], 'L2_gnn_Ws2': _L2_gnn_in['Ws2'], 'L2_gnn_bs2': _L2_gnn_in['bs2'], 'L3_gnn_W': _L3_gnn_in['W'], 'L3_gnn_b': _L3_gnn_in['b']}

def reference(x, src, dst, edge_attr_32, L0_gnn_W, L0_gnn_src_attn, L0_gnn_dst_attn, L1_gnn_We1, L1_gnn_be1, L1_gnn_We2, L1_gnn_be2, L1_gnn_Wn1, L1_gnn_bn1, L1_gnn_Wn2, L1_gnn_bn2, L2_gnn_Wq1, L2_gnn_bq1, L2_gnn_Wk1, L2_gnn_bk1, L2_gnn_Wv1, L2_gnn_bv1, L2_gnn_We1, L2_gnn_Ws1, L2_gnn_bs1, L2_gnn_Wq2, L2_gnn_bq2, L2_gnn_Wk2, L2_gnn_bk2, L2_gnn_Wv2, L2_gnn_bv2, L2_gnn_We2, L2_gnn_Ws2, L2_gnn_bs2, L3_gnn_W, L3_gnn_b):
    import jax
    import jax.numpy as jnp

    def _L0_gnn_ref(x, edge_indices, W, src_attn, dst_attn):
        import jax, jax.numpy as jnp
        import numpy as np
        N_NODES = 12500
        N_EDGES = 156250
        D_IN = 64
        H = 8
        HD = 8
        NEG_SLOPE = 0.2
        n = x.shape[0]
        row, col = (edge_indices[0], edge_indices[1])
        xp = (x @ W.T).reshape(n, H, HD)
        src_score = (xp * src_attn).sum(-1)
        dst_score = (xp * dst_attn).sum(-1)
        e = jax.nn.leaky_relu(src_score[row] + dst_score[col], negative_slope=NEG_SLOPE)
        m = jax.ops.segment_max(e, row, num_segments=n)
        ex = jnp.exp(e - m[row])
        den = jax.ops.segment_sum(ex, row, num_segments=n)
        alpha = ex / den[row]
        vals = xp[col] * alpha[:, :, None]
        out = jax.ops.segment_sum(vals, row, num_segments=n)
        return out.reshape(n, H * HD)

    def _L1_gnn_ref(x, start, end, We1, be1, We2, be2, Wn1, bn1, Wn2, bn2):
        import jax, jax.numpy as jnp
        import numpy as np
        N_NODES = 12500
        N_EDGES = 125000
        D = 64
        H = 128
        n = x.shape[0]
        xs = x[start]
        edge_inputs = jnp.concatenate([xs, x[end]], axis=1)
        h = jax.nn.relu(edge_inputs @ We1 + be1)
        e = jax.nn.sigmoid(h @ We2 + be2)
        m = e * xs
        m_sum = jax.ops.segment_sum(m, end, num_segments=n)
        m_max = jax.ops.segment_max(m, end, num_segments=n)
        m_max = jnp.where(jnp.isneginf(m_max), jnp.float32(0.0), m_max)
        messages = jnp.concatenate([m_max, m_sum], axis=-1)
        node_inputs = jnp.concatenate([messages, x], axis=1)
        h2 = jax.nn.relu(node_inputs @ Wn1 + bn1)
        x_out = h2 @ Wn2 + bn2 + x
        return x_out

    def _L2_gnn_ref(x, edge_index, flepe, Wq1, bq1, Wk1, bk1, Wv1, bv1, We1, Ws1, bs1, Wq2, bq2, Wk2, bk2, Wv2, bv2, We2, Ws2, bs2):
        import jax, jax.numpy as jnp
        import numpy as np
        N = 6250
        E = 200000
        DIN = 64
        DH = 64
        DOUT = 64
        DE = 32

        def _segment_softmax(alpha, dst, n):
            m = jax.ops.segment_max(alpha, dst, num_segments=n)
            m = jnp.where(jnp.isfinite(m), m, 0.0)
            ex = jnp.exp(alpha - m[dst])
            s = jax.ops.segment_sum(ex, dst, num_segments=n)
            return ex / (s[dst] + 1e-16)

        def _transformer_conv(x, src, dst, edge_attr, Wq, bq, Wk, bk, Wv, bv, We, Ws, bs):
            d = Wq.shape[1]
            q = x @ Wq + bq
            k = x @ Wk + bk
            v = x @ Wv + bv
            e = edge_attr @ We
            k_j = k[src] + e
            alpha = jnp.sum(q[dst] * k_j, axis=-1) / jnp.sqrt(jnp.float32(d))
            a = _segment_softmax(alpha, dst, x.shape[0])
            msg = (v[src] + e) * a[:, None]
            agg = jax.ops.segment_sum(msg, dst, num_segments=x.shape[0])
            return agg + (x @ Ws + bs)
        src, dst = (edge_index[0], edge_index[1])
        h = _transformer_conv(x, src, dst, flepe, Wq1, bq1, Wk1, bk1, Wv1, bv1, We1, Ws1, bs1)
        h = jax.nn.relu(h)
        out = _transformer_conv(h, src, dst, flepe, Wq2, bq2, Wk2, bk2, Wv2, bv2, We2, Ws2, bs2)
        return out

    def _L3_gnn_ref(x, edge_index, W, b):
        import jax, jax.numpy as jnp
        import numpy as np
        N_NODES = 12500
        N_EDGES = 200000
        D = 64
        row, col = (edge_index[0], edge_index[1])
        n = x.shape[0]
        deg = jax.ops.segment_sum(jnp.ones(col.shape[0], dtype=x.dtype), col, num_segments=n)
        deg_inv_sqrt = jnp.where(deg > 0, jax.lax.rsqrt(jnp.maximum(deg, 1)), jnp.zeros_like(deg))
        norm = deg_inv_sqrt[row] * deg_inv_sqrt[col]
        h = x @ W.T + b
        msg = h[row] * norm[:, None]
        out = jax.ops.segment_sum(msg, col, num_segments=n)
        return out
    edge_index = jnp.stack([src, dst])
    h = jnp.maximum(_layernorm(x, axis=-1), 0.0)
    x = x + _L0_gnn_ref(h, edge_index, L0_gnn_W, L0_gnn_src_attn, L0_gnn_dst_attn)
    h = jnp.maximum(_layernorm(x, axis=-1), 0.0)
    x = x + _L1_gnn_ref(h, src, dst, L1_gnn_We1, L1_gnn_be1, L1_gnn_We2, L1_gnn_be2, L1_gnn_Wn1, L1_gnn_bn1, L1_gnn_Wn2, L1_gnn_bn2)
    h = jnp.maximum(_layernorm(x, axis=-1), 0.0)
    x = x + _L2_gnn_ref(h, edge_index, edge_attr_32, L2_gnn_Wq1, L2_gnn_bq1, L2_gnn_Wk1, L2_gnn_bk1, L2_gnn_Wv1, L2_gnn_bv1, L2_gnn_We1, L2_gnn_Ws1, L2_gnn_bs1, L2_gnn_Wq2, L2_gnn_bq2, L2_gnn_Wk2, L2_gnn_bk2, L2_gnn_Wv2, L2_gnn_bv2, L2_gnn_We2, L2_gnn_Ws2, L2_gnn_bs2)
    h = jnp.maximum(_layernorm(x, axis=-1), 0.0)
    x = x + _L3_gnn_ref(h, edge_index, L3_gnn_W, L3_gnn_b)
    return x

_drawn_inputs = setup_inputs


def setup_inputs(seed=0):
    import zlib

    import numpy as np

    out = dict(_drawn_inputs(seed))
    spreads = {'L1_gnn_be1': (0.0, 0.355),
     'L1_gnn_bn1': (0.0, 0.322),
     'L1_gnn_bn2': (0.0, 0.1),
     'L2_gnn_bq1': (0.0, 0.522),
     'L2_gnn_bk1': (0.0, 0.8),
     'L2_gnn_bv1': (0.0, 0.1),
     'L2_gnn_bs1': (0.0, 0.1),
     'L2_gnn_bq2': (0.0, 0.565),
     'L2_gnn_bk2': (0.0, 0.8),
     'L2_gnn_bv2': (0.0, 0.1),
     'L2_gnn_bs2': (0.0, 0.1)}
    factors = {'L3_gnn_b': 8.0}
    for name, (base, spread) in spreads.items():
        noise = np.random.default_rng([zlib.crc32(name.encode()), seed]).standard_normal(out[name].shape)
        drawn = base * np.exp(spread * noise) if base else spread * noise
        out[name] = jnp.asarray(drawn.astype(out[name].dtype))
    for name, factor in factors.items():
        out[name] = (out[name] * factor).astype(out[name].dtype)
    return out
```

```python
import numpy as np
import concourse.bass as bass
from concourse import mybir
from concourse.alu_op_type import AluOpType as ALU
from contextlib import ExitStack

F32 = mybir.dt.float32
BF16 = mybir.dt.bfloat16
I32 = mybir.dt.int32
ACT = mybir.ActivationFunctionType
AX = mybir.AxisListType.X

P = 128
N_NODES = 12500
N_EDGES = 200000
NT = 98
NN = NT * P
ET = 1568
NE = ET * P
G = 8
NGRP = ET // G
RB, NB = 98, 16
NG = 7
NNG = NT // NG
BIG = 3.0e38
EPS = 1e-5
D = 64


class Count:

    def __init__(self, sem):
        self.sem, self.base = sem, 0

    def at(self, n):
        return n + self.base

    def passed(self, n):
        self.base += n


class Chain:

    def __init__(self, eng, count, per=0, i=0):
        self.eng, self.count, self.per, self.i, self.n = eng, count, per, i, 0

    def link(self, ins):
        self.n += 1
        ins.then_inc(self.count.sem, 1)
        self.eng.wait_ge(self.count.sem, self.count.at(self.n) if self.per == 0 else self.i * self.per + self.count.at(self.n))

    def close(self):
        assert self.per == 0 or self.n == self.per, self.n


class Program:
    def __init__(self, nc, ctx):
        self.nc, self.ctx, self.counts, self.uses = nc, ctx, {}, {}

    def fresh(self, name):
        self.uses[name] = self.uses.get(name, 0) + 1
        return name if self.uses[name] == 1 else f"{name}_{self.uses[name]}"

    def count(self, name):
        if name not in self.counts:
            self.counts[name] = Count(self.ctx.enter_context(self.nc.semaphore(name)))
        return self.counts[name]

    def sb(self, name, shape, dt=F32, ctx=None):
        return (ctx or self.ctx).enter_context(self.nc.sbuf_tensor(self.fresh(name), shape, dt))

    def ps(self, name, shape, ctx, dt=F32):
        return ctx.enter_context(self.nc.psum_tensor(self.fresh(name), shape, dt))

    def dram(self, name, shape, dt=F32):
        return self.nc.dram_tensor(name, shape, dt, kind="Internal").ap()


def constants(pr, C):
    nc = pr.nc
    s = pr.count("const_made")
    C.ident = pr.sb("ident", [P, P])
    C.before = pr.sb("before", [P, P])
    C.after = pr.sb("after", [P, P])
    C.iota = pr.sb("iota", [P, P])
    C.ones = pr.sb("ones", [P, P])
    C.zeros = pr.sb("zeros", [P, 1])
    with nc.Block() as block:
        @block.gpsimd
        def _(gp):
            gp.memset(C.ident[:, :], 0.0).then_inc(s.sem, 1)
            gp.memset(C.zeros[:, :], 0.0).then_inc(s.sem, 1)
            gp.memset(C.ones[:, :], 1.0).then_inc(s.sem, 1)
            gp.memset(C.before[:, :], 1.0).then_inc(s.sem, 1)
            gp.memset(C.after[:, :], 1.0).then_inc(s.sem, 1)
            gp.iota(C.iota[:, :], [[1, P]], base=0, channel_multiplier=0,
                    allow_small_or_imprecise_dtypes=True).then_inc(s.sem, 1)
            gp.wait_ge(s.sem, 6)
            gp.affine_select(out=C.ident[:, :], in_=C.ident[:, :], compare_op=ALU.not_equal, fill=1.0, base=0,
                             pattern=[[-1, P]], channel_multiplier=1).then_inc(s.sem, 1)
            gp.affine_select(out=C.before[:, :], in_=C.before[:, :], compare_op=ALU.is_gt, fill=0.0, base=0,
                             pattern=[[1, P]], channel_multiplier=-1).then_inc(s.sem, 1)
            gp.affine_select(out=C.after[:, :], in_=C.after[:, :], compare_op=ALU.is_gt, fill=0.0, base=0,
                             pattern=[[-1, P]], channel_multiplier=1).then_inc(s.sem, 1)
            gp.wait_ge(s.sem, 9)


def zero_heads(pr, C):
    nc = pr.nc
    with ExitStack() as ctx:
        z = pr.sb("zero_rows", [P, 8192], ctx=ctx)
        made, done = pr.count("zeros_made"), pr.count("zeros_written")
        n = 0
        with nc.Block() as block:
            @block.vector
            def _(v):
                v.memset(z[:, :], 0.0).then_inc(made.sem, 1)

            @block.sync
            def _(sp):
                n = 0
                sp.wait_ge(made.sem, 1)
                for buf, w in ((C.heads8, 8), (C.heads64, 64), (C.heads128, 128)):
                    flat = buf.rearrange("(q p r) w -> q p (r w)", p=P, q=w // 4 if w > 8 else 2)
                    for q in range(flat.shape[0]):
                        sp.dma_start(flat[q], z[:, 0:flat.shape[2]]).then_inc(done.sem, 16)
                        n += 16
                sp.wait_ge(done.sem, n)


def block_at(b):
    return (b // 4) * 512 + (b % 4) * RB


def blocks(ps):
    return ps[:, :].rearrange("p (k c) -> p k c", k=4)[:, :, 0:4 * RB]


def by_bank(ap):
    return ap.rearrange("p (k c) -> p k c", k=4)


def read_ids(pr, C):
    nc = pr.nc
    with ExitStack() as ctx:
        raw = [pr.sb(f"ids_raw{j}", [RB, NB, P], I32, ctx) for j in range(2)]
        rowf = [pr.sb(f"ids_rowf{j}", [RB, NB, P], F32, ctx) for j in range(2)]
        fk = pr.sb("ids_fk", [RB, NB, P + 1], F32, ctx)
        pair = pr.sb("ids_pair", [P, ET, 2], F32, ctx)
        colf = pr.sb("ids_colf", [P, ET], F32, ctx)
        coli = pr.sb("ids_coli", [P, ET], I32, ctx)
        digit = pr.sb("ids_digit", [P, ET], I32, ctx)
        ps = [pr.ps(f"ids_ps{j}", [P, 2048], ctx) for j in range(2)]
        ld, cv, tr, dv, st = (pr.count(n) for n in ("ids_loaded", "ids_converted", "ids_turned", "ids_dve", "ids_stored"))
        ready = {}
        with nc.Block() as block:
            @block.sync
            def _(sp):
                for j, a in enumerate((C.dst, C.src)):
                    sp.dma_start(raw[j][:, :, :], a.rearrange("(b r c) -> r b c", r=RB, c=P)).then_inc(ld.sem, 16)

            @block.vector
            def _(v):
                ch = Chain(v, dv)
                v.wait_ge(ld.sem, 32)
                for j in range(2):
                    v.tensor_copy(rowf[j][:, :, :], raw[j][:, :, :]).then_inc(cv.sem, 1)
                v.wait_ge(cv.sem, 2)
                ch.link(v.memset(fk[:, :, :], -BIG))
                ch.link(v.tensor_tensor(fk[:, :, 1:P], rowf[0][:, :, 1:P], rowf[0][:, :, 0:P - 1], ALU.not_equal))
                ch.link(v.tensor_scalar(fk[:, :, 1:P], fk[:, :, 1:P], -BIG, None, ALU.mult))
                ready["fk"] = ch.n
                for j, (lo, hi) in enumerate(((C.lo_d, C.hi_d), (C.lo_s, C.hi_s))):
                    v.wait_ge(tr.sem, j + 1)
                    dest = C.seg_sb if j == 0 else colf
                    ch.link(v.tensor_copy(by_bank(dest[:, :]), blocks(ps[j])))
                    ch.link(v.tensor_copy(pair[:, :, j], dest[:, :]))
                    ch.link(v.tensor_copy(coli[:, :], dest[:, :]))
                    ch.link(v.tensor_scalar(digit[:, :], coli[:, :], P - 1, None, ALU.bitwise_and))
                    ch.link(v.tensor_copy(lo[:, :], digit[:, :]))
                    ch.link(v.tensor_scalar(digit[:, :], coli[:, :], 7, None, ALU.arith_shift_right))
                    ch.link(v.tensor_copy(hi[:, :], digit[:, :]))
                ready["all"] = ch.n

            @block.tensor
            def _(pe):
                pe.wait_ge(cv.sem, 2)
                for j in range(2):
                    for b in range(NB):
                        ins = pe.transpose(ps[j][:, block_at(b):block_at(b) + RB], rowf[j][:, b, :], C.ident[0:RB, 0:RB])
                    ins.then_inc(tr.sem, 1)

            @block.scalar
            def _(act):
                act.wait_ge(dv.sem, ready["fk"])
                act.dma_start(C.fk_dst.rearrange("(b r) c -> r b c", r=RB), fk[:, :, :]).then_inc(st.sem, 16)
                act.wait_ge(dv.sem, ready["all"])
                act.dma_start(C.pairs, pair[:, :, :].rearrange("p t j -> p (t j)")).then_inc(st.sem, 16)
                act.dma_start(C.src_col_i, coli[:, :]).then_inc(st.sem, 16)
                act.dma_start(C.dst_col, C.seg_sb[:, :]).then_inc(st.sem, 16)
                act.dma_start(C.src_col, colf[:, :]).then_inc(st.sem, 16)
                act.wait_ge(st.sem, 80)


def count_nodes(pr, C):
    nc = pr.nc
    with ExitStack() as ctx:
        low = [[pr.sb(f"hist_low{j}{k}", [P, G, P], BF16, ctx) for k in range(2)] for j in range(2)]
        high = [[pr.sb(f"hist_high{j}{k}", [P, G, NT], BF16, ctx) for k in range(2)] for j in range(2)]
        zero = pr.sb("hist_zero", [P, P], BF16, ctx)
        tot = pr.sb("hist_tot", [P, NT], F32, ctx)
        run = pr.sb("hist_run", [P, NT], F32, ctx)
        tmp = pr.sb("hist_tmp", [P, NT], F32, ctx)
        hist = [pr.ps(f"hist_ps{j}", [P, 512], ctx) for j in range(2)]
        pre = pr.ps("hist_pre", [P, 512], ctx)
        zr, onehot, used, summed, copied, dv = (pr.count(n) for n in (
            "hist_zero", "hist_onehot", "hist_used", "hist_summed", "hist_copied", "hist_dve"))
        digits = ((C.lo_d, C.hi_d), (C.lo_s, C.hi_s))
        with nc.Block() as block:
            @block.vector
            def _(v):
                v.memset(zero[:, :], 0.0).then_inc(zr.sem, 1)
                with v.Fori(0, NGRP // 2) as i:
                    for k in range(2):
                        g = 2 * i + k
                        v.wait_ge(used.sem, g + 1)
                        for j, (lo, hi) in enumerate(digits):
                            v.tensor_tensor(low[j][k][:, :, :], C.iota[:, :].unsqueeze(1).to_broadcast([P, G, P]),
                                            lo[:, bass.ds(G * g, G)].unsqueeze(2).to_broadcast([P, G, P]), ALU.is_equal)
                            ins = v.tensor_tensor(high[j][k][:, :, :], C.iota[:, 0:NT].unsqueeze(1).to_broadcast([P, G, NT]),
                                                  hi[:, bass.ds(G * g, G)].unsqueeze(2).to_broadcast([P, G, NT]), ALU.is_equal)
                        ins.then_inc(onehot.sem, 1)
                ch = Chain(v, dv)
                v.wait_ge(summed.sem, 1)
                for j, (cnt, start) in enumerate(((C.cnt_d, C.start_d), (C.cnt_s, C.start_s))):
                    ch.link(v.tensor_copy(cnt[:, :], hist[j][:, 0:NT]))
                    v.sem_inc(copied.sem, 1)
                    v.wait_ge(summed.sem, j + 2)
                    ch.link(v.tensor_copy(tot[:, :], pre[:, NT:2 * NT]))
                    ch.link(v.tensor_tensor_scan(run[:, :], C.ones[:, 0:NT], tot[:, :], 0.0, ALU.mult, ALU.add))
                    ch.link(v.tensor_tensor(run[:, :], run[:, :], tot[:, :], ALU.subtract))
                    ch.link(v.tensor_tensor(start[:, :], pre[:, 0:NT], run[:, :], ALU.add))

            @block.tensor
            def _(pe):
                pe.wait_ge(zr.sem, 1)
                pe.sem_inc(used.sem, 2)
                for j in range(2):
                    pe.matmul(hist[j][:, 0:NT], zero[:, :], zero[:, 0:NT], start=True, stop=False, skip_group_check=True)
                with pe.Fori(0, NGRP // 2) as i:
                    for k in range(2):
                        pe.wait_ge(onehot.sem, 2 * i + (k + 1))
                        for j in range(2):
                            for t in range(G):
                                ins = pe.matmul(hist[j][:, 0:NT], low[j][k][:, t, :], high[j][k][:, t, :],
                                                start=False, stop=False, skip_group_check=True)
                        ins.then_inc(used.sem, 1)
                for j in range(2):
                    ins = pe.matmul(hist[j][:, 0:NT], zero[:, :], zero[:, 0:NT], start=False, stop=True, skip_group_check=True)
                ins.then_inc(summed.sem, 1)
                for j, cnt in enumerate((C.cnt_d, C.cnt_s)):
                    pe.wait_ge(dv.sem, 1 + 5 * j)
                    pe.matmul(pre[:, 0:NT], C.before[:, :], cnt[:, :], start=True, stop=True)
                    pe.matmul(pre[:, NT:2 * NT], C.ones[:, :], cnt[:, :], start=True, stop=True).then_inc(summed.sem, 1)


def sort_by_src(pr, C):
    nc = pr.nc
    with ExitStack() as ctx:
        sb, pscope = (lambda n, s, d=F32: pr.sb("rank_" + n, s, d, ctx)), (lambda n, s, d=F32: pr.ps("rank_" + n, s, ctx, d))
        seg = [sb(f"seg{k}", [P, G]) for k in range(2)]
        pair = [sb(f"pair{k}", [P, G, 2]) for k in range(2)]
        place = [sb(f"place{k}", [P, G], I32) for k in range(2)]
        low = sb("low", [P, G, P], BF16)
        high = sb("high", [P, G, NT], BF16)
        lowT = sb("lowT", [P, G, P])
        identb = sb("identb", [P, P], BF16)
        sofar = [sb(f"sofar{n}", [P, NT]) for n in range(2)]
        earlier = sb("earlier", [P, G, P])
        picked = sb("picked", [P, G, NT])
        rank = sb("rank", [P, G])
        base = sb("base", [P, G])
        row_ps = pscope("row_ps", [P, 1024])
        lowT_ps = pscope("lowT_ps", [P, 1024], BF16)
        total = pscope("total", [P, 512])
        pick_ps = pscope("pick_ps", [P, 1024])
        ident_made, load, placed, scattered, rowed, onehot, lowed, turned, snap, counted, dv, done = (
            pr.count("rank_" + n) for n in ("ident", "load", "placed", "scattered", "rowed", "onehot", "lowed", "turned",
                                            "snap", "counted", "dve", "done"))
        gate = pr.count("pool_gate")
        load = [pr.count(f"rank_load{k}") for k in range(2)]
        scattered = [pr.count(f"rank_scattered{k}") for k in range(2)]
        with nc.Block() as block:
            @block.sync
            def _(sp):
                def load_group(g, k):
                    sp.dma_start(seg[k][:, :], C.src_col[:, bass.ds(G * g, G)]).then_inc(load[k].sem, 16)
                    sp.dma_start(pair[k][:, :, :].rearrange("p t j -> p (t j)"),
                                 C.pairs[:, bass.ds(2 * G * g, 2 * G)]).then_inc(load[k].sem, 16)

                for k in range(2):
                    load_group(k, k)
                with sp.Fori(0, NGRP // 2 - 1) as i:
                    for k in range(2):
                        sp.wait_ge(scattered[k].sem, i * (16 * G) + 16 * G)
                        load_group(2 * i + (k + 2), k)

            @block.gpsimd
            def _(gp):
                with gp.Fori(0, NGRP // 2) as i:
                    for k in range(2):
                        gp.wait_ge(placed.sem, 2 * i + (k + 1))
                        gp.sem_inc(gate.sem, 1)
                        for t in range(G):
                            gp.indirect_dma_start(C.sorted_pairs, bass.IndirectOffsetOnAxis(ap=place[k][:, t:t + 1], axis=0),
                                                  pair[k][:, t, :], None).then_inc(scattered[k].sem, 16)
                for k in range(2):
                    gp.wait_ge(scattered[k].sem, (NGRP // 2) * 16 * G)

            @block.vector
            def _(v):
                v.tensor_copy(identb[:, :], C.ident[:, :]).then_inc(ident_made.sem, 1)
                with v.Fori(0, NGRP // 2) as i:
                    for k in range(2):
                        g = 2 * i + k
                        ch = Chain(v, dv, 6, g)
                        v.wait_ge(counted.sem, g * G + 1)
                        v.tensor_tensor(low[:, :, :], C.iota[:, :].unsqueeze(1).to_broadcast([P, G, P]),
                                        C.lo_s[:, bass.ds(G * g, G)].unsqueeze(2).to_broadcast([P, G, P]), ALU.is_equal)
                        v.tensor_tensor(high[:, :, :], C.iota[:, 0:NT].unsqueeze(1).to_broadcast([P, G, NT]),
                                        C.hi_s[:, bass.ds(G * g, G)].unsqueeze(2).to_broadcast([P, G, NT]), ALU.is_equal).then_inc(onehot.sem, 1)
                        v.wait_ge(load[k].sem, i * 32 + 32)
                        v.wait_ge(rowed.sem, g + 1)
                        ch.link(v.tensor_tensor(earlier[:, :, :], row_ps[:, :].rearrange("p (t e) -> p t e", t=G),
                                                seg[k][:, :].unsqueeze(2).to_broadcast([P, G, P]), ALU.is_equal))
                        ch.link(v.tensor_tensor(earlier[:, :, :], earlier[:, :, :],
                                                C.after[:, :].unsqueeze(1).to_broadcast([P, G, P]), ALU.mult))
                        ch.link(v.tensor_reduce(rank[:, :], earlier[:, :, :], AX, ALU.add))
                        v.wait_ge(counted.sem, g * G + (G + 1))
                        v.wait_ge(onehot.sem, g + 1)
                        ch.link(v.tensor_tensor(picked[:, :, :].rearrange("p (a b) c -> p a (b c)", a=2),
                                                pick_ps[:, :].rearrange("p (a c) -> p a c", a=2)[:, :, 0:4 * NT],
                                                high[:, :, :].rearrange("p (a b) c -> p a (b c)", a=2), ALU.mult))
                        ch.link(v.tensor_reduce(base[:, :], picked[:, :, :], AX, ALU.add))
                        ch.link(v.tensor_tensor(place[k][:, :], base[:, :], rank[:, :], ALU.add))
                        v.sem_inc(placed.sem, 1)
                        ch.close()

            @block.tensor
            def _(pe):
                pe.wait_ge(ident_made.sem, 1)
                pe.matmul(total[:, 0:NT], C.ident[:, :], C.start_s[:, :], start=True, stop=True,
                          skip_group_check=True).then_inc(counted.sem, 1)
                with pe.Fori(0, NGRP // 2) as i:
                    for k in range(2):
                        g = 2 * i + k
                        pe.wait_ge(load[k].sem, i * 32 + 32)
                        pe.wait_ge(onehot.sem, g + 1)
                        for t in range(G):
                            ins = pe.transpose(row_ps[:, t * P:(t + 1) * P], seg[k][:, t:t + 1].to_broadcast([P, P]), C.ident[:, :])
                        ins.then_inc(rowed.sem, 1)
                        for t in range(G):
                            ins = pe.transpose(lowT_ps[:, t * P:(t + 1) * P], low[:, t, :], identb[:, :])
                        ins.then_inc(lowed.sem, 1)
                        pe.wait_ge(turned.sem, g + 1)
                        for t in range(G):
                            at = (t // 4) * 512 + (t % 4) * NT
                            pe.wait_ge(snap.sem, g * G + (t + 1))
                            pe.matmul(pick_ps[:, at:at + NT], lowT[:, t, :], sofar[t % 2][:, :], start=True, stop=True)
                            pe.matmul(total[:, 0:NT], low[:, t, :], high[:, t, :], start=False, stop=True,
                                      skip_group_check=True).then_inc(counted.sem, 1)

            @block.scalar
            def _(act):
                with act.Fori(0, NGRP // 2) as i:
                    for k in range(2):
                        g = 2 * i + k
                        act.wait_ge(lowed.sem, g + 1)
                        act.activation(lowT[:, :, :].rearrange("p t e -> p (t e)"), lowT_ps[:, :], ACT.Copy).then_inc(turned.sem, 1)
                        for t in range(G):
                            act.wait_ge(counted.sem, g * G + (t + 1))
                            act.activation(sofar[t % 2][:, :], total[:, 0:NT], ACT.Copy).then_inc(snap.sem, 1)


def read_sorted(pr, C):
    nc = pr.nc
    with ExitStack() as ctx:
        raw = pr.sb("srt_raw", [RB, NB, P, 2], F32, ctx)
        rowf = [pr.sb(f"srt_rowf{j}", [RB, NB, P], F32, ctx) for j in range(2)]
        fk = pr.sb("srt_fk", [RB, NB, P + 1], F32, ctx)
        colf = pr.sb("srt_colf", [P, ET], F32, ctx)
        coli = pr.sb("srt_coli", [P, ET], I32, ctx)
        ps = [pr.ps(f"srt_ps{j}", [P, 2048], ctx) for j in range(2)]
        ld, tr, dv, st = (pr.count(n) for n in ("srt_loaded", "srt_turned", "srt_dve", "srt_stored"))
        with nc.Block() as block:
            @block.sync
            def _(sp):
                sp.dma_start(raw[:, :, :, :].rearrange("r b c j -> r b (c j)"),
                             C.sorted_pairs.rearrange("(b r c) j -> r b (c j)", r=RB, c=P)).then_inc(ld.sem, 16)

            @block.vector
            def _(v):
                ch = Chain(v, dv)
                v.wait_ge(ld.sem, 16)
                for j in range(2):
                    ch.link(v.tensor_copy(rowf[j][:, :, :], raw[:, :, :, j]))
                ch.link(v.memset(fk[:, :, :], -BIG))
                ch.link(v.tensor_tensor(fk[:, :, 1:P], rowf[1][:, :, 1:P], rowf[1][:, :, 0:P - 1], ALU.not_equal))
                ch.link(v.tensor_scalar(fk[:, :, 1:P], fk[:, :, 1:P], -BIG, None, ALU.mult))
                v.wait_ge(tr.sem, 1)
                v.tensor_copy(by_bank(coli[:, :]), blocks(ps[0]))
                ch.link(v.tensor_copy(by_bank(colf[:, :]), blocks(ps[1])))

            @block.tensor
            def _(pe):
                pe.wait_ge(dv.sem, 2)
                for j in range(2):
                    for b in range(NB):
                        ins = pe.transpose(ps[j][:, block_at(b):block_at(b) + RB], rowf[j][:, b, :], C.ident[0:RB, 0:RB])
                ins.then_inc(tr.sem, 1)

            @block.scalar
            def _(act):
                act.wait_ge(dv.sem, 5)
                for h in range(8):
                    act.dma_start(C.fk_src.rearrange("(b r) h c -> r b h c", r=RB)[:, :, h, :], fk[:, :, :]).then_inc(st.sem, 16)
                act.wait_ge(dv.sem, 6)
                act.dma_start(C.dst_of_sorted, coli[:, :]).then_inc(st.sem, 16)
                act.dma_start(C.src_sorted_col, colf[:, :]).then_inc(st.sem, 16)
                act.wait_ge(st.sem, 160)


def node_bounds(pr, C):
    nc = pr.nc
    with ExitStack() as ctx:
        f = [pr.sb(f"nb_f{j}", [P, NT], F32, ctx) for j in range(4)]
        n = [pr.sb(f"nb_i{j}", [P, NT], I32, ctx) for j in range(4)]
        out_i = [pr.sb(f"nb_out{j}", [P, NT], I32, ctx) for j in range(6)]
        dv, st = pr.count("bounds_dve"), pr.count("bounds_stored")
        with nc.Block() as block:
            @block.vector
            def _(v):
                ch = Chain(v, dv)
                for j, (cnt, start, has, spans) in enumerate(((C.cnt_d, C.start_d, C.has_d, C.spans_d),
                                                              (C.cnt_s, C.start_s, C.has_s, C.spans_s))):
                    ch.link(v.tensor_scalar(has[:, :], cnt[:, :], 0.5, None, ALU.is_gt))
                    ch.link(v.tensor_tensor(f[0][:, :], start[:, :], cnt[:, :], ALU.add))
                    ch.link(v.tensor_scalar(f[0][:, :], f[0][:, :], -1.0, 0.0, ALU.add, ALU.max))
                    ch.link(v.tensor_copy(out_i[3 * j + 1][:, :], f[0][:, :]))
                    ch.link(v.tensor_scalar(n[0][:, :], out_i[3 * j + 1][:, :], 7, None, ALU.arith_shift_right))
                    ch.link(v.tensor_copy(f[1][:, :], n[0][:, :]))
                    ch.link(v.tensor_copy(n[1][:, :], start[:, :]))
                    ch.link(v.tensor_scalar(n[2][:, :], n[1][:, :], 7, None, ALU.arith_shift_right))
                    ch.link(v.tensor_copy(f[2][:, :], n[2][:, :]))
                    ch.link(v.tensor_tensor(spans[:, :], f[1][:, :], f[2][:, :], ALU.is_gt))
                    ch.link(v.tensor_tensor(spans[:, :], spans[:, :], has[:, :], ALU.mult))
                    ch.link(v.tensor_scalar(f[1][:, :], f[1][:, :], -1.0, 0.0, ALU.add, ALU.max))
                    ch.link(v.tensor_copy(out_i[3 * j + 2][:, :], f[1][:, :]))
                    ch.link(v.tensor_scalar(f[3][:, :], has[:, :], -float(NE), float(NE), ALU.mult, ALU.add))
                    ch.link(v.tensor_tensor(f[3][:, :], f[3][:, :], start[:, :], ALU.add))
                    ch.link(v.tensor_copy(out_i[3 * j][:, :], f[3][:, :]))

            @block.sync
            def _(sp):
                sp.wait_ge(dv.sem, 32)
                for j, rows in enumerate((C.ix_dst, C.ix_src)):
                    for q in range(3):
                        sp.dma_start(rows[q], out_i[3 * j + q][:, :]).then_inc(st.sem, 16)
                sp.wait_ge(st.sem, 96)


def tile_starts(pr, C):
    nc = pr.nc
    with ExitStack() as ctx:
        last = [pr.sb(f"ts_last{j}", [P, ET], F32, ctx) for j in range(2)]
        first = [pr.sb(f"ts_first{j}", [RB, NB], F32, ctx) for j in range(2)]
        ld, dv, st = (pr.count(n) for n in ("starts_loaded", "starts_dve", "starts_stored"))
        with nc.Block() as block:
            @block.sync
            def _(sp):
                for j, col in enumerate((C.dst_col, C.src_sorted_col)):
                    sp.dma_start(last[j][:, :], col[P - 1:P, :].to_broadcast([P, ET])).then_inc(ld.sem, 16)
                    with nc.allow_non_contiguous_dma(reason="one word of each tile"):
                        sp.dma_start(first[j][:, :], col[0, :].rearrange("(b r) -> r b", r=RB)).then_inc(ld.sem, 16)

            @block.vector
            def _(v):
                ch = Chain(v, dv)
                v.wait_ge(ld.sem, 64)
                for j, (keep, idx) in enumerate(((C.keep_d, C.first_d), (C.keep_s, C.first_s))):
                    ch.link(v.memset(keep[:, 0:1], 0.0))
                    ch.link(v.tensor_tensor(keep[:, 1:ET], last[j][:, 1:ET], last[j][:, 0:ET - 1], ALU.is_equal))
                    ch.link(v.tensor_copy(idx[:, :], first[j][:, :]))


def head_rows(pr, C, tag, table, rows_dram, width, heads, bounds, first):
    nc = pr.nc
    with ExitStack() as ctx:
        rows = pr.sb("hr_rows", [RB, NB * width], F32, ctx)
        got, put = pr.count("hr_gathered"), pr.count("hr_written")
        with nc.Block() as block:
            @block.gpsimd
            def _(gp):
                for b in range(NB):
                    gp.indirect_dma_start(rows[:, b * width:(b + 1) * width], None, table,
                                          bass.IndirectOffsetOnAxis(ap=first[:, b:b + 1], axis=0)).then_inc(got.sem, 16)

            @block.sync
            def _(sp):
                sp.wait_ge(got.sem, got.at(16 * NB))
                sp.dma_start(heads.rearrange("(b r e) w -> r b e w", r=RB, e=P)[:, :, 0, :],
                             rows[:, :].rearrange("r (b w) -> r b w", w=width)).then_inc(put.sem, 16)
                sp.wait_ge(put.sem, put.at(16))
        got.passed(16 * NB)
        put.passed(16)


def layernorm_relu(pr, C, x, h):
    nc = pr.nc
    with ExitStack() as ctx:
        big = pr.sb("ln_big", [P, NT, D], F32, ctx)
        mean = pr.sb("ln_mean", [P, NT], F32, ctx)
        var = pr.sb("ln_var", [P, NT], F32, ctx)
        std = pr.sb("ln_std", [P, NT], F32, ctx)
        dv, sq = pr.count("ln_dve"), pr.count("ln_rooted")
        with nc.Block() as block:
            @block.vector
            def _(v):
                ch = Chain(v, dv)
                wide = lambda a: a[:, :].unsqueeze(2).to_broadcast([P, NT, D])
                ch.link(v.tensor_reduce(mean[:, :], x[:, :, :], AX, ALU.add))
                ch.link(v.tensor_scalar(mean[:, :], mean[:, :], 1.0 / D, None, ALU.mult))
                ch.link(v.tensor_tensor(h[:, :, :], x[:, :, :], wide(mean), ALU.subtract))
                ch.link(v.tensor_tensor(big[:, :, :], h[:, :, :], h[:, :, :], ALU.mult))
                ch.link(v.tensor_reduce(var[:, :], big[:, :, :], AX, ALU.add))
                ch.link(v.tensor_scalar(var[:, :], var[:, :], 1.0 / D, EPS, ALU.mult, ALU.add))
                v.wait_ge(sq.sem, sq.at(1))
                ch.link(v.reciprocal(std[:, :], std[:, :]))
                ch.link(v.tensor_tensor(h[:, :, :], h[:, :, :], wide(std), ALU.mult))
                ch.link(v.tensor_scalar(h[:, :, :], h[:, :, :], 0.0, None, ALU.max))

            @block.scalar
            def _(act):
                act.wait_ge(dv.sem, dv.at(6))
                act.activation(std[:, :], var[:, :], ACT.Sqrt).then_inc(sq.sem, 1)
        dv.passed(9)
        sq.passed(1)


def project(pr, C, h, weights, bias, tables, heads=None, keep=None, row_scale=None, scores=None):
    nc = pr.nc
    width = max(c + w.shape[1] for w, c in weights)
    total = width + (16 if scores else 0)
    pitch = 512 // (4 if width <= 128 else 2)
    with ExitStack() as ctx:
        w_sb = pr.sb("pj_w", [D + 1, width], F32, ctx)
        att = pr.sb("pj_att", [P, 2, D], F32, ctx)
        stage = pr.sb("pj_stage", [P, NG, D], F32, ctx)
        hT = pr.sb("pj_hT", [D + 1, NG * P], F32, ctx)
        res = pr.sb("pj_res", [P, NG, total], F32, ctx)
        tmp = pr.sb("pj_tmp", [P, NG, 2, D], F32, ctx)
        idx = pr.sb("pj_idx", [P, NG], I32, ctx)
        trp = pr.ps("pj_trp", [P, 1024], ctx)
        acc = pr.ps("pj_acc", [P, 4 * 512], ctx)
        ld, ini, staged, turned, moved, made, scored, stored, scat, ixl, gate, free = (
            pr.count("pj_" + n) for n in ("loaded", "ones", "staged", "turned", "moved", "made", "scored", "stored",
                                          "scattered", "index", "gate", "free"))
        turned2 = pr.count("pj_products")
        pe_gate = pr.count("pe_gate")
        nload = 16 * (len(weights) + len(bias) + (2 if scores else 0))
        nstore = 16 * len(tables)
        with nc.Block() as block:
            @block.sync
            def _(sp):
                for w, c in weights:
                    sp.dma_start(w_sb[0:D, c:c + w.shape[1]], w).then_inc(ld.sem, 16)
                sp.wait_ge(ini.sem, ini.at(2))
                for b, c in bias:
                    sp.dma_start(w_sb[D:D + 1, c:c + b.shape[0]], b.unsqueeze(0)).then_inc(ld.sem, 16)
                if scores:
                    for j, a in enumerate(scores):
                        sp.dma_start(att[:, j, :], a.rearrange("a h d -> a (h d)").to_broadcast([P, D])).then_inc(ld.sem, 16)
                with sp.Fori(0, NNG) as i:
                    if heads:
                        sp.wait_ge(free.sem, i + free.at(1))
                        sp.dma_start(idx[:, :], heads[4][:, bass.ds(NG * i, NG)]).then_inc(ixl.sem, 16)
                    sp.wait_ge(scored.sem, i + scored.at(1))
                    for n, (tab, c, wd) in enumerate(tables):
                        src = stage[:, :, :] if c is None else res[:, :, c:c + wd]
                        dst = tab[0] if isinstance(tab, tuple) else tab
                        at = tab[1] if isinstance(tab, tuple) else 0
                        sp.dma_start(dst.rearrange("(t p) w -> p t w", p=P)[:, bass.ds(NG * i, NG), at:at + wd], src)\
                            .then_inc(stored.sem, 16)
                    if heads:
                        sp.wait_ge(scat.sem, i * (16 * NG) + scat.at(16 * NG))
                    sp.wait_ge(stored.sem, i * nstore + stored.at(nstore))
                    sp.sem_inc(free.sem, 1)

            @block.gpsimd
            def _(gp):
                if heads:
                    with gp.Fori(0, NNG) as i:
                        gp.wait_ge(ixl.sem, i * 16 + ixl.at(16))
                        gp.wait_ge(scored.sem, i + scored.at(1))
                        gp.sem_inc(gate.sem, 1)
                        for t in range(NG):
                            gp.indirect_dma_start(heads[0], bass.IndirectOffsetOnAxis(ap=idx[:, t:t + 1], axis=0),
                                                  res[:, t, heads[2]:heads[2] + heads[3]], None,
                                                  bounds_check=NE - 1, oob_is_err=False).then_inc(scat.sem, 16)

            @block.vector
            def _(v):
                v.memset(hT[D:D + 1, :], 1.0).then_inc(ini.sem, 1)
                v.memset(w_sb[D:D + 1, :], 0.0).then_inc(ini.sem, 1)
                v.sem_inc(free.sem, 1)
                with v.Fori(0, NNG) as i:
                    v.wait_ge(free.sem, i + free.at(1))
                    v.tensor_copy(stage[:, :, :], h[:, bass.ds(NG * i, NG), :]).then_inc(staged.sem, 1)
                    v.wait_ge(made.sem, i + made.at(1))
                    if scores:
                        v.wait_ge(ld.sem, ld.at(nload))
                        for j in range(2):
                            v.tensor_tensor(tmp[:, :, j, :], res[:, :, 0:D], att[:, j, :].unsqueeze(1).to_broadcast([P, NG, D]), ALU.mult)\
                                .then_inc(turned2.sem, 1)
                        v.wait_ge(turned2.sem, i * 2 + turned2.at(2))
                        for j in range(2):
                            ins = v.tensor_reduce(res[:, :, D + 8 * j:D + 8 * j + 8],
                                                  tmp[:, :, j, :].rearrange("p t (h d) -> p t h d", h=8), AX, ALU.add)
                        ins.then_inc(scored.sem, 1)
                    else:
                        if row_scale is not None:
                            v.tensor_tensor(res[:, :, 0:D], res[:, :, 0:D],
                                            row_scale[:, bass.ds(NG * i, NG)].unsqueeze(2).to_broadcast([P, NG, D]), ALU.mult)\
                                .then_inc(scored.sem, 1)
                        elif keep is not None:
                            v.tensor_copy(keep[0][:, bass.ds(NG * i, NG), :], res[:, :, keep[1]:keep[1] + D]).then_inc(scored.sem, 1)
                        else:
                            v.sem_inc(scored.sem, 1)

            @block.tensor
            def _(pe):
                pe.wait_ge(ld.sem, ld.at(nload))
                pe.wait_ge(ini.sem, ini.at(2))
                with pe.Fori(0, NNG) as i:
                    pe.wait_ge(staged.sem, i + staged.at(1))
                    pe.sem_inc(pe_gate.sem, 1)
                    for t in range(NG):
                        ins = pe.transpose(trp[0:D, t * P:(t + 1) * P], stage[:, t, :], C.ident[:, :])
                    ins.then_inc(turned.sem, 1)
                    pe.wait_ge(moved.sem, i + moved.at(1))
                    for t in range(NG):
                        ins = pe.matmul(acc[:, t * pitch:t * pitch + width], hT[:, t * P:(t + 1) * P], w_sb[:, :], start=True, stop=True)
                    ins.then_inc(turned.sem, 1)

            @block.scalar
            def _(act):
                act.wait_ge(ini.sem, ini.at(1))
                with act.Fori(0, NNG) as i:
                    act.wait_ge(turned.sem, i * 2 + turned.at(1))
                    act.activation(hT[0:D, :], trp[0:D, 0:NG * P], ACT.Copy).then_inc(moved.sem, 1)
                    act.wait_ge(turned.sem, i * 2 + turned.at(2))
                    act.activation(res[:, :, 0:width], acc[:, 0:NG * pitch].rearrange("p (t c) -> p t c", t=NG)[:, :, 0:width],
                                   ACT.Copy).then_inc(made.sem, 1)
        ld.passed(nload)
        ini.passed(2)
        for c in (staged, moved, made, scored):
            c.passed(NNG)
        turned.passed(2 * NNG)
        free.passed(NNG + 1)
        stored.passed(nstore * NNG)
        if heads:
            scat.passed(16 * NG * NNG)
            ixl.passed(16 * NNG)
        if scores:
            turned2.passed(2 * NNG)



class EdgeIO:

    def __init__(self, pr, tag, ctx, loads, table, width, part, part_width):
        self.pr, self.table, self.width, self.part = pr, table, width, part
        self.slot = {n: [pr.sb(f"{tag}_{n}{k}", s, t, ctx) for k in range(2)] for n, s, t, _ in loads}
        self.loads = {n: f for n, _, _, f in loads}
        self.rows = [pr.sb(f"{tag}_rows{k}", [P, G, width], F32, ctx) for k in range(2)]
        self.out = [pr.sb(f"{tag}_out{k}", [P, G, part_width], F32, ctx) for k in range(2)]
        self.loaded = [pr.count(f"e_loaded{k}") for k in range(2)]
        self.gathered = [pr.count(f"e_gathered{k}") for k in range(2)]
        self.stored = [pr.count(f"e_stored{k}") for k in range(2)]
        self.done, self.free, self.gate = pr.count("e_done"), pr.count("e_out_free"), pr.count("e_gate")
        self.ready = pr.count("e_ready")
        self.per_load = 16 * sum(len(f) for f in self.loads.values())

    def sync(self, sp):
        def load_group(g, k):
            for n, parts in self.loads.items():
                for part, source in parts:
                    sp.dma_start(part(self.slot[n][k]), source(g)).then_inc(self.loaded[k].sem, 16)

        def store_group(g, i, k):
            view = self.part.rearrange("(t p) w -> p t w", p=P)
            sp.dma_start(view[:, bass.ds(G * g, G), :], self.out[k][:, :, :]).then_inc(self.stored[k].sem, 16)
            sp.wait_ge(self.stored[k].sem, i * 16 + self.stored[k].at(16))
            sp.sem_inc(self.free.sem, 1)

        for k in range(2):
            load_group(k, k)
        sp.sem_inc(self.free.sem, 2)
        with sp.Fori(0, NGRP // 2 - 1) as i:
            for k in range(2):
                sp.wait_ge(self.done.sem, 2 * i + self.done.at(k + 1))
                load_group(2 * i + (k + 2), k)
                store_group(2 * i + k, i, k)
        for k in range(2):
            sp.wait_ge(self.done.sem, self.done.at(NGRP - 1 + k))
            store_group(NGRP - 2 + k, NGRP // 2 - 1, k)

    def gather(self, gp):
        index = next(iter(self.slot))
        with gp.Fori(0, NGRP // 2) as i:
            for k in range(2):
                gp.wait_ge(self.loaded[k].sem, i * self.per_load + self.loaded[k].at(self.per_load))
                gp.sem_inc(self.gate.sem, 1)
                for t in range(G):
                    gp.indirect_dma_start(self.rows[k][:, t, :], None, self.table,
                                          bass.IndirectOffsetOnAxis(ap=self.slot[index][k][:, t:t + 1], axis=0))\
                        .then_inc(self.gathered[k].sem, 16)

    def wait_loaded(self, eng, i, k):
        eng.wait_ge(self.loaded[k].sem, i * self.per_load + self.loaded[k].at(self.per_load))

    def wait_gathered(self, eng, i, k):
        eng.wait_ge(self.gathered[k].sem, i * (16 * G) + self.gathered[k].at(16 * G))

    def wait_out_free(self, eng, g):
        eng.wait_ge(self.free.sem, g + self.free.at(1))

    def passed(self):
        for k in range(2):
            self.loaded[k].passed(self.per_load * (NGRP // 2))
            self.gathered[k].passed(16 * G * (NGRP // 2))
            self.stored[k].passed(16 * (NGRP // 2))
        self.done.passed(NGRP)
        self.free.passed(NGRP + 2)
        self.ready.passed(NGRP + 1)


def whole(a):
    return a[:, :]


def whole3(a):
    return a[:, :, :]


def tile_rows(rows):
    view = rows.rearrange("(t p) w -> p t w", p=P)
    return lambda g: view[:, bass.ds(G * g, G), :]


def common_loads(index_col, seg_col):
    return [("index", [P, G], I32, [(whole, lambda g: index_col[:, bass.ds(G * g, G)])]),
            ("seg", [P, G], F32, [(whole, lambda g: seg_col[:, bass.ds(G * g, G)])])]


def banked(ps, w):
    if G * w <= 512:
        return ps[:, 0:G * w].rearrange("p (a c) -> p a c", a=1), 1, lambda t: t * w
    return ps[:, :].rearrange("p (a c) -> p a c", a=2)[:, :, 0:4 * w], 2, lambda t: (t // 4) * 512 + (t % 4) * w


def softmax_edges(pr, C, tag, H, table, seg_col, index_col, heads, fk, part, edge_w=None):
    nc = pr.nc
    gat = H == 8
    HW = 8 if gat else D
    W = D + H
    NF = G * H if gat else G
    with ExitStack() as ctx:
        loads = common_loads(index_col, seg_col) + [
            ("heads", [P, G, HW], F32, [(whole3, tile_rows(heads))]),
            ("fk", [NF, P + 1], F32, [(whole, lambda g: fk[bass.ds(NF * g, NF), :])]),
        ]
        if not gat:
            loads.append(("attr", [P, G, 32], F32, [(whole3, tile_rows(C.edge_attr))]))
        io = EdgeIO(pr, tag, ctx, loads, table, D + 8 if gat else 2 * D, part, W + H)
        slots = io.slot
        same = pr.sb(f"{tag}_same", [P, G, P], F32, ctx)
        score = pr.sb(f"{tag}_score", [P, G, H], F32, ctx)
        leaky = pr.sb(f"{tag}_leaky", [P, G, H], F32, ctx)
        fwd = pr.sb(f"{tag}_fwd", [NF, P], F32, ctx)
        bwd = pr.sb(f"{tag}_bwd", [NF, P], F32, ctx)
        shifted = pr.sb(f"{tag}_shifted", [P, G, H], F32, ctx)
        vals = pr.sb(f"{tag}_vals", [P, G, W], F32, ctx)
        weight = pr.sb(f"{tag}_weight", [P, G, H], F32, ctx)
        row_ps = pr.ps(f"{tag}_row_ps", [P, G * P], ctx)
        small = pr.ps(f"{tag}_small", [P, 512], ctx)
        head_ps = pr.ps(f"{tag}_head_ps", [P, 512], ctx)
        sum_ps = pr.ps(f"{tag}_sum_ps", [P, 1024], ctx)
        if not gat:
            ew = pr.sb(f"{tag}_ew", [P, 4, D], F32, ctx)
            attrT = pr.sb(f"{tag}_attrT", [P, 2, P], F32, ctx)
            both = pr.sb(f"{tag}_both", [P, G, 2, D], F32, ctx)
            prod = pr.sb(f"{tag}_prod", [P, G, D], F32, ctx)
            attr_ps = pr.ps(f"{tag}_attr_ps", [P, 512], ctx)
            edge_ps = pr.ps(f"{tag}_edge_ps", [P, 512], ctx)
        sums, _, sum_at = banked(sum_ps, W)
        c = {n: pr.count("s_" + n) for n in ("rowed", "same", "spread", "scored", "turned", "peaked", "back", "shifted",
                                             "weighed", "valued", "summed", "dve", "act", "edge_w", "attr_turned",
                                             "attr_moved", "edged", "ew_loaded")}
        pe_gate = pr.count("pe_gate")
        dper = 4 if gat else 5
        with nc.Block() as block:
            @block.sync
            def _(sp):
                if not gat:
                    sp.wait_ge(c["edge_w"].sem, c["edge_w"].at(1))
                    for q in range(4):
                        sp.dma_start(ew[32 * q:32 * q + 32, q, :], edge_w).then_inc(c["ew_loaded"].sem, 16)
                io.sync(sp)

            @block.gpsimd
            def _(gp):
                io.gather(gp)

            @block.vector
            def _(v):
                if not gat:
                    v.memset(ew[:, :, :], 0.0).then_inc(c["edge_w"].sem, 1)
                with v.Fori(0, NGRP // 2) as i:
                    for k in range(2):
                        g = 2 * i + k
                        ch = Chain(v, c["dve"], dper, g)
                        rows, seg, fks = io.rows[k], slots["seg"][k], slots["fk"][k]
                        io.wait_loaded(v, i, k)
                        v.wait_ge(c["rowed"].sem, g + c["rowed"].at(1))
                        v.wait_ge(io.ready.sem, g + io.ready.at(1))
                        v.tensor_tensor(same[:, :, :], row_ps[:, :].rearrange("p (t e) -> p t e", t=G),
                                        seg[:, :].unsqueeze(2).to_broadcast([P, G, P]), ALU.is_equal).then_inc(c["same"].sem, 1)
                        io.wait_gathered(v, i, k)
                        if gat:
                            v.wait_ge(c["spread"].sem, g + c["spread"].at(1))
                            ch.link(v.tensor_tensor(score[:, :, :], rows[:, :, D:D + H],
                                                    head_ps[:, 0:G * H].rearrange("p (t h) -> p t h", t=G), ALU.add))
                            v.scalar_tensor_tensor(out=leaky[:, :, :], in0=score[:, :, :], scalar=0.2, in1=score[:, :, :],
                                                   op0=ALU.mult, op1=ALU.max).then_inc(c["scored"].sem, 1)
                        else:
                            v.wait_ge(c["edged"].sem, g + c["edged"].at(1))
                            ch.link(v.tensor_tensor(both[:, :, :, :], rows[:, :, :].rearrange("p t (j d) -> p t j d", j=2),
                                                    edge_ps[:, :].rearrange("p (t d) -> p t d", t=G).unsqueeze(2)
                                                    .to_broadcast([P, G, 2, D]), ALU.add))
                            v.wait_ge(c["spread"].sem, g + c["spread"].at(1))
                            ch.link(v.scalar_tensor_tensor(out=prod[:, :, :], in0=both[:, :, 0, :], scalar=float(D) ** -0.5,
                                                           in1=head_ps[:, :].rearrange("p (t d) -> p t d", t=G),
                                                           op0=ALU.mult, op1=ALU.mult))
                            v.tensor_reduce(leaky[:, :, :], prod[:, :, :], AX, ALU.add).then_inc(c["scored"].sem, 1)
                        v.wait_ge(c["turned"].sem, g + c["turned"].at(1))
                        v.tensor_tensor_scan(fwd[:, :], fks[:, 0:P], small[0:NF, 0:P], -BIG, ALU.add, ALU.max)
                        ch.link(v.tensor_tensor_scan(bwd[:, ::-1], fks[:, 1:P + 1][:, ::-1], small[0:NF, 0:P][:, ::-1], -BIG,
                                                     ALU.add, ALU.max))
                        ch.link(v.tensor_tensor(fwd[:, :], fwd[:, :], bwd[:, :], ALU.max))
                        v.sem_inc(c["peaked"].sem, 1)
                        v.wait_ge(c["back"].sem, g + c["back"].at(1))
                        v.tensor_tensor(shifted[:, :, :], leaky[:, :, :],
                                        small[:, P:P + G * H].rearrange("p (t h) -> p t h", t=G), ALU.subtract)\
                            .then_inc(c["shifted"].sem, 1)
                        v.wait_ge(c["weighed"].sem, g + c["weighed"].at(1))
                        v.tensor_copy(vals[:, :, D:D + H], weight[:, :, :])
                        if gat:
                            ch.link(v.tensor_tensor(vals[:, :, 0:D].rearrange("p t (h d) -> p t h d", h=H),
                                                    rows[:, :, 0:D].rearrange("p t (h d) -> p t h d", h=H),
                                                    weight[:, :, :].unsqueeze(3).to_broadcast([P, G, H, D // H]), ALU.mult))
                        else:
                            ch.link(v.tensor_tensor(vals[:, :, 0:D], both[:, :, 1, :],
                                                    weight[:, :, :].to_broadcast([P, G, D]), ALU.mult))
                        v.sem_inc(c["valued"].sem, 1)
                        ch.close()

            @block.tensor
            def _(pe):
                if not gat:
                    pe.wait_ge(c["ew_loaded"].sem, c["ew_loaded"].at(64))
                with pe.Fori(0, NGRP // 2) as i:
                    for k in range(2):
                        g = 2 * i + k
                        io.wait_loaded(pe, i, k)
                        for t in range(G):
                            ins = pe.transpose(row_ps[:, t * P:(t + 1) * P], slots["seg"][k][:, t:t + 1].to_broadcast([P, P]), C.ident[:, :])
                        ins.then_inc(c["rowed"].sem, 1)
                        if not gat:
                            for q in range(2):
                                ins = pe.transpose(attr_ps[:, q * P:(q + 1) * P],
                                                   slots["attr"][k][:, 4 * q:4 * q + 4, :].rearrange("p t c -> p (t c)"), C.ident[:, :])
                            ins.then_inc(c["attr_turned"].sem, 1)
                            pe.wait_ge(c["attr_moved"].sem, g + c["attr_moved"].at(1))
                            for q in range(2):
                                ins = pe.matmul(edge_ps[:, q * 256:(q + 1) * 256], attrT[:, q, :], ew[:, :, :].rearrange("p q d -> p (q d)"),
                                                start=True, stop=True)
                            ins.then_inc(c["edged"].sem, 1)
                        pe.wait_ge(c["same"].sem, g + c["same"].at(1))
                        for t in range(G):
                            ins = pe.matmul(head_ps[:, t * HW:(t + 1) * HW], same[:, t, :], slots["heads"][k][:, t, :], start=True, stop=True)
                        ins.then_inc(c["spread"].sem, 1)
                        pe.wait_ge(c["scored"].sem, g + c["scored"].at(1))
                        pe.wait_ge(io.ready.sem, g + io.ready.at(1))
                        pe.sem_inc(pe_gate.sem, 1)
                        pe.transpose(small[0:NF, 0:P], leaky[:, :, :].rearrange("p t h -> p (t h)"), C.ident[:, :]).then_inc(c["turned"].sem, 1)
                        pe.wait_ge(c["peaked"].sem, g + c["peaked"].at(1))
                        pe.sem_inc(pe_gate.sem, 1)
                        pe.transpose(small[:, P:P + NF], fwd[:, :], C.ident[0:NF, 0:NF]).then_inc(c["back"].sem, 1)
                        pe.wait_ge(c["valued"].sem, g + c["valued"].at(1))
                        for t in range(G):
                            ins = pe.matmul(sum_ps[:, sum_at(t):sum_at(t) + W], same[:, t, :], vals[:, t, :], start=True, stop=True)
                        ins.then_inc(c["summed"].sem, 1)

            @block.scalar
            def _(act):
                act.sem_inc(io.ready.sem, 1)
                with act.Fori(0, NGRP // 2) as i:
                    for k in range(2):
                        g = 2 * i + k
                        if not gat:
                            act.wait_ge(c["attr_turned"].sem, g + c["attr_turned"].at(1))
                            act.activation(attrT[:, :, :].rearrange("p q e -> p (q e)"), attr_ps[:, 0:2 * P], ACT.Copy)\
                                .then_inc(c["attr_moved"].sem, 1)
                        act.wait_ge(c["shifted"].sem, g + c["shifted"].at(1))
                        act.activation(weight[:, :, :], shifted[:, :, :], ACT.Exp).then_inc(c["weighed"].sem, 1)
                        io.wait_out_free(act, g)
                        act.activation(io.out[k][:, :, W:W + H], small[:, P:P + NF].rearrange("p (t h) -> p t h", t=G), ACT.Copy)\
                            .then_inc(c["act"].sem, 1)
                        act.wait_ge(c["summed"].sem, g + c["summed"].at(1))
                        act.activation(io.out[k][:, :, 0:W].rearrange("p (a b) w -> p a b w", a=sums.shape[1]),
                                       sums.rearrange("p a (b w) -> p a b w", w=W), ACT.Copy).then_inc(c["act"].sem, 1)
                        act.wait_ge(c["act"].sem, g * 2 + c["act"].at(2))
                        act.sem_inc(io.ready.sem, 1)
                        act.sem_inc(io.done.sem, 1)
        io.passed()
        for n in ("rowed", "same", "spread", "scored", "turned", "peaked", "back", "shifted", "weighed", "valued", "summed"):
            c[n].passed(NGRP)
        c["act"].passed(2 * NGRP)
        c["dve"].passed(dper * NGRP)
        if not gat:
            c["edge_w"].passed(1)
            c["ew_loaded"].passed(64)
            for n in ("attr_turned", "attr_moved", "edged"):
                c[n].passed(NGRP)


def mlp_edges(pr, C, table, heads, part, be2, We2):
    nc = pr.nc
    H2 = 2 * D
    tag = "m"
    with ExitStack() as ctx:
        def fk_of(par):
            view = C.fk_dst.rearrange("(g j two) c -> g two j c", two=2, j=G // 2)
            return lambda g: view[bass.ds(g, 1), par, :, 0:P].to_broadcast([D, G // 2, P])

        loads = common_loads(C.src_col_i, C.dst_col) + [
            ("heads", [P, G, H2], F32, [(whole3, tile_rows(heads))]),
            ("fk", [P, G // 2, P], F32, [(lambda a: a[0:D, :, :], fk_of(0)), (lambda a: a[D:P, :, :], fk_of(1))]),
        ]
        io = EdgeIO(pr, tag, ctx, loads, table, H2 + D, part, H2)
        slots = io.slot
        same = pr.sb("m_same", [P, G, P], F32, ctx)
        hidden = pr.sb("m_hidden", [P, G, H2], F32, ctx)
        logit = pr.sb("m_logit", [P, G], F32, ctx)
        gate = pr.sb("m_gate", [P, G], F32, ctx)
        msg = pr.sb("m_msg", [P, G, D], F32, ctx)
        top = pr.sb("m_top", [P, G // 2 * P], F32, ctx)
        w2 = pr.sb("m_w2", [P, H2], F32, ctx)
        b2 = pr.sb("m_b2", [P, 1], F32, ctx)
        row_ps = pr.ps("m_row_ps", [P, G * P], ctx)
        head_ps = pr.ps("m_head_ps", [P, G * H2], ctx)
        sum_ps = pr.ps("m_sum_ps", [P, 512], ctx)
        msgT_ps = pr.ps("m_msgT_ps", [P, 512], ctx)
        top_ps = pr.ps("m_top_ps", [P, 512], ctx)
        c = {n: pr.count("s_" + n) for n in ("rowed", "same", "spread", "scored", "turned", "peaked", "back",
                                             "weighed", "valued", "summed", "dve", "act", "edge_w")}
        with nc.Block() as block:
            @block.sync
            def _(sp):
                sp.dma_start(w2[:, :], We2.rearrange("k a -> a k").to_broadcast([P, H2])).then_inc(c["edge_w"].sem, 16)
                sp.dma_start(b2[:, :], be2.unsqueeze(0).to_broadcast([P, 1])).then_inc(c["edge_w"].sem, 16)
                io.sync(sp)

            @block.gpsimd
            def _(gp):
                io.gather(gp)

            @block.vector
            def _(v):
                v.wait_ge(c["edge_w"].sem, c["edge_w"].at(32))
                with v.Fori(0, NGRP // 2) as i:
                    for k in range(2):
                        g = 2 * i + k
                        ch = Chain(v, c["dve"], 2, g)
                        rows, seg = io.rows[k], slots["seg"][k]
                        io.wait_loaded(v, i, k)
                        v.wait_ge(c["rowed"].sem, g + c["rowed"].at(1))
                        v.wait_ge(io.ready.sem, g + io.ready.at(1))
                        v.tensor_tensor(same[:, :, :], row_ps[:, :].rearrange("p (t e) -> p t e", t=G),
                                        seg[:, :].unsqueeze(2).to_broadcast([P, G, P]), ALU.is_equal).then_inc(c["same"].sem, 1)
                        io.wait_gathered(v, i, k)
                        v.wait_ge(c["spread"].sem, g + c["spread"].at(1))
                        ch.link(v.tensor_tensor(hidden[:, :, :], rows[:, :, 0:H2],
                                                head_ps[:, :].rearrange("p (t w) -> p t w", t=G), ALU.add))
                        ch.link(v.scalar_tensor_tensor(out=hidden[:, :, :], in0=hidden[:, :, :], scalar=0.0,
                                                       in1=w2[:, :].unsqueeze(1).to_broadcast([P, G, H2]), op0=ALU.max, op1=ALU.mult))
                        v.tensor_reduce(logit[:, :], hidden[:, :, :], AX, ALU.add).then_inc(c["scored"].sem, 1)
                        v.wait_ge(c["weighed"].sem, g + c["weighed"].at(1))
                        v.tensor_tensor(msg[:, :, :], rows[:, :, H2:H2 + D], gate[:, :].unsqueeze(2).to_broadcast([P, G, D]),
                                        ALU.mult).then_inc(c["valued"].sem, 1)
                        v.wait_ge(c["turned"].sem, g + c["turned"].at(1))
                        v.tensor_tensor_scan(top[:, :], slots["fk"][k][:, :, :].rearrange("p j e -> p (j e)"), msgT_ps[:, :],
                                             -BIG, ALU.add, ALU.max).then_inc(c["peaked"].sem, 1)
                        ch.close()

            @block.tensor
            def _(pe):
                with pe.Fori(0, NGRP // 2) as i:
                    for k in range(2):
                        g = 2 * i + k
                        io.wait_loaded(pe, i, k)
                        for t in range(G):
                            ins = pe.transpose(row_ps[:, t * P:(t + 1) * P], slots["seg"][k][:, t:t + 1].to_broadcast([P, P]), C.ident[:, :])
                        ins.then_inc(c["rowed"].sem, 1)
                        pe.wait_ge(c["same"].sem, g + c["same"].at(1))
                        for t in range(G):
                            ins = pe.matmul(head_ps[:, t * H2:(t + 1) * H2], same[:, t, :], slots["heads"][k][:, t, :], start=True, stop=True)
                        ins.then_inc(c["spread"].sem, 1)
                        pe.wait_ge(c["valued"].sem, g + c["valued"].at(1))
                        pe.wait_ge(io.ready.sem, g + io.ready.at(1))
                        for j in range(G // 2):
                            ins = pe.transpose(msgT_ps[:, j * P:(j + 1) * P], msg[:, 2 * j:2 * j + 2, :].rearrange("p t d -> p (t d)"), C.ident[:, :])
                        ins.then_inc(c["turned"].sem, 1)
                        for t in range(G):
                            ins = pe.matmul(sum_ps[:, t * D:(t + 1) * D], same[:, t, :], msg[:, t, :], start=True, stop=True)
                        ins.then_inc(c["summed"].sem, 1)
                        pe.wait_ge(c["peaked"].sem, g + c["peaked"].at(1))
                        for j in range(G // 2):
                            ins = pe.transpose(top_ps[:, j * P:(j + 1) * P], top[:, j * P:(j + 1) * P], C.ident[:, :])
                        ins.then_inc(c["back"].sem, 1)

            @block.scalar
            def _(act):
                act.wait_ge(c["edge_w"].sem, c["edge_w"].at(32))
                act.sem_inc(io.ready.sem, 1)
                with act.Fori(0, NGRP // 2) as i:
                    for k in range(2):
                        g = 2 * i + k
                        act.wait_ge(c["scored"].sem, g + c["scored"].at(1))
                        act.activation(gate[:, :], logit[:, :], ACT.Sigmoid, bias=b2[:, :]).then_inc(c["weighed"].sem, 1)
                        io.wait_out_free(act, g)
                        act.wait_ge(c["summed"].sem, g + c["summed"].at(1))
                        act.activation(io.out[k][:, :, 0:D], sum_ps[:, :].rearrange("p (t d) -> p t d", t=G), ACT.Copy).then_inc(c["act"].sem, 1)
                        act.wait_ge(c["back"].sem, g + c["back"].at(1))
                        act.activation(io.out[k][:, :, D:H2], top_ps[:, :].rearrange("p (t d) -> p t d", t=G), ACT.Copy).then_inc(c["act"].sem, 1)
                        act.wait_ge(c["act"].sem, g * 2 + c["act"].at(2))
                        act.sem_inc(io.ready.sem, 1)
                        act.sem_inc(io.done.sem, 1)
        io.passed()
        for n in ("rowed", "same", "spread", "scored", "turned", "peaked", "back", "weighed", "valued", "summed"):
            c[n].passed(NGRP)
        c["act"].passed(2 * NGRP)
        c["dve"].passed(2 * NGRP)
        c["edge_w"].passed(32)


def gcn_edges(pr, C, table, part):
    nc = pr.nc
    with ExitStack() as ctx:
        io = EdgeIO(pr, "g", ctx, common_loads(C.src_col_i, C.dst_col), table, D, part, D)
        slots = io.slot
        same = [pr.sb(f"g_same{k}", [P, G, P], F32, ctx) for k in range(2)]
        row_ps = pr.ps("g_row_ps", [P, G * P], ctx)
        sum_ps = pr.ps("g_sum_ps", [P, 512], ctx)
        c = {n: pr.count("s_" + n) for n in ("rowed", "same", "summed", "act")}
        with nc.Block() as block:
            @block.sync
            def _(sp):
                io.sync(sp)

            @block.gpsimd
            def _(gp):
                io.gather(gp)

            @block.vector
            def _(v):
                with v.Fori(0, NGRP // 2) as i:
                    for k in range(2):
                        g = 2 * i + k
                        io.wait_loaded(v, i, k)
                        v.wait_ge(c["rowed"].sem, g + c["rowed"].at(1))
                        v.tensor_tensor(same[k][:, :, :], row_ps[:, :].rearrange("p (t e) -> p t e", t=G),
                                        slots["seg"][k][:, :].unsqueeze(2).to_broadcast([P, G, P]), ALU.is_equal)\
                            .then_inc(c["same"].sem, 1)

            @block.tensor
            def _(pe):
                with pe.Fori(0, NGRP // 2) as i:
                    for k in range(2):
                        g = 2 * i + k
                        io.wait_loaded(pe, i, k)
                        for t in range(G):
                            ins = pe.transpose(row_ps[:, t * P:(t + 1) * P], slots["seg"][k][:, t:t + 1].to_broadcast([P, P]), C.ident[:, :])
                        ins.then_inc(c["rowed"].sem, 1)
                        pe.wait_ge(c["same"].sem, g + c["same"].at(1))
                        io.wait_gathered(pe, i, k)
                        pe.wait_ge(io.ready.sem, g + io.ready.at(1))
                        for t in range(G):
                            ins = pe.matmul(sum_ps[:, t * D:(t + 1) * D], same[k][:, t, :], io.rows[k][:, t, :], start=True, stop=True)
                        ins.then_inc(c["summed"].sem, 1)

            @block.scalar
            def _(act):
                act.sem_inc(io.ready.sem, 1)
                with act.Fori(0, NGRP // 2) as i:
                    for k in range(2):
                        g = 2 * i + k
                        io.wait_out_free(act, g)
                        act.wait_ge(c["summed"].sem, g + c["summed"].at(1))
                        act.activation(io.out[k][:, :, :], sum_ps[:, :].rearrange("p (t d) -> p t d", t=G), ACT.Copy).then_inc(c["act"].sem, 1)
                        act.wait_ge(c["act"].sem, g + c["act"].at(1))
                        act.sem_inc(io.ready.sem, 1)
                        act.sem_inc(io.done.sem, 1)
        io.passed()
        for n in ("rowed", "same", "summed", "act"):
            c[n].passed(NGRP)


def carry(pr, C, kind, part, carry_dram, keep, H=0):
    nc = pr.nc
    soft = kind == "softmax"
    W = {"sum": D, "sum_max": 2 * D, "softmax": D + H}[kind]
    with ExitStack() as ctx:
        t_rows = pr.sb("c_rows", [RB, NB, W + H], F32, ctx)
        wide = pr.sb("c_wide", [RB, NB, W], F32, ctx)
        n = [pr.sb(f"c_buf{j}", [P, ET], F32, ctx) for j in range(6 if soft else 3)]
        back = pr.sb("c_back", [RB, NB, 2 * W if soft else W], F32, ctx)
        ps = [pr.ps(f"c_ps{j}", [P, 2048], ctx) for j in range(2)]
        ld, dv, tr, ex, st = (pr.count("c_" + x) for x in ("loaded", "dve", "turned", "exp", "stored"))
        marks = {}
        with nc.Block() as block:
            @block.sync
            def _(sp):
                sp.dma_start(t_rows[:, :, :], part.rearrange("(b r e) w -> r b e w", r=RB, e=P)[:, :, P - 1, :]).then_inc(ld.sem, 16)

            @block.vector
            def _(v):
                ch = Chain(v, dv)
                v.wait_ge(ld.sem, ld.at(16))
                if soft:
                    ch.link(v.tensor_copy(wide[:, :, 0:D].rearrange("r b (h d) -> r b h d", h=H),
                                          t_rows[:, :, W:W + H].unsqueeze(3).to_broadcast([RB, NB, H, D // H])))
                    ch.link(v.tensor_copy(wide[:, :, D:W], t_rows[:, :, W:W + H]))
                marks["wide"] = ch.n
                v.wait_ge(tr.sem, tr.at(1))
                val, pen = n[0], n[1]
                ch.link(v.tensor_scalar(pen[:, :], keep[:, :], BIG, -BIG, ALU.mult, ALU.add))
                ch.link(v.tensor_copy(by_bank(val[0:W, :]), blocks(ps[0])[0:W]))
                if kind == "sum":
                    ch.link(v.tensor_tensor_scan(n[2][0:W, :], keep[0:W, :], val[0:W, :], 0.0, ALU.mult, ALU.add))
                elif kind == "sum_max":
                    ch.link(v.tensor_tensor_scan(n[2][0:D, :], keep[0:D, :], val[0:D, :], 0.0, ALU.mult, ALU.add))
                    ch.link(v.tensor_tensor_scan(n[2][D:W, :], pen[D:W, :], val[D:W, :], -BIG, ALU.add, ALU.max))
                else:
                    top, peak, ratio = n[2], n[3], n[4]
                    ch.link(v.tensor_copy(by_bank(top[0:W, :]), blocks(ps[1])[0:W]))
                    ch.link(v.tensor_tensor_scan(peak[0:W, :], pen[0:W, :], top[0:W, :], -BIG, ALU.add, ALU.max))
                    ch.link(v.memset(ratio[0:W, 0:1], 0.0))
                    ch.link(v.tensor_tensor(ratio[0:W, 1:ET], peak[0:W, 0:ET - 1], peak[0:W, 1:ET], ALU.subtract))
                    ch.link(v.tensor_scalar(ratio[0:W, :], ratio[0:W, :], 0.0, None, ALU.min))
                    ch.link(v.tensor_tensor(top[0:W, :], top[0:W, :], peak[0:W, :], ALU.subtract))
                    marks["exp"] = ch.n
                    v.wait_ge(ex.sem, ex.at(2))
                    ch.link(v.tensor_tensor(ratio[0:W, :], ratio[0:W, :], keep[0:W, :], ALU.mult))
                    ch.link(v.tensor_tensor(val[0:W, :], val[0:W, :], top[0:W, :], ALU.mult))
                    ch.link(v.tensor_tensor_scan(n[5][0:W, :], ratio[0:W, :], val[0:W, :], 0.0, ALU.mult, ALU.add))
                marks["scanned"] = ch.n
                v.wait_ge(tr.sem, tr.at(2))
                for j in range(2 if soft else 1):
                    ch.link(v.tensor_copy(back[:, :, j * W:(j + 1) * W], ps[j][0:RB, :].rearrange("r (b w) -> r b w", b=NB)[:, :, 0:W]))
                marks["back"] = ch.n

            @block.tensor
            def _(pe):
                pe.wait_ge(ld.sem, ld.at(16))
                if soft:
                    pe.wait_ge(dv.sem, dv.at(marks["wide"]))
                for j in range(2 if soft else 1):
                    for b in range(NB):
                        ins = pe.transpose(ps[j][0:W, block_at(b):block_at(b) + RB], t_rows[:, b, 0:W] if j == 0 else wide[:, b, :],
                                           C.ident[0:RB, 0:RB])
                ins.then_inc(tr.sem, 1)
                pe.wait_ge(dv.sem, dv.at(marks["scanned"]))
                res = (n[5], n[3]) if soft else (n[2],)
                for j, r in enumerate(res):
                    for b in range(NB):
                        ins = pe.transpose(ps[j][0:RB, b * P:b * P + W], r[0:W, b * RB:(b + 1) * RB], C.ident[0:W, 0:W])
                ins.then_inc(tr.sem, 1)

            @block.scalar
            def _(act):
                if soft:
                    act.wait_ge(dv.sem, dv.at(marks["exp"]))
                    act.activation(n[4][0:W, :], n[4][0:W, :], ACT.Exp).then_inc(ex.sem, 1)
                    act.activation(n[2][0:W, :], n[2][0:W, :], ACT.Exp).then_inc(ex.sem, 1)
                act.wait_ge(dv.sem, dv.at(marks["back"]))
                act.dma_start(carry_dram.rearrange("(b r) w -> r b w", r=RB), back[:, :, :]).then_inc(st.sem, 16)
                act.wait_ge(st.sem, st.at(16))
        ld.passed(16)
        dv.passed(marks["back"])
        tr.passed(2)
        st.passed(16)
        if soft:
            ex.passed(2)


def node_results(pr, C, kind, part, carry_dram, ix, has, spans, result, H=0, eps=0.0):
    nc = pr.nc
    soft = kind == "softmax"
    W = {"sum": D, "sum_max": 2 * D, "softmax": D + H}[kind]
    PW, CW = W + H, 2 * W if soft else W
    with ExitStack() as ctx:
        index = [pr.sb(f"n_index{k}", [P, 2, NG], I32, ctx) for k in range(2)]
        own = [pr.sb(f"n_own{k}", [P, NG, PW], F32, ctx) for k in range(2)]
        old = [pr.sb(f"n_old{k}", [P, NG, CW], F32, ctx) for k in range(2)]
        pen = pr.sb("n_pen", [P, NG], F32, ctx)
        top = pr.sb("n_top", [P, NG, max(H, 1)], F32, ctx)
        dif = pr.sb("n_dif", [P, NG, 2, max(H, 1)], F32, ctx)
        mul = pr.sb("n_mul", [P, NG, 2, max(H, 1)], F32, ctx)
        acc = pr.sb("n_acc", [P, NG, W], F32, ctx)
        ld = [pr.count(f"n_loaded{k}") for k in range(2)]
        got = [pr.count(f"n_gathered{k}") for k in range(2)]
        done, dv, ask, ex, gate = (pr.count("n_" + x) for x in ("done", "dve", "asked", "exp", "gate"))
        per = 12 if soft else {"sum": 3, "sum_max": 5}[kind]
        with nc.Block() as block:
            @block.sync
            def _(sp):
                def load(g, k):
                    for q in range(2):
                        sp.dma_start(index[k][:, q, :], ix[1 + q][:, bass.ds(NG * g, NG)]).then_inc(ld[k].sem, 16)
                for k in range(2):
                    load(k, k)
                with sp.Fori(0, NNG // 2 - 1) as i:
                    for k in range(2):
                        sp.wait_ge(done.sem, 2 * i + done.at(k + 1))
                        load(2 * i + (k + 2), k)

            @block.gpsimd
            def _(gp):
                with gp.Fori(0, NNG // 2) as i:
                    for k in range(2):
                        gp.wait_ge(ld[k].sem, i * 32 + ld[k].at(32))
                        gp.sem_inc(gate.sem, 1)
                        for q, (rows, src) in enumerate(((own[k], part), (old[k], carry_dram))):
                            for t in range(NG):
                                gp.indirect_dma_start(rows[:, t, :], None, src,
                                                      bass.IndirectOffsetOnAxis(ap=index[k][:, q, t:t + 1], axis=0)).then_inc(got[k].sem, 16)

            @block.vector
            def _(v):
                with v.Fori(0, NNG // 2) as i:
                    for k in range(2):
                        g = 2 * i + k
                        ch = Chain(v, dv, per, g)
                        tiles = bass.ds(NG * g, NG)
                        over = lambda m, w: m[:, tiles].unsqueeze(2).to_broadcast([P, NG, w])
                        v.wait_ge(got[k].sem, i * (32 * NG) + got[k].at(32 * NG))
                        o, c = own[k], old[k]
                        if not soft:
                            ch.link(v.tensor_tensor(c[:, :, 0:D], c[:, :, 0:D], over(spans, D), ALU.mult))
                            ch.link(v.tensor_tensor(o[:, :, 0:D], o[:, :, 0:D], c[:, :, 0:D], ALU.add))
                            if kind == "sum_max":
                                ch.link(v.tensor_tensor(c[:, :, D:W], c[:, :, D:W], over(spans, D), ALU.mult))
                                ch.link(v.tensor_tensor(o[:, :, D:W], o[:, :, D:W], c[:, :, D:W], ALU.max))
                            ch.link(v.tensor_tensor(result[:, tiles, :], o[:, :, :], over(has, W), ALU.mult))
                        else:
                            ch.link(v.tensor_scalar(pen[:, :], spans[:, tiles], BIG, -BIG, ALU.mult, ALU.add))
                            cm = c[:, :, W + D:W + D + H]
                            ch.link(v.tensor_tensor(cm, cm, pen[:, :].unsqueeze(2).to_broadcast([P, NG, H]), ALU.add))
                            ch.link(v.tensor_tensor(top[:, :, :], o[:, :, W:W + H], cm, ALU.max))
                            ch.link(v.tensor_tensor(dif[:, :, 0, :], o[:, :, W:W + H], top[:, :, :], ALU.subtract))
                            ch.link(v.tensor_tensor(dif[:, :, 1, :], cm, top[:, :, :], ALU.subtract))
                            v.sem_inc(ask.sem, 1)
                            v.wait_ge(ex.sem, g + ex.at(1))
                            for q, rows in enumerate((o, c)):
                                v.tensor_tensor(rows[:, :, 0:D].rearrange("p t (h d) -> p t h d", h=H),
                                                rows[:, :, 0:D].rearrange("p t (h d) -> p t h d", h=H),
                                                mul[:, :, q, :].unsqueeze(3).to_broadcast([P, NG, H, D // H]), ALU.mult)
                                ch.link(v.tensor_tensor(rows[:, :, D:W], rows[:, :, D:W], mul[:, :, q, :], ALU.mult))
                            ch.link(v.tensor_tensor(acc[:, :, :], o[:, :, 0:W], c[:, :, 0:W], ALU.add))
                            ch.link(v.tensor_scalar(acc[:, :, D:W], acc[:, :, D:W], eps, None, ALU.add))
                            ch.link(v.reciprocal(acc[:, :, D:W], acc[:, :, D:W]))
                            ch.link(v.tensor_tensor(acc[:, :, D:W], acc[:, :, D:W], over(has, H), ALU.mult))
                            ch.link(v.tensor_tensor(result[:, tiles, :].rearrange("p t (h d) -> p t h d", h=H),
                                                    acc[:, :, 0:D].rearrange("p t (h d) -> p t h d", h=H),
                                                    acc[:, :, D:W].unsqueeze(3).to_broadcast([P, NG, H, D // H]), ALU.mult))
                        v.sem_inc(done.sem, 1)
                        ch.close()

            @block.scalar
            def _(act):
                if soft:
                    with act.Fori(0, NNG) as i:
                        act.wait_ge(ask.sem, i + ask.at(1))
                        act.activation(mul[:, :, :, :], dif[:, :, :, :], ACT.Exp).then_inc(ex.sem, 1)
        for k in range(2):
            ld[k].passed(32 * (NNG // 2))
            got[k].passed(32 * NG * (NNG // 2))
        done.passed(NNG)
        dv.passed(per * NNG)
        if soft:
            ask.passed(NNG)
            ex.passed(NNG)


def elementwise(pr, steps):
    dv = pr.count("ew_steps")
    with pr.nc.Block() as block:
        @block.vector
        def _(v):
            ch = Chain(v, dv)
            for step in steps:
                ch.link(step(v))
    dv.passed(len(steps))


def node_mlp(pr, C, msgs, h, Wn1, bn1, Wn2, bn2, result):
    nc = pr.nc
    with ExitStack() as ctx:
        w1m = pr.sb("nm_w1m", [P, P], F32, ctx)
        w1h = pr.sb("nm_w1h", [D, P], F32, ctx)
        w2 = pr.sb("nm_w2", [P, D], F32, ctx)
        b1 = pr.sb("nm_b1", [P, 1], F32, ctx)
        b2 = pr.sb("nm_b2", [P, D], F32, ctx)
        sm = pr.sb("nm_sm", [P, NG, P], F32, ctx)
        sh = pr.sb("nm_sh", [P, NG, D], F32, ctx)
        mT = pr.sb("nm_mT", [P, NG * P], F32, ctx)
        hT = pr.sb("nm_hT", [D, NG * P], F32, ctx)
        hid = pr.sb("nm_hid", [P, NG * P], F32, ctx)
        pm = pr.ps("nm_pm", [P, 1024], ctx)
        ph = pr.ps("nm_ph", [P, 1024], ctx)
        p1 = pr.ps("nm_p1", [P, 1024], ctx)
        p2 = pr.ps("nm_p2", [P, 512], ctx)
        ld, stg, tr, mv, l1, l1a, l2, fin = (pr.count("nm_" + x) for x in ("loaded", "staged", "turned", "moved", "first",
                                                                          "activated", "second", "finished"))
        with nc.Block() as block:
            @block.sync
            def _(sp):
                sp.dma_start(w1m[0:D, :], Wn1[D:2 * D, :]).then_inc(ld.sem, 16)
                sp.dma_start(w1m[D:P, :], Wn1[0:D, :]).then_inc(ld.sem, 16)
                sp.dma_start(w1h[:, :], Wn1[2 * D:3 * D, :]).then_inc(ld.sem, 16)
                sp.dma_start(w2[:, :], Wn2).then_inc(ld.sem, 16)
                with nc.allow_non_contiguous_dma(reason="a bias, a word a partition"):
                    sp.dma_start(b1[:, :], bn1.unsqueeze(1)).then_inc(ld.sem, 16)
                sp.dma_start(b2[:, :], bn2.unsqueeze(0).to_broadcast([P, D])).then_inc(ld.sem, 16)

            @block.vector
            def _(v):
                v.wait_ge(ld.sem, 96)
                with v.Fori(0, NNG) as i:
                    tiles = bass.ds(NG * i, NG)
                    v.tensor_copy(sm[:, :, :], msgs[:, tiles, :])
                    v.tensor_copy(sh[:, :, :], h[:, tiles, :]).then_inc(stg.sem, 1)
                    v.wait_ge(l2.sem, i + 1)
                    v.tensor_tensor(result[:, tiles, :], p2[:, 0:NG * D].rearrange("p (t d) -> p t d", t=NG),
                                    b2[:, :].unsqueeze(1).to_broadcast([P, NG, D]), ALU.add).then_inc(fin.sem, 1)

            @block.tensor
            def _(pe):
                pe.wait_ge(ld.sem, 96)
                with pe.Fori(0, NNG) as i:
                    pe.wait_ge(stg.sem, i + 1)
                    for t in range(NG):
                        pe.transpose(pm[:, t * P:(t + 1) * P], sm[:, t, :], C.ident[:, :])
                        ins = pe.transpose(ph[0:D, t * P:(t + 1) * P], sh[:, t, :], C.ident[:, :])
                    ins.then_inc(tr.sem, 1)
                    pe.wait_ge(mv.sem, i * 2 + 2)
                    for a, b in ((0, 512), (512, NG * P)):
                        pe.matmul(p1[:, a:b], w1m[:, :], mT[:, a:b], start=True, stop=False)
                        ins = pe.matmul(p1[:, a:b], w1h[:, :], hT[:, a:b], start=False, stop=True)
                    ins.then_inc(l1.sem, 1)
                    pe.wait_ge(l1a.sem, i + 1)
                    for t in range(NG):
                        ins = pe.matmul(p2[:, t * D:(t + 1) * D], hid[:, t * P:(t + 1) * P], w2[:, :], start=True, stop=True)
                    ins.then_inc(l2.sem, 1)

            @block.scalar
            def _(act):
                act.wait_ge(ld.sem, 96)
                with act.Fori(0, NNG) as i:
                    act.wait_ge(tr.sem, i + 1)
                    act.activation(mT[:, :], pm[:, 0:NG * P], ACT.Copy).then_inc(mv.sem, 1)
                    act.activation(hT[:, :], ph[0:D, 0:NG * P], ACT.Copy).then_inc(mv.sem, 1)
                    act.wait_ge(l1.sem, i + 1)
                    act.activation(hid[:, :], p1[:, 0:NG * P], ACT.Relu, bias=b1[:, :]).then_inc(l1a.sem, 1)


def gnn(nc, A, out):
    with ExitStack() as ctx:
        pr = Program(nc, ctx)

        class C:
            pass
        C.src, C.dst, C.edge_attr = A["src"], A["dst"], A["edge_attr_32"]
        C.pairs = pr.dram("pairs", (P, ET * 2))
        C.src_col_i = pr.dram("src_col_i", (P, ET), I32)
        C.src_col = pr.dram("src_col", (P, ET))
        C.dst_col = pr.dram("dst_col", (P, ET))
        C.fk_dst = pr.dram("fk_dst", (ET, P + 1))
        C.fk_src = pr.dram("fk_src", (ET, 8, P + 1))
        C.sorted_pairs = pr.dram("sorted_pairs", (NE, 2))
        C.dst_of_sorted = pr.dram("dst_of_sorted", (P, ET), I32)
        C.src_sorted_col = pr.dram("src_sorted_col", (P, ET))
        C.heads8, C.heads64, C.heads128 = (pr.dram(f"heads{w}", (NE, w)) for w in (8, 64, 128))
        C.ix_dst, C.ix_src = (pr.dram(n, (3, P, NT), I32) for n in ("ix_dst", "ix_src"))
        C.cnt_d, C.start_d, C.has_d, C.spans_d = (pr.sb(n + "_d", [P, NT]) for n in ("cnt", "start", "has", "spans"))
        C.cnt_s, C.start_s, C.has_s, C.spans_s = (pr.sb(n + "_s", [P, NT]) for n in ("cnt", "start", "has", "spans"))
        C.deg_scale = pr.sb("deg_scale", [P, NT])
        C.keep_d, C.keep_s = (pr.sb(n, [P, ET]) for n in ("keep_d", "keep_s"))
        C.first_d, C.first_s = (pr.sb(n, [RB, NB], I32) for n in ("first_d", "first_s"))
        constants(pr, C)
        zero_heads(pr, C)
        with ExitStack() as early:
            C.seg_sb = pr.sb("seg_sb", [P, ET], F32, early)
            C.lo_d, C.hi_d, C.lo_s, C.hi_s = (pr.sb(n, [P, ET], F32, early) for n in ("lo_d", "hi_d", "lo_s", "hi_s"))
            read_ids(pr, C)
            count_nodes(pr, C)
            sort_by_src(pr, C)
        read_sorted(pr, C)
        node_bounds(pr, C)
        tile_starts(pr, C)

        x, h, skip = (pr.sb(n, [P, NT, D]) for n in ("x", "h", "skip"))
        ld, st, sq = pr.count("x_loaded"), pr.count("y_stored"), pr.count("deg_rooted")
        with nc.Block() as block:
            @block.sync
            def _(sp):
                sp.dma_start(x[:, :, :], A["x"].rearrange("(t p) d -> p t d", p=P)).then_inc(ld.sem, 16)
                sp.wait_ge(ld.sem, 16)

            @block.vector
            def _(v):
                v.tensor_scalar(C.deg_scale[:, :], C.cnt_d[:, :], 1.0, None, ALU.max).then_inc(sq.sem, 1)
                v.wait_ge(sq.sem, 2)
                v.reciprocal(C.deg_scale[:, :], C.deg_scale[:, :]).then_inc(sq.sem, 1)
                v.wait_ge(sq.sem, 3)
                v.tensor_tensor(C.deg_scale[:, :], C.deg_scale[:, :], C.has_d[:, :], ALU.mult)

            @block.scalar
            def _(act):
                act.wait_ge(sq.sem, 1)
                act.activation(C.deg_scale[:, :], C.deg_scale[:, :], ACT.Sqrt).then_inc(sq.sem, 1)

        def add_to(dst, a, b):
            return lambda v: v.tensor_tensor(dst[:, :, :], a[:, :, :], b[:, :, :], ALU.add)

        layernorm_relu(pr, C, x, h)
        T0, S0 = pr.dram("T0", (NN, D + 8)), pr.dram("S0", (NN, 8))
        project(pr, C, h, [(A["L0_gnn_W"], 0)], [], [(T0, 0, D + 8), (S0, D + 8, 8)],
                heads=(C.heads8, None, D + 8, 8, C.ix_src[0]), scores=(A["L0_gnn_dst_attn"], A["L0_gnn_src_attn"]))
        head_rows(pr, C, "s0", S0, None, 8, C.heads8, None, C.first_s)
        part0, carry0 = pr.dram("part0", (NE, D + 16)), pr.dram("carry0", (ET, 2 * (D + 8)))
        softmax_edges(pr, C, "a", 8, T0, C.src_sorted_col, C.dst_of_sorted, C.heads8,
                      C.fk_src.rearrange("t h c -> (t h) c"), part0)
        carry(pr, C, "softmax", part0, carry0, C.keep_s, 8)
        node_results(pr, C, "softmax", part0, carry0, C.ix_src, C.has_s, C.spans_s, h, 8)
        elementwise(pr, [add_to(x, x, h)])

        layernorm_relu(pr, C, x, h)
        T1, B1 = pr.dram("T1", (NN, 3 * D)), pr.dram("B1", (NN, 2 * D))
        We1 = A["L1_gnn_We1"]
        project(pr, C, h, [(We1[0:D, :], 0), (We1[D:2 * D, :], 2 * D)], [(A["L1_gnn_be1"], 2 * D)],
                [((T1, 0), 0, 2 * D), ((T1, 2 * D), None, D), (B1, 2 * D, 2 * D)],
                heads=(C.heads128, None, 2 * D, 2 * D, C.ix_dst[0]))
        head_rows(pr, C, "b1", B1, None, 2 * D, C.heads128, None, C.first_d)
        part1, carry1 = pr.dram("part1", (NE, 2 * D)), pr.dram("carry1", (ET, 2 * D))
        mlp_edges(pr, C, T1, C.heads128, part1, A["L1_gnn_be2"], A["L1_gnn_We2"])
        carry(pr, C, "sum_max", part1, carry1, C.keep_d)
        with ExitStack() as l1:
            msgs = pr.sb("msgs", [P, NT, 2 * D], F32, l1)
            node_results(pr, C, "sum_max", part1, carry1, C.ix_dst, C.has_d, C.spans_d, msgs)
            node_mlp(pr, C, msgs, h, A["L1_gnn_Wn1"], A["L1_gnn_bn1"], A["L1_gnn_Wn2"], A["L1_gnn_bn2"], skip)
        elementwise(pr, [add_to(x, x, skip), add_to(x, x, h)])

        layernorm_relu(pr, C, x, h)
        part2, carry2 = pr.dram("part2", (NE, D + 2)), pr.dram("carry2", (ET, 2 * (D + 1)))
        for layer in ("1", "2"):
            w = {n: A["L2_gnn_" + n + layer] for n in ("Wq", "bq", "Wk", "bk", "Wv", "bv", "We", "Ws", "bs")}
            KV, Q = pr.dram("KV" + layer, (NN, 2 * D)), pr.dram("Q" + layer, (NN, D))
            project(pr, C, h, [(w["W" + n], D * j) for j, n in enumerate("qkvs")], [(w["b" + n], D * j) for j, n in enumerate("qkvs")],
                    [(KV, D, 2 * D), (Q, 0, D)], heads=(C.heads64, None, 0, D, C.ix_dst[0]), keep=(skip, 3 * D))
            head_rows(pr, C, "q", Q, None, D, C.heads64, None, C.first_d)
            softmax_edges(pr, C, "t" + layer, 1, KV, C.dst_col, C.src_col_i, C.heads64, C.fk_dst, part2, w["We"])
            carry(pr, C, "softmax", part2, carry2, C.keep_d, 1)
            node_results(pr, C, "softmax", part2, carry2, C.ix_dst, C.has_d, C.spans_d, h, 1, 1e-16)
            if layer == "1":
                elementwise(pr, [add_to(h, h, skip), lambda v: v.tensor_scalar(h[:, :, :], h[:, :, :], 0.0, None, ALU.max)])
            else:
                elementwise(pr, [add_to(x, x, h), add_to(x, x, skip)])

        layernorm_relu(pr, C, x, h)
        HN = pr.dram("HN", (NN, D))
        project(pr, C, h, [(A["L3_gnn_W"], 0)], [(A["L3_gnn_b"], 0)], [(HN, 0, D)], row_scale=C.deg_scale)
        part3, carry3 = pr.dram("part3", (NE, D)), pr.dram("carry3", (ET, D))
        gcn_edges(pr, C, HN, part3)
        carry(pr, C, "sum", part3, carry3, C.keep_d)
        node_results(pr, C, "sum", part3, carry3, C.ix_dst, C.has_d, C.spans_d, h)
        wide = C.deg_scale[:, :].unsqueeze(2).to_broadcast([P, NT, D])
        elementwise(pr, [lambda v: v.tensor_tensor(h[:, :, :], h[:, :, :], wide, ALU.mult), add_to(x, x, h)])
        with nc.Block() as block:
            @block.sync
            def _(sp):
                full = N_NODES // P
                sp.dma_start(out[0:full * P, :].rearrange("(t p) d -> p t d", p=P), x[:, 0:full, :]).then_inc(st.sem, 16)
                sp.dma_start(out[full * P:N_NODES, :], x[0:N_NODES - full * P, full, :]).then_inc(st.sem, 16)
                sp.wait_ge(st.sem, 32)


def kernel(**inputs):
    import concourse.bacc as _bacc
    from concourse import mybir as _mybir
    from concourse.bass_utils import run_bass_kernel_spmd as _run

    nc = _bacc.Bacc("TRN2", target_bir_lowering=False, num_devices=1)
    laid = {k: np.asarray(v) for k, v in inputs.items()}
    for k in ("src", "dst"):
        laid[k] = np.pad(laid[k], (0, NE - N_EDGES), constant_values=NN - 1)
    laid["x"] = np.pad(laid["x"], ((0, NN - N_NODES), (0, 0)))
    laid["edge_attr_32"] = np.pad(laid["edge_attr_32"], ((0, NE - N_EDGES), (0, 0)))
    laid["L0_gnn_W"] = laid["L0_gnn_W"].T
    laid["L3_gnn_W"] = laid["L3_gnn_W"].T
    arrays, A = {}, {}
    for k, v in laid.items():
        arrays["in_" + k] = np.ascontiguousarray(v)
        A[k] = nc.dram_tensor("in_" + k, v.shape, _mybir.dt.from_np(v.dtype), kind="ExternalInput").ap()
    out = nc.dram_tensor("out0", (N_NODES, D), _mybir.dt.float32, kind="ExternalOutput").ap()
    gnn(nc, A, out)
    r = _run(nc, [arrays], core_ids=[0])
    return r.results[0]["out0"]
```

```python
import numpy as np
import concourse.bass as bass
from concourse import mybir
from concourse.alu_op_type import AluOpType as ALU
from contextlib import ExitStack

F32 = mybir.dt.float32
BF16 = mybir.dt.bfloat16
I32 = mybir.dt.int32
ACT = mybir.ActivationFunctionType
AX = mybir.AxisListType.X

P = 128
N_NODES = 12500
N_EDGES = 200000
NT = 98
NN = NT * P
ET = 1568
NE = ET * P
G = 8
NGRP = ET // G
S = 4
RB, NB = 98, 16
NG = 7
NNG = NT // NG
BIG = 3.0e38
EPS = 1e-5
D = 64


class Count:

    def __init__(self, sem):
        self.sem, self.base = sem, 0

    def at(self, n):
        return n + self.base

    def passed(self, n):
        self.base += n


class Chain:

    def __init__(self, eng, count, per=0, i=0):
        self.eng, self.count, self.per, self.i, self.n = eng, count, per, i, 0

    def link(self, ins):
        self.n += 1
        ins.then_inc(self.count.sem, 1)
        self.eng.wait_ge(self.count.sem, self.count.at(self.n) if self.per == 0 else self.i * self.per + self.count.at(self.n))

    def close(self):
        assert self.per == 0 or self.n == self.per, self.n


class Program:
    def __init__(self, nc, ctx):
        self.nc, self.ctx, self.counts, self.uses = nc, ctx, {}, {}

    def fresh(self, name):
        self.uses[name] = self.uses.get(name, 0) + 1
        return name if self.uses[name] == 1 else f"{name}_{self.uses[name]}"

    def count(self, name):
        if name not in self.counts:
            self.counts[name] = Count(self.ctx.enter_context(self.nc.semaphore(name)))
        return self.counts[name]

    def sb(self, name, shape, dt=F32, ctx=None):
        return (ctx or self.ctx).enter_context(self.nc.sbuf_tensor(self.fresh(name), shape, dt))

    def ps(self, name, shape, ctx, dt=F32):
        return ctx.enter_context(self.nc.psum_tensor(self.fresh(name), shape, dt))

    def dram(self, name, shape, dt=F32):
        return self.nc.dram_tensor(name, shape, dt, kind="Internal").ap()


def constants(pr, C):
    nc = pr.nc
    s = pr.count("const_made")
    C.ident = pr.sb("ident", [P, P])
    C.before = pr.sb("before", [P, P])
    C.after = pr.sb("after", [P, P])
    C.iota = pr.sb("iota", [P, P])
    C.ones = pr.sb("ones", [P, P])
    C.zeros = pr.sb("zeros", [P, 1])
    with nc.Block() as block:
        @block.gpsimd
        def _(gp):
            gp.memset(C.ident[:, :], 0.0).then_inc(s.sem, 1)
            gp.memset(C.zeros[:, :], 0.0).then_inc(s.sem, 1)
            gp.memset(C.ones[:, :], 1.0).then_inc(s.sem, 1)
            gp.memset(C.before[:, :], 1.0).then_inc(s.sem, 1)
            gp.memset(C.after[:, :], 1.0).then_inc(s.sem, 1)
            gp.iota(C.iota[:, :], [[1, P]], base=0, channel_multiplier=0,
                    allow_small_or_imprecise_dtypes=True).then_inc(s.sem, 1)
            gp.wait_ge(s.sem, 6)
            gp.affine_select(out=C.ident[:, :], in_=C.ident[:, :], compare_op=ALU.not_equal, fill=1.0, base=0,
                             pattern=[[-1, P]], channel_multiplier=1).then_inc(s.sem, 1)
            gp.affine_select(out=C.before[:, :], in_=C.before[:, :], compare_op=ALU.is_gt, fill=0.0, base=0,
                             pattern=[[1, P]], channel_multiplier=-1).then_inc(s.sem, 1)
            gp.affine_select(out=C.after[:, :], in_=C.after[:, :], compare_op=ALU.is_gt, fill=0.0, base=0,
                             pattern=[[-1, P]], channel_multiplier=1).then_inc(s.sem, 1)
            gp.wait_ge(s.sem, 9)


def zero_heads(pr, C):
    nc = pr.nc
    with ExitStack() as ctx:
        z = pr.sb("zero_rows", [P, 8192], ctx=ctx)
        made, done = pr.count("zeros_made"), pr.count("zeros_written")
        n = 0
        with nc.Block() as block:
            @block.vector
            def _(v):
                v.memset(z[:, :], 0.0).then_inc(made.sem, 1)

            @block.sync
            def _(sp):
                n = 0
                sp.wait_ge(made.sem, 1)
                for buf, w in ((C.heads8, 8), (C.heads64, 64), (C.heads128, 128)):
                    flat = buf.rearrange("(q p r) w -> q p (r w)", p=P, q=w // 4 if w > 8 else 2)
                    for q in range(flat.shape[0]):
                        sp.dma_start(flat[q], z[:, 0:flat.shape[2]]).then_inc(done.sem, 16)
                        n += 16
                sp.wait_ge(done.sem, n)


def block_at(b):
    return (b // 4) * 512 + (b % 4) * RB


def blocks(ps):
    return ps[:, :].rearrange("p (k c) -> p k c", k=4)[:, :, 0:4 * RB]


def by_bank(ap):
    return ap.rearrange("p (k c) -> p k c", k=4)


def read_ids(pr, C):
    nc = pr.nc
    with ExitStack() as ctx:
        raw = [pr.sb(f"ids_raw{j}", [RB, NB, P], I32, ctx) for j in range(2)]
        rowf = [pr.sb(f"ids_rowf{j}", [RB, NB, P], F32, ctx) for j in range(2)]
        fk = pr.sb("ids_fk", [RB, NB, P + 1], F32, ctx)
        pair = pr.sb("ids_pair", [P, ET, 2], F32, ctx)
        colf = pr.sb("ids_colf", [P, ET], F32, ctx)
        coli = pr.sb("ids_coli", [P, ET], I32, ctx)
        digit = pr.sb("ids_digit", [P, ET], I32, ctx)
        ps = [pr.ps(f"ids_ps{j}", [P, 2048], ctx) for j in range(2)]
        ld, cv, tr, dv, st = (pr.count(n) for n in ("ids_loaded", "ids_converted", "ids_turned", "ids_dve", "ids_stored"))
        ready = {}
        with nc.Block() as block:
            @block.sync
            def _(sp):
                for j, a in enumerate((C.dst, C.src)):
                    sp.dma_start(raw[j][:, :, :], a.rearrange("(b r c) -> r b c", r=RB, c=P)).then_inc(ld.sem, 16)

            @block.vector
            def _(v):
                ch = Chain(v, dv)
                v.wait_ge(ld.sem, 32)
                for j in range(2):
                    v.tensor_copy(rowf[j][:, :, :], raw[j][:, :, :]).then_inc(cv.sem, 1)
                v.wait_ge(cv.sem, 2)
                ch.link(v.memset(fk[:, :, :], -BIG))
                ch.link(v.tensor_tensor(fk[:, :, 1:P], rowf[0][:, :, 1:P], rowf[0][:, :, 0:P - 1], ALU.not_equal))
                ch.link(v.tensor_scalar(fk[:, :, 1:P], fk[:, :, 1:P], -BIG, None, ALU.mult))
                ready["fk"] = ch.n
                for j, (lo, hi) in enumerate(((C.lo_d, C.hi_d), (C.lo_s, C.hi_s))):
                    v.wait_ge(tr.sem, j + 1)
                    dest = C.seg_sb if j == 0 else colf
                    ch.link(v.tensor_copy(by_bank(dest[:, :]), blocks(ps[j])))
                    ch.link(v.tensor_copy(pair[:, :, j], dest[:, :]))
                    ch.link(v.tensor_copy(coli[:, :], dest[:, :]))
                    ch.link(v.tensor_scalar(digit[:, :], coli[:, :], P - 1, None, ALU.bitwise_and))
                    ch.link(v.tensor_copy(lo[:, :], digit[:, :]))
                    ch.link(v.tensor_scalar(digit[:, :], coli[:, :], 7, None, ALU.arith_shift_right))
                    ch.link(v.tensor_copy(hi[:, :], digit[:, :]))
                ready["all"] = ch.n

            @block.tensor
            def _(pe):
                pe.wait_ge(cv.sem, 2)
                for j in range(2):
                    for b in range(NB):
                        ins = pe.transpose(ps[j][:, block_at(b):block_at(b) + RB], rowf[j][:, b, :], C.ident[0:RB, 0:RB])
                    ins.then_inc(tr.sem, 1)

            @block.scalar
            def _(act):
                act.wait_ge(dv.sem, ready["fk"])
                act.dma_start(C.fk_dst.rearrange("(b r) c -> r b c", r=RB), fk[:, :, :]).then_inc(st.sem, 16)
                act.wait_ge(dv.sem, ready["all"])
                act.dma_start(C.pairs, pair[:, :, :].rearrange("p t j -> p (t j)")).then_inc(st.sem, 16)
                act.dma_start(C.src_col_i, coli[:, :]).then_inc(st.sem, 16)
                act.dma_start(C.dst_col, C.seg_sb[:, :]).then_inc(st.sem, 16)
                act.dma_start(C.src_col, colf[:, :]).then_inc(st.sem, 16)
                act.wait_ge(st.sem, 80)


def count_nodes(pr, C):
    nc = pr.nc
    with ExitStack() as ctx:
        low = [[pr.sb(f"hist_low{j}{k}", [P, G, P], BF16, ctx) for k in range(2)] for j in range(2)]
        high = [[pr.sb(f"hist_high{j}{k}", [P, G, NT], BF16, ctx) for k in range(2)] for j in range(2)]
        zero = pr.sb("hist_zero", [P, P], BF16, ctx)
        tot = pr.sb("hist_tot", [P, NT], F32, ctx)
        run = pr.sb("hist_run", [P, NT], F32, ctx)
        tmp = pr.sb("hist_tmp", [P, NT], F32, ctx)
        hist = [pr.ps(f"hist_ps{j}", [P, 512], ctx) for j in range(2)]
        pre = pr.ps("hist_pre", [P, 512], ctx)
        zr, onehot, used, summed, copied, dv = (pr.count(n) for n in (
            "hist_zero", "hist_onehot", "hist_used", "hist_summed", "hist_copied", "hist_dve"))
        digits = ((C.lo_d, C.hi_d), (C.lo_s, C.hi_s))
        with nc.Block() as block:
            @block.vector
            def _(v):
                v.memset(zero[:, :], 0.0).then_inc(zr.sem, 1)
                with v.Fori(0, NGRP // 2) as i:
                    for k in range(2):
                        g = 2 * i + k
                        v.wait_ge(used.sem, g + 1)
                        for j, (lo, hi) in enumerate(digits):
                            v.tensor_tensor(low[j][k][:, :, :], C.iota[:, :].unsqueeze(1).to_broadcast([P, G, P]),
                                            lo[:, bass.ds(G * g, G)].unsqueeze(2).to_broadcast([P, G, P]), ALU.is_equal)
                            ins = v.tensor_tensor(high[j][k][:, :, :], C.iota[:, 0:NT].unsqueeze(1).to_broadcast([P, G, NT]),
                                                  hi[:, bass.ds(G * g, G)].unsqueeze(2).to_broadcast([P, G, NT]), ALU.is_equal)
                        ins.then_inc(onehot.sem, 1)
                ch = Chain(v, dv)
                v.wait_ge(summed.sem, 1)
                for j, (cnt, start) in enumerate(((C.cnt_d, C.start_d), (C.cnt_s, C.start_s))):
                    ch.link(v.tensor_copy(cnt[:, :], hist[j][:, 0:NT]))
                    v.sem_inc(copied.sem, 1)
                    v.wait_ge(summed.sem, j + 2)
                    ch.link(v.tensor_copy(tot[:, :], pre[:, NT:2 * NT]))
                    ch.link(v.tensor_tensor_scan(run[:, :], C.ones[:, 0:NT], tot[:, :], 0.0, ALU.mult, ALU.add))
                    ch.link(v.tensor_tensor(run[:, :], run[:, :], tot[:, :], ALU.subtract))
                    ch.link(v.tensor_tensor(start[:, :], pre[:, 0:NT], run[:, :], ALU.add))

            @block.tensor
            def _(pe):
                pe.wait_ge(zr.sem, 1)
                pe.sem_inc(used.sem, 2)
                for j in range(2):
                    pe.matmul(hist[j][:, 0:NT], zero[:, :], zero[:, 0:NT], start=True, stop=False, skip_group_check=True)
                with pe.Fori(0, NGRP // 2) as i:
                    for k in range(2):
                        pe.wait_ge(onehot.sem, 2 * i + (k + 1))
                        for j in range(2):
                            for t in range(G):
                                ins = pe.matmul(hist[j][:, 0:NT], low[j][k][:, t, :], high[j][k][:, t, :],
                                                start=False, stop=False, skip_group_check=True)
                        ins.then_inc(used.sem, 1)
                for j in range(2):
                    ins = pe.matmul(hist[j][:, 0:NT], zero[:, :], zero[:, 0:NT], start=False, stop=True, skip_group_check=True)
                ins.then_inc(summed.sem, 1)
                for j, cnt in enumerate((C.cnt_d, C.cnt_s)):
                    pe.wait_ge(dv.sem, 1 + 5 * j)
                    pe.matmul(pre[:, 0:NT], C.before[:, :], cnt[:, :], start=True, stop=True)
                    pe.matmul(pre[:, NT:2 * NT], C.ones[:, :], cnt[:, :], start=True, stop=True).then_inc(summed.sem, 1)


def sort_by_src(pr, C):
    nc = pr.nc
    with ExitStack() as ctx:
        sb, pscope = (lambda n, s, d=F32: pr.sb("rank_" + n, s, d, ctx)), (lambda n, s, d=F32: pr.ps("rank_" + n, s, ctx, d))
        seg = [sb(f"seg{k}", [P, G]) for k in range(2)]
        pair = [sb(f"pair{k}", [P, G, 2]) for k in range(2)]
        place = [sb(f"place{k}", [P, G], I32) for k in range(2)]
        low = sb("low", [P, G, P], BF16)
        high = sb("high", [P, G, NT], BF16)
        lowT = sb("lowT", [P, G, P])
        identb = sb("identb", [P, P], BF16)
        sofar = [sb(f"sofar{n}", [P, NT]) for n in range(2)]
        earlier = sb("earlier", [P, G, P])
        picked = sb("picked", [P, G, NT])
        rank = sb("rank", [P, G])
        base = sb("base", [P, G])
        row_ps = pscope("row_ps", [P, 1024])
        lowT_ps = pscope("lowT_ps", [P, 1024], BF16)
        total = pscope("total", [P, 512])
        pick_ps = pscope("pick_ps", [P, 1024])
        ident_made, load, placed, scattered, rowed, onehot, lowed, turned, snap, counted, dv, done = (
            pr.count("rank_" + n) for n in ("ident", "load", "placed", "scattered", "rowed", "onehot", "lowed", "turned",
                                            "snap", "counted", "dve", "done"))
        gate = pr.count("pool_gate")
        load = [pr.count(f"rank_load{k}") for k in range(2)]
        scattered = [pr.count(f"rank_scattered{k}") for k in range(2)]
        with nc.Block() as block:
            @block.sync
            def _(sp):
                def load_group(g, k):
                    sp.dma_start(seg[k][:, :], C.src_col[:, bass.ds(G * g, G)]).then_inc(load[k].sem, 16)
                    sp.dma_start(pair[k][:, :, :].rearrange("p t j -> p (t j)"),
                                 C.pairs[:, bass.ds(2 * G * g, 2 * G)]).then_inc(load[k].sem, 16)

                for k in range(2):
                    load_group(k, k)
                with sp.Fori(0, NGRP // 2 - 1) as i:
                    for k in range(2):
                        sp.wait_ge(scattered[k].sem, i * (16 * G) + 16 * G)
                        load_group(2 * i + (k + 2), k)

            @block.gpsimd
            def _(gp):
                with gp.Fori(0, NGRP // 2) as i:
                    for k in range(2):
                        gp.wait_ge(placed.sem, 2 * i + (k + 1))
                        gp.sem_inc(gate.sem, 1)
                        for t in range(G):
                            gp.indirect_dma_start(C.sorted_pairs, bass.IndirectOffsetOnAxis(ap=place[k][:, t:t + 1], axis=0),
                                                  pair[k][:, t, :], None).then_inc(scattered[k].sem, 16)
                for k in range(2):
                    gp.wait_ge(scattered[k].sem, (NGRP // 2) * 16 * G)

            @block.vector
            def _(v):
                v.tensor_copy(identb[:, :], C.ident[:, :]).then_inc(ident_made.sem, 1)
                with v.Fori(0, NGRP // 2) as i:
                    for k in range(2):
                        g = 2 * i + k
                        ch = Chain(v, dv, 6, g)
                        v.wait_ge(counted.sem, g * G + 1)
                        v.tensor_tensor(low[:, :, :], C.iota[:, :].unsqueeze(1).to_broadcast([P, G, P]),
                                        C.lo_s[:, bass.ds(G * g, G)].unsqueeze(2).to_broadcast([P, G, P]), ALU.is_equal)
                        v.tensor_tensor(high[:, :, :], C.iota[:, 0:NT].unsqueeze(1).to_broadcast([P, G, NT]),
                                        C.hi_s[:, bass.ds(G * g, G)].unsqueeze(2).to_broadcast([P, G, NT]), ALU.is_equal).then_inc(onehot.sem, 1)
                        v.wait_ge(load[k].sem, i * 32 + 32)
                        v.wait_ge(rowed.sem, g + 1)
                        ch.link(v.tensor_tensor(earlier[:, :, :], row_ps[:, :].rearrange("p (t e) -> p t e", t=G),
                                                seg[k][:, :].unsqueeze(2).to_broadcast([P, G, P]), ALU.is_equal))
                        ch.link(v.tensor_tensor(earlier[:, :, :], earlier[:, :, :],
                                                C.after[:, :].unsqueeze(1).to_broadcast([P, G, P]), ALU.mult))
                        ch.link(v.tensor_reduce(rank[:, :], earlier[:, :, :], AX, ALU.add))
                        v.wait_ge(counted.sem, g * G + (G + 1))
                        v.wait_ge(onehot.sem, g + 1)
                        ch.link(v.tensor_tensor(picked[:, :, :].rearrange("p (a b) c -> p a (b c)", a=2),
                                                pick_ps[:, :].rearrange("p (a c) -> p a c", a=2)[:, :, 0:4 * NT],
                                                high[:, :, :].rearrange("p (a b) c -> p a (b c)", a=2), ALU.mult))
                        ch.link(v.tensor_reduce(base[:, :], picked[:, :, :], AX, ALU.add))
                        ch.link(v.tensor_tensor(place[k][:, :], base[:, :], rank[:, :], ALU.add))
                        v.sem_inc(placed.sem, 1)
                        ch.close()

            @block.tensor
            def _(pe):
                pe.wait_ge(ident_made.sem, 1)
                pe.matmul(total[:, 0:NT], C.ident[:, :], C.start_s[:, :], start=True, stop=True,
                          skip_group_check=True).then_inc(counted.sem, 1)
                with pe.Fori(0, NGRP // 2) as i:
                    for k in range(2):
                        g = 2 * i + k
                        pe.wait_ge(load[k].sem, i * 32 + 32)
                        pe.wait_ge(onehot.sem, g + 1)
                        for t in range(G):
                            ins = pe.transpose(row_ps[:, t * P:(t + 1) * P], seg[k][:, t:t + 1].to_broadcast([P, P]), C.ident[:, :])
                        ins.then_inc(rowed.sem, 1)
                        for t in range(G):
                            ins = pe.transpose(lowT_ps[:, t * P:(t + 1) * P], low[:, t, :], identb[:, :])
                        ins.then_inc(lowed.sem, 1)
                        pe.wait_ge(turned.sem, g + 1)
                        for t in range(G):
                            at = (t // 4) * 512 + (t % 4) * NT
                            pe.wait_ge(snap.sem, g * G + (t + 1))
                            pe.matmul(pick_ps[:, at:at + NT], lowT[:, t, :], sofar[t % 2][:, :], start=True, stop=True)
                            pe.matmul(total[:, 0:NT], low[:, t, :], high[:, t, :], start=False, stop=True,
                                      skip_group_check=True).then_inc(counted.sem, 1)

            @block.scalar
            def _(act):
                with act.Fori(0, NGRP // 2) as i:
                    for k in range(2):
                        g = 2 * i + k
                        act.wait_ge(lowed.sem, g + 1)
                        act.activation(lowT[:, :, :].rearrange("p t e -> p (t e)"), lowT_ps[:, :], ACT.Copy).then_inc(turned.sem, 1)
                        for t in range(G):
                            act.wait_ge(counted.sem, g * G + (t + 1))
                            act.activation(sofar[t % 2][:, :], total[:, 0:NT], ACT.Copy).then_inc(snap.sem, 1)


def read_sorted(pr, C):
    nc = pr.nc
    with ExitStack() as ctx:
        raw = pr.sb("srt_raw", [RB, NB, P, 2], F32, ctx)
        rowf = [pr.sb(f"srt_rowf{j}", [RB, NB, P], F32, ctx) for j in range(2)]
        fk = pr.sb("srt_fk", [RB, NB, P + 1], F32, ctx)
        colf = pr.sb("srt_colf", [P, ET], F32, ctx)
        coli = pr.sb("srt_coli", [P, ET], I32, ctx)
        ps = [pr.ps(f"srt_ps{j}", [P, 2048], ctx) for j in range(2)]
        ld, tr, dv, st = (pr.count(n) for n in ("srt_loaded", "srt_turned", "srt_dve", "srt_stored"))
        with nc.Block() as block:
            @block.sync
            def _(sp):
                sp.dma_start(raw[:, :, :, :].rearrange("r b c j -> r b (c j)"),
                             C.sorted_pairs.rearrange("(b r c) j -> r b (c j)", r=RB, c=P)).then_inc(ld.sem, 16)

            @block.vector
            def _(v):
                ch = Chain(v, dv)
                v.wait_ge(ld.sem, 16)
                for j in range(2):
                    ch.link(v.tensor_copy(rowf[j][:, :, :], raw[:, :, :, j]))
                ch.link(v.memset(fk[:, :, :], -BIG))
                ch.link(v.tensor_tensor(fk[:, :, 1:P], rowf[1][:, :, 1:P], rowf[1][:, :, 0:P - 1], ALU.not_equal))
                ch.link(v.tensor_scalar(fk[:, :, 1:P], fk[:, :, 1:P], -BIG, None, ALU.mult))
                v.wait_ge(tr.sem, 1)
                v.tensor_copy(by_bank(coli[:, :]), blocks(ps[0]))
                ch.link(v.tensor_copy(by_bank(colf[:, :]), blocks(ps[1])))

            @block.tensor
            def _(pe):
                pe.wait_ge(dv.sem, 2)
                for j in range(2):
                    for b in range(NB):
                        ins = pe.transpose(ps[j][:, block_at(b):block_at(b) + RB], rowf[j][:, b, :], C.ident[0:RB, 0:RB])
                ins.then_inc(tr.sem, 1)

            @block.scalar
            def _(act):
                act.wait_ge(dv.sem, 5)
                for h in range(8):
                    act.dma_start(C.fk_src.rearrange("(b r) h c -> r b h c", r=RB)[:, :, h, :], fk[:, :, :]).then_inc(st.sem, 16)
                act.wait_ge(dv.sem, 6)
                act.dma_start(C.dst_of_sorted, coli[:, :]).then_inc(st.sem, 16)
                act.dma_start(C.src_sorted_col, colf[:, :]).then_inc(st.sem, 16)
                act.wait_ge(st.sem, 160)


def node_bounds(pr, C):
    nc = pr.nc
    with ExitStack() as ctx:
        f = [pr.sb(f"nb_f{j}", [P, NT], F32, ctx) for j in range(4)]
        n = [pr.sb(f"nb_i{j}", [P, NT], I32, ctx) for j in range(4)]
        out_i = [pr.sb(f"nb_out{j}", [P, NT], I32, ctx) for j in range(6)]
        dv, st = pr.count("bounds_dve"), pr.count("bounds_stored")
        with nc.Block() as block:
            @block.vector
            def _(v):
                ch = Chain(v, dv)
                for j, (cnt, start, has, spans) in enumerate(((C.cnt_d, C.start_d, C.has_d, C.spans_d),
                                                              (C.cnt_s, C.start_s, C.has_s, C.spans_s))):
                    ch.link(v.tensor_scalar(has[:, :], cnt[:, :], 0.5, None, ALU.is_gt))
                    ch.link(v.tensor_tensor(f[0][:, :], start[:, :], cnt[:, :], ALU.add))
                    ch.link(v.tensor_scalar(f[0][:, :], f[0][:, :], -1.0, 0.0, ALU.add, ALU.max))
                    ch.link(v.tensor_copy(out_i[3 * j + 1][:, :], f[0][:, :]))
                    ch.link(v.tensor_scalar(n[0][:, :], out_i[3 * j + 1][:, :], 7, None, ALU.arith_shift_right))
                    ch.link(v.tensor_copy(f[1][:, :], n[0][:, :]))
                    ch.link(v.tensor_copy(n[1][:, :], start[:, :]))
                    ch.link(v.tensor_scalar(n[2][:, :], n[1][:, :], 7, None, ALU.arith_shift_right))
                    ch.link(v.tensor_copy(f[2][:, :], n[2][:, :]))
                    ch.link(v.tensor_tensor(spans[:, :], f[1][:, :], f[2][:, :], ALU.is_gt))
                    ch.link(v.tensor_tensor(spans[:, :], spans[:, :], has[:, :], ALU.mult))
                    ch.link(v.tensor_scalar(f[1][:, :], f[1][:, :], -1.0, 0.0, ALU.add, ALU.max))
                    ch.link(v.tensor_copy(out_i[3 * j + 2][:, :], f[1][:, :]))
                    ch.link(v.tensor_scalar(f[3][:, :], has[:, :], -float(NE), float(NE), ALU.mult, ALU.add))
                    ch.link(v.tensor_tensor(f[3][:, :], f[3][:, :], start[:, :], ALU.add))
                    ch.link(v.tensor_copy(out_i[3 * j][:, :], f[3][:, :]))

            @block.sync
            def _(sp):
                sp.wait_ge(dv.sem, 32)
                for j, rows in enumerate((C.ix_dst, C.ix_src)):
                    for q in range(3):
                        sp.dma_start(rows[q], out_i[3 * j + q][:, :]).then_inc(st.sem, 16)
                sp.wait_ge(st.sem, 96)


def tile_starts(pr, C):
    nc = pr.nc
    with ExitStack() as ctx:
        last = [pr.sb(f"ts_last{j}", [P, ET], F32, ctx) for j in range(2)]
        first = [pr.sb(f"ts_first{j}", [RB, NB], F32, ctx) for j in range(2)]
        ld, dv, st = (pr.count(n) for n in ("starts_loaded", "starts_dve", "starts_stored"))
        with nc.Block() as block:
            @block.sync
            def _(sp):
                for j, col in enumerate((C.dst_col, C.src_sorted_col)):
                    sp.dma_start(last[j][:, :], col[P - 1:P, :].to_broadcast([P, ET])).then_inc(ld.sem, 16)
                    with nc.allow_non_contiguous_dma(reason="one word of each tile"):
                        sp.dma_start(first[j][:, :], col[0, :].rearrange("(b r) -> r b", r=RB)).then_inc(ld.sem, 16)

            @block.vector
            def _(v):
                ch = Chain(v, dv)
                v.wait_ge(ld.sem, 64)
                for j, (keep, idx) in enumerate(((C.keep_d, C.first_d), (C.keep_s, C.first_s))):
                    ch.link(v.memset(keep[:, 0:1], 0.0))
                    ch.link(v.tensor_tensor(keep[:, 1:ET], last[j][:, 1:ET], last[j][:, 0:ET - 1], ALU.is_equal))
                    ch.link(v.tensor_copy(idx[:, :], first[j][:, :]))


def head_rows(pr, C, tag, table, rows_dram, width, heads, bounds, first):
    nc = pr.nc
    with ExitStack() as ctx:
        rows = pr.sb("hr_rows", [RB, NB * width], F32, ctx)
        got, put = pr.count("hr_gathered"), pr.count("hr_written")
        with nc.Block() as block:
            @block.gpsimd
            def _(gp):
                for b in range(NB):
                    gp.indirect_dma_start(rows[:, b * width:(b + 1) * width], None, table,
                                          bass.IndirectOffsetOnAxis(ap=first[:, b:b + 1], axis=0)).then_inc(got.sem, 16)

            @block.sync
            def _(sp):
                sp.wait_ge(got.sem, got.at(16 * NB))
                sp.dma_start(heads.rearrange("(b r e) w -> r b e w", r=RB, e=P)[:, :, 0, :],
                             rows[:, :].rearrange("r (b w) -> r b w", w=width)).then_inc(put.sem, 16)
                sp.wait_ge(put.sem, put.at(16))
        got.passed(16 * NB)
        put.passed(16)


def layernorm_relu(pr, C, x, h):
    nc = pr.nc
    with ExitStack() as ctx:
        big = pr.sb("ln_big", [P, NT, D], F32, ctx)
        mean = pr.sb("ln_mean", [P, NT], F32, ctx)
        var = pr.sb("ln_var", [P, NT], F32, ctx)
        std = pr.sb("ln_std", [P, NT], F32, ctx)
        dv, sq = pr.count("ln_dve"), pr.count("ln_rooted")
        with nc.Block() as block:
            @block.vector
            def _(v):
                ch = Chain(v, dv)
                wide = lambda a: a[:, :].unsqueeze(2).to_broadcast([P, NT, D])
                ch.link(v.tensor_reduce(mean[:, :], x[:, :, :], AX, ALU.add))
                ch.link(v.tensor_scalar(mean[:, :], mean[:, :], 1.0 / D, None, ALU.mult))
                ch.link(v.tensor_tensor(h[:, :, :], x[:, :, :], wide(mean), ALU.subtract))
                ch.link(v.tensor_tensor(big[:, :, :], h[:, :, :], h[:, :, :], ALU.mult))
                ch.link(v.tensor_reduce(var[:, :], big[:, :, :], AX, ALU.add))
                ch.link(v.tensor_scalar(var[:, :], var[:, :], 1.0 / D, EPS, ALU.mult, ALU.add))
                v.wait_ge(sq.sem, sq.at(1))
                ch.link(v.reciprocal(std[:, :], std[:, :]))
                ch.link(v.tensor_tensor(h[:, :, :], h[:, :, :], wide(std), ALU.mult))
                ch.link(v.tensor_scalar(h[:, :, :], h[:, :, :], 0.0, None, ALU.max))

            @block.scalar
            def _(act):
                act.wait_ge(dv.sem, dv.at(6))
                act.activation(std[:, :], var[:, :], ACT.Sqrt).then_inc(sq.sem, 1)
        dv.passed(9)
        sq.passed(1)


def project(pr, C, h, weights, bias, tables, heads=(), keep=None, row_scale=None, scores=None):
    nc = pr.nc
    width = max(c + w.shape[1] for w, c in weights)
    total = width + (16 if scores else 0)
    pitch = 512 // (4 if width <= P else 2)
    with ExitStack() as ctx:
        w_sb = pr.sb("pj_w", [D + 1, width], F32, ctx)
        att = pr.sb("pj_att", [P, 2, D], F32, ctx)
        stage = [pr.sb(f"pj_stage{k}", [P, NG, D], F32, ctx) for k in range(2)]
        hT = pr.sb("pj_hT", [D + 1, NG * P], F32, ctx)
        res = [pr.sb(f"pj_res{k}", [P, NG, total], F32, ctx) for k in range(2)]
        tmp = pr.sb("pj_tmp", [P, NG, 2, D], F32, ctx)
        idx = [pr.sb(f"pj_idx{k}", [P, max(len(heads), 1), NG], I32, ctx) for k in range(2)]
        trp = pr.ps("pj_trp", [P, 1024], ctx)
        acc = pr.ps("pj_acc", [P, 4 * 512], ctx)
        ld, ini, staged, turned, moved, made, products, scored, gate, pe_gate, free = (
            pr.count("pj_" + n) for n in ("loaded", "rows_set", "staged", "turned", "moved", "made", "products", "scored",
                                          "gate", "pe_gate", "free"))
        stored, scat, ixl = ([pr.count(f"pj_{n}{k}") for k in range(2)] for n in ("stored", "scattered", "index"))
        nload = 16 * (len(weights) + len(bias) + (2 if scores else 0))
        nstore, nix, nscat = 16 * len(tables), 16 * len(heads), 16 * NG * len(heads)
        with nc.Block() as block:
            @block.sync
            def _(sp):
                for w, c in weights:
                    sp.dma_start(w_sb[0:D, c:c + w.shape[1]], w).then_inc(ld.sem, 16)
                sp.wait_ge(ini.sem, ini.at(2))
                for b, c in bias:
                    sp.dma_start(w_sb[D:D + 1, c:c + b.shape[0]], b.unsqueeze(0)).then_inc(ld.sem, 16)
                if scores:
                    for j, a in enumerate(scores):
                        sp.dma_start(att[:, j, :], a.rearrange("a h d -> a (h d)").to_broadcast([P, D])).then_inc(ld.sem, 16)

                def load_index(g, k):
                    for j, hd in enumerate(heads):
                        sp.dma_start(idx[k][:, j, :], hd[3][:, bass.ds(NG * g, NG)]).then_inc(ixl[k].sem, 16)

                def store(g, i, k):
                    sp.wait_ge(scored.sem, g + scored.at(1))
                    for tab, at, c, wd in tables:
                        src = stage[k][:, :, :] if c is None else res[k][:, :, c:c + wd]
                        sp.dma_start(tab.rearrange("(t p) w -> p t w", p=P)[:, bass.ds(NG * g, NG), at:at + wd], src)\
                            .then_inc(stored[k].sem, 16)
                    if heads:
                        sp.wait_ge(scat[k].sem, i * nscat + scat[k].at(nscat))

                def release(i, k):
                    sp.wait_ge(stored[k].sem, i * nstore + stored[k].at(nstore))
                    sp.sem_inc(free.sem, 1)

                for k in range(2):
                    load_index(k, k)
                with sp.Fori(0, NNG // 2 - 1) as i:
                    for k in range(2):
                        g = 2 * i + k
                        store(g, i, k)
                        load_index(g + 2, k)
                        release(i, k)
                for k in range(2):
                    store(NNG - 2 + k, NNG // 2 - 1, k)
                    release(NNG // 2 - 1, k)

            @block.gpsimd
            def _(gp):
                if heads:
                    with gp.Fori(0, NNG // 2) as i:
                        for k in range(2):
                            gp.wait_ge(ixl[k].sem, i * nix + ixl[k].at(nix))
                            gp.wait_ge(scored.sem, 2 * i + scored.at(k + 1))
                            gp.sem_inc(gate.sem, 1)
                            for j, (buf, c, wd, _) in enumerate(heads):
                                for t in range(NG):
                                    gp.indirect_dma_start(buf, bass.IndirectOffsetOnAxis(ap=idx[k][:, j, t:t + 1], axis=0),
                                                          res[k][:, t, c:c + wd], None,
                                                          bounds_check=NE - 1, oob_is_err=False).then_inc(scat[k].sem, 16)

            @block.vector
            def _(v):
                v.memset(hT[D:D + 1, :], 1.0).then_inc(ini.sem, 1)
                v.memset(w_sb[D:D + 1, :], 0.0).then_inc(ini.sem, 1)
                v.sem_inc(free.sem, 2)
                with v.Fori(0, NNG // 2) as i:
                    for k in range(2):
                        g = 2 * i + k
                        tiles = bass.ds(NG * g, NG)
                        v.wait_ge(free.sem, g + free.at(1))
                        v.tensor_copy(stage[k][:, :, :], h[:, tiles, :]).then_inc(staged.sem, 1)
                        v.wait_ge(made.sem, g + made.at(1))
                        if scores:
                            v.wait_ge(ld.sem, ld.at(nload))
                            for j in range(2):
                                v.tensor_tensor(tmp[:, :, j, :], res[k][:, :, 0:D], att[:, j, :].unsqueeze(1).to_broadcast([P, NG, D]),
                                                ALU.mult).then_inc(products.sem, 1)
                            v.wait_ge(products.sem, g * 2 + products.at(2))
                            for j in range(2):
                                ins = v.tensor_reduce(res[k][:, :, D + 8 * j:D + 8 * j + 8],
                                                      tmp[:, :, j, :].rearrange("p t (h d) -> p t h d", h=8), AX, ALU.add)
                            ins.then_inc(scored.sem, 1)
                            v.wait_ge(scored.sem, g + scored.at(1))
                        elif row_scale is not None:
                            v.tensor_tensor(res[k][:, :, 0:D], res[k][:, :, 0:D], row_scale[:, tiles].unsqueeze(2).to_broadcast([P, NG, D]),
                                            ALU.mult).then_inc(scored.sem, 1)
                        elif keep is not None:
                            v.tensor_copy(keep[0][:, tiles, :], res[k][:, :, keep[1]:keep[1] + D]).then_inc(scored.sem, 1)
                        else:
                            v.sem_inc(scored.sem, 1)

            @block.tensor
            def _(pe):
                pe.wait_ge(ld.sem, ld.at(nload))
                pe.wait_ge(ini.sem, ini.at(2))
                with pe.Fori(0, NNG // 2) as i:
                    for k in range(2):
                        g = 2 * i + k
                        pe.wait_ge(staged.sem, g + staged.at(1))
                        pe.sem_inc(pe_gate.sem, 1)
                        for t in range(NG):
                            ins = pe.transpose(trp[0:D, t * P:(t + 1) * P], stage[k][:, t, :], C.ident[:, :])
                        ins.then_inc(turned.sem, 1)
                        pe.wait_ge(moved.sem, g + moved.at(1))
                        for t in range(NG):
                            ins = pe.matmul(acc[:, t * pitch:t * pitch + width], hT[:, t * P:(t + 1) * P], w_sb[:, :], start=True, stop=True)
                        ins.then_inc(turned.sem, 1)

            @block.scalar
            def _(act):
                act.wait_ge(ini.sem, ini.at(2))
                with act.Fori(0, NNG // 2) as i:
                    for k in range(2):
                        g = 2 * i + k
                        act.wait_ge(turned.sem, g * 2 + turned.at(1))
                        act.activation(hT[0:D, :], trp[0:D, 0:NG * P], ACT.Copy).then_inc(moved.sem, 1)
                        act.wait_ge(turned.sem, g * 2 + turned.at(2))
                        act.activation(res[k][:, :, 0:width], acc[:, 0:NG * pitch].rearrange("p (t c) -> p t c", t=NG)[:, :, 0:width],
                                       ACT.Copy).then_inc(made.sem, 1)
        ld.passed(nload)
        ini.passed(2)
        for c in (staged, moved, made, scored):
            c.passed(NNG)
        turned.passed(2 * NNG)
        free.passed(NNG + 2)
        for k in range(2):
            stored[k].passed(nstore * (NNG // 2))
            scat[k].passed(nscat * (NNG // 2))
            ixl[k].passed(nix * (NNG // 2))
        if scores:
            products.passed(2 * NNG)



def groups(eng):
    with eng.Fori(0, NGRP // S - 1) as i:
        for k in range(S):
            yield i, k, (i + (k + 1) // S, (k + 1) % S)
    i = NGRP // S - 1
    for k in range(S):
        yield i, k, (i, k + 1) if k + 1 < S else None


class EdgeIO:

    def __init__(self, pr, tag, ctx, loads, table, width, part, part_width):
        self.table, self.part = table, part
        self.slot = {n: [pr.sb(f"{tag}_{n}{k}", s, t, ctx) for k in range(S)] for n, s, t, _ in loads}
        self.loads = {n: f for n, _, _, f in loads}
        self.rows = [pr.sb(f"{tag}_rows{k}", [P, G, width], F32, ctx) for k in range(S)]
        self.out = [pr.sb(f"{tag}_out{k}", [P, G, part_width], F32, ctx) for k in range(S)]
        self.loaded = [pr.count(f"e_loaded{k}") for k in range(S)]
        self.gathered = [pr.count(f"e_gathered{k}") for k in range(S)]
        self.stored = [pr.count(f"e_stored{k}") for k in range(S)]
        self.done, self.free, self.gate = pr.count("e_done"), pr.count("e_out_free"), pr.count("e_gate")
        self.ready = pr.count("e_ready")
        self.per_load = 16 * sum(len(f) for f in self.loads.values())

    def sync(self, sp):
        view = self.part.rearrange("(t p) w -> p t w", p=P)

        def load_group(g, k):
            for n, parts in self.loads.items():
                for part, source in parts:
                    sp.dma_start(part(self.slot[n][k]), source(g)).then_inc(self.loaded[k].sem, 16)

        for k in range(S):
            load_group(k, k)
        sp.sem_inc(self.free.sem, S)
        for i, k, after in groups(sp):
            g = S * i + k
            sp.wait_ge(self.done.sem, g + self.done.at(1))
            if not (isinstance(i, int)):
                load_group(g + S, k)
            sp.dma_start(view[:, bass.ds(G * g, G), :], self.out[k][:, :, :]).then_inc(self.stored[k].sem, 16)
            sp.wait_ge(self.stored[k].sem, i * 16 + self.stored[k].at(16))
            sp.sem_inc(self.free.sem, 1)

    def gather(self, gp):
        index = next(iter(self.slot))
        for i, k, after in groups(gp):
            self.wait_loaded(gp, i, k)
            gp.sem_inc(self.gate.sem, 1)
            for t in range(G):
                gp.indirect_dma_start(self.rows[k][:, t, :], None, self.table,
                                      bass.IndirectOffsetOnAxis(ap=self.slot[index][k][:, t:t + 1], axis=0))\
                    .then_inc(self.gathered[k].sem, 16)

    def wait_loaded(self, eng, i, k):
        eng.wait_ge(self.loaded[k].sem, i * self.per_load + self.loaded[k].at(self.per_load))

    def wait_gathered(self, eng, i, k):
        eng.wait_ge(self.gathered[k].sem, i * (16 * G) + self.gathered[k].at(16 * G))

    def wait_out_free(self, eng, g):
        eng.wait_ge(self.free.sem, g + self.free.at(1))

    def passed(self):
        for k in range(S):
            self.loaded[k].passed(self.per_load * (NGRP // S))
            self.gathered[k].passed(16 * G * (NGRP // S))
            self.stored[k].passed(16 * (NGRP // S))
        self.done.passed(NGRP)
        self.free.passed(NGRP + S)
        self.ready.passed(NGRP + 1)


def whole(a):
    return a[:, :]


def whole3(a):
    return a[:, :, :]


def tile_rows(rows):
    view = rows.rearrange("(t p) w -> p t w", p=P)
    return lambda g: view[:, bass.ds(G * g, G), :]


def common_loads(index_col, seg_col):
    return [("index", [P, G], I32, [(whole, lambda g: index_col[:, bass.ds(G * g, G)])]),
            ("seg", [P, G], F32, [(whole, lambda g: seg_col[:, bass.ds(G * g, G)])])]


def banked(ps, w):
    if G * w <= 512:
        return ps[:, 0:G * w].rearrange("p (a c) -> p a c", a=1), 1, lambda t: t * w
    return ps[:, :].rearrange("p (a c) -> p a c", a=2)[:, :, 0:4 * w], 2, lambda t: (t // 4) * 512 + (t % 4) * w


def softmax_edges(pr, C, tag, H, table, seg_col, index_col, heads, fk, part, edge_w=None):
    nc = pr.nc
    gat = H == 8
    HW = 8 if gat else D
    W = D + H
    NF = G * H if gat else G
    with ExitStack() as ctx:
        loads = common_loads(index_col, seg_col) + [
            ("heads", [P, G, HW], F32, [(whole3, tile_rows(heads))]),
            ("fk", [NF, P + 1], F32, [(whole, lambda g: fk[bass.ds(NF * g, NF), :])]),
        ]
        if not gat:
            loads.append(("attr", [P, G, 32], F32, [(whole3, tile_rows(C.edge_attr))]))
        io = EdgeIO(pr, tag, ctx, loads, table, D + 8 if gat else 2 * D, part, W + H)
        slots = io.slot
        same = [pr.sb(f"{tag}_same{k}", [P, G, P], F32, ctx) for k in range(2)]
        score = pr.sb(f"{tag}_score", [P, G, H], F32, ctx)
        leaky = pr.sb(f"{tag}_leaky", [P, G, H], F32, ctx)
        fwd = pr.sb(f"{tag}_fwd", [NF, P], F32, ctx)
        bwd = pr.sb(f"{tag}_bwd", [NF, P], F32, ctx)
        shifted = pr.sb(f"{tag}_shifted", [P, G, H], F32, ctx)
        vals = pr.sb(f"{tag}_vals", [P, G, W], F32, ctx)
        weight = pr.sb(f"{tag}_weight", [P, G, H], F32, ctx)
        row_ps = pr.ps(f"{tag}_row_ps", [P, G * P], ctx)
        small = pr.ps(f"{tag}_small", [P, 512], ctx)
        head_ps = pr.ps(f"{tag}_head_ps", [P, 512], ctx)
        sum_ps = pr.ps(f"{tag}_sum_ps", [P, 1024], ctx)
        if not gat:
            ew = pr.sb(f"{tag}_ew", [P, 4, D], F32, ctx)
            attrT = pr.sb(f"{tag}_attrT", [P, 2, P], F32, ctx)
            both = pr.sb(f"{tag}_both", [P, G, 2, D], F32, ctx)
            prod = pr.sb(f"{tag}_prod", [P, G, D], F32, ctx)
            attr_ps = pr.ps(f"{tag}_attr_ps", [P, 512], ctx)
            edge_ps = pr.ps(f"{tag}_edge_ps", [P, 512], ctx)
        sums, _, sum_at = banked(sum_ps, W)
        c = {n: pr.count("s_" + n) for n in ("rowed", "same", "spread", "scored", "turned", "peaked", "back", "shifted",
                                             "weighed", "valued", "summed", "dve", "act", "edge_w", "attr_turned",
                                             "attr_moved", "edged", "ew_loaded")}
        pe_gate = pr.count("pe_gate")
        dper = 2 if gat else 3
        with nc.Block() as block:
            @block.sync
            def _(sp):
                if not gat:
                    sp.wait_ge(c["edge_w"].sem, c["edge_w"].at(1))
                    for q in range(4):
                        sp.dma_start(ew[32 * q:32 * q + 32, q, :], edge_w).then_inc(c["ew_loaded"].sem, 16)
                io.sync(sp)

            @block.gpsimd
            def _(gp):
                io.gather(gp)

            @block.vector
            def _(v):
                if not gat:
                    v.memset(ew[:, :, :], 0.0).then_inc(c["edge_w"].sem, 1)

                def compare(i, k):
                    g = S * i + k
                    io.wait_loaded(v, i, k)
                    v.wait_ge(c["rowed"].sem, g + c["rowed"].at(1))
                    v.tensor_tensor(same[k % 2][:, :, :], row_ps[:, :].rearrange("p (t e) -> p t e", t=G),
                                    slots["seg"][k][:, :].unsqueeze(2).to_broadcast([P, G, P]), ALU.is_equal)\
                        .then_inc(c["same"].sem, 1)

                compare(0, 0)
                for i, k, after in groups(v):
                    g = S * i + k
                    ch = Chain(v, c["dve"], dper, g)
                    rows, fks = io.rows[k], slots["fk"][k]
                    io.wait_loaded(v, i, k)
                    io.wait_gathered(v, i, k)
                    if gat:
                        v.wait_ge(c["spread"].sem, g + c["spread"].at(1))
                        ch.link(v.tensor_tensor(score[:, :, :], rows[:, :, D:D + H],
                                                head_ps[:, 0:G * H].rearrange("p (t h) -> p t h", t=G), ALU.add))
                        v.scalar_tensor_tensor(out=leaky[:, :, :], in0=score[:, :, :], scalar=0.2, in1=score[:, :, :],
                                               op0=ALU.mult, op1=ALU.max).then_inc(c["scored"].sem, 1)
                    else:
                        v.wait_ge(c["edged"].sem, g + c["edged"].at(1))
                        ch.link(v.tensor_tensor(both[:, :, :, :], rows[:, :, :].rearrange("p t (j d) -> p t j d", j=2),
                                                edge_ps[:, :].rearrange("p (t d) -> p t d", t=G).unsqueeze(2)
                                                .to_broadcast([P, G, 2, D]), ALU.add))
                        v.wait_ge(c["spread"].sem, g + c["spread"].at(1))
                        ch.link(v.scalar_tensor_tensor(out=prod[:, :, :], in0=both[:, :, 0, :], scalar=float(D) ** -0.5,
                                                       in1=head_ps[:, :].rearrange("p (t d) -> p t d", t=G),
                                                       op0=ALU.mult, op1=ALU.mult))
                        v.tensor_reduce(leaky[:, :, :], prod[:, :, :], AX, ALU.add).then_inc(c["scored"].sem, 1)
                    v.wait_ge(io.ready.sem, g + io.ready.at(1))
                    if after:
                        compare(*after)
                    v.wait_ge(c["turned"].sem, g + c["turned"].at(1))
                    v.tensor_tensor_scan(fwd[:, :], fks[:, 0:P], small[0:NF, 0:P], -BIG, ALU.add, ALU.max)
                    ch.link(v.tensor_tensor_scan(bwd[:, ::-1], fks[:, 1:P + 1][:, ::-1], small[0:NF, 0:P][:, ::-1], -BIG,
                                                 ALU.add, ALU.max))
                    v.tensor_tensor(fwd[:, :], fwd[:, :], bwd[:, :], ALU.max).then_inc(c["peaked"].sem, 1)
                    v.wait_ge(c["back"].sem, g + c["back"].at(1))
                    v.tensor_tensor(shifted[:, :, :], leaky[:, :, :],
                                    small[:, P:P + G * H].rearrange("p (t h) -> p t h", t=G), ALU.subtract)\
                        .then_inc(c["shifted"].sem, 1)
                    v.wait_ge(c["weighed"].sem, g + c["weighed"].at(1))
                    v.tensor_copy(vals[:, :, D:D + H], weight[:, :, :])
                    if gat:
                        ins = v.tensor_tensor(vals[:, :, 0:D].rearrange("p t (h d) -> p t h d", h=H),
                                              rows[:, :, 0:D].rearrange("p t (h d) -> p t h d", h=H),
                                              weight[:, :, :].unsqueeze(3).to_broadcast([P, G, H, D // H]), ALU.mult)
                    else:
                        ins = v.tensor_tensor(vals[:, :, 0:D], both[:, :, 1, :], weight[:, :, :].to_broadcast([P, G, D]), ALU.mult)
                    ins.then_inc(c["valued"].sem, 1)
                    v.wait_ge(c["valued"].sem, g + c["valued"].at(1))
                    ch.close()

            @block.tensor
            def _(pe):
                if not gat:
                    pe.wait_ge(c["ew_loaded"].sem, c["ew_loaded"].at(64))

                def lay_out(i, k):
                    g = S * i + k
                    io.wait_loaded(pe, i, k)
                    for t in range(G):
                        ins = pe.transpose(row_ps[:, t * P:(t + 1) * P], slots["seg"][k][:, t:t + 1].to_broadcast([P, P]), C.ident[:, :])
                    ins.then_inc(c["rowed"].sem, 1)

                def features(i, k):
                    g = S * i + k
                    for q in range(2):
                        ins = pe.transpose(attr_ps[:, q * P:(q + 1) * P],
                                           slots["attr"][k][:, 4 * q:4 * q + 4, :].rearrange("p t c -> p (t c)"), C.ident[:, :])
                    ins.then_inc(c["attr_turned"].sem, 1)
                    pe.wait_ge(c["attr_moved"].sem, g + c["attr_moved"].at(1))
                    for q in range(2):
                        ins = pe.matmul(edge_ps[:, q * 256:(q + 1) * 256], attrT[:, q, :], ew[:, :, :].rearrange("p q d -> p (q d)"),
                                        start=True, stop=True)
                    ins.then_inc(c["edged"].sem, 1)

                def spread(i, k):
                    g = S * i + k
                    pe.wait_ge(c["same"].sem, g + c["same"].at(1))
                    for t in range(G):
                        ins = pe.matmul(head_ps[:, t * HW:(t + 1) * HW], same[k % 2][:, t, :], slots["heads"][k][:, t, :], start=True, stop=True)
                    ins.then_inc(c["spread"].sem, 1)

                lay_out(0, 0)
                if not gat:
                    features(0, 0)
                spread(0, 0)
                for i, k, after in groups(pe):
                    g = S * i + k
                    if after:
                        lay_out(*after)
                    pe.wait_ge(c["scored"].sem, g + c["scored"].at(1))
                    pe.wait_ge(io.ready.sem, g + io.ready.at(1))
                    pe.sem_inc(pe_gate.sem, 1)
                    pe.transpose(small[0:NF, 0:P], leaky[:, :, :].rearrange("p t h -> p (t h)"), C.ident[:, :]).then_inc(c["turned"].sem, 1)
                    if after and not gat:
                        features(*after)
                    pe.wait_ge(c["peaked"].sem, g + c["peaked"].at(1))
                    pe.sem_inc(pe_gate.sem, 1)
                    pe.transpose(small[:, P:P + NF], fwd[:, :], C.ident[0:NF, 0:NF]).then_inc(c["back"].sem, 1)
                    if after:
                        spread(*after)
                    pe.wait_ge(c["valued"].sem, g + c["valued"].at(1))
                    for t in range(G):
                        ins = pe.matmul(sum_ps[:, sum_at(t):sum_at(t) + W], same[k % 2][:, t, :], vals[:, t, :], start=True, stop=True)
                    ins.then_inc(c["summed"].sem, 1)

            @block.scalar
            def _(act):
                def move_features(i, k):
                    g = S * i + k
                    act.wait_ge(c["attr_turned"].sem, g + c["attr_turned"].at(1))
                    act.activation(attrT[:, :, :].rearrange("p q e -> p (q e)"), attr_ps[:, 0:2 * P], ACT.Copy)\
                        .then_inc(c["attr_moved"].sem, 1)

                act.sem_inc(io.ready.sem, 1)
                if not gat:
                    move_features(0, 0)
                for i, k, after in groups(act):
                    g = S * i + k
                    if after and not gat:
                        move_features(*after)
                    act.wait_ge(c["shifted"].sem, g + c["shifted"].at(1))
                    act.activation(weight[:, :, :], shifted[:, :, :], ACT.Exp).then_inc(c["weighed"].sem, 1)
                    io.wait_out_free(act, g)
                    act.activation(io.out[k][:, :, W:W + H], small[:, P:P + NF].rearrange("p (t h) -> p t h", t=G), ACT.Copy)\
                        .then_inc(c["act"].sem, 1)
                    act.wait_ge(c["summed"].sem, g + c["summed"].at(1))
                    act.activation(io.out[k][:, :, 0:W].rearrange("p (a b) w -> p a b w", a=sums.shape[1]),
                                   sums.rearrange("p a (b w) -> p a b w", w=W), ACT.Copy).then_inc(c["act"].sem, 1)
                    act.wait_ge(c["act"].sem, g * 2 + c["act"].at(2))
                    act.sem_inc(io.ready.sem, 1)
                    act.sem_inc(io.done.sem, 1)
        io.passed()
        for n in ("rowed", "same", "spread", "scored", "turned", "peaked", "back", "shifted", "weighed", "valued", "summed"):
            c[n].passed(NGRP)
        c["act"].passed(2 * NGRP)
        c["dve"].passed(dper * NGRP)
        if not gat:
            c["edge_w"].passed(1)
            c["ew_loaded"].passed(64)
            for n in ("attr_turned", "attr_moved", "edged"):
                c[n].passed(NGRP)


def mlp_edges(pr, C, table, heads, part, be2, We2):
    nc = pr.nc
    H2 = 2 * D
    tag = "m"
    with ExitStack() as ctx:
        def fk_of(par):
            view = C.fk_dst.rearrange("(g j two) c -> g two j c", two=2, j=G // 2)
            return lambda g: view[bass.ds(g, 1), par, :, 0:P].to_broadcast([D, G // 2, P])

        loads = common_loads(C.src_col_i, C.dst_col) + [
            ("heads", [P, G, H2], F32, [(whole3, tile_rows(heads))]),
            ("fk", [P, G // 2, P], F32, [(lambda a: a[0:D, :, :], fk_of(0)), (lambda a: a[D:P, :, :], fk_of(1))]),
        ]
        io = EdgeIO(pr, tag, ctx, loads, table, H2 + D, part, H2)
        slots = io.slot
        same = [pr.sb(f"m_same{k}", [P, G, P], F32, ctx) for k in range(2)]
        hidden = pr.sb("m_hidden", [P, G, H2], F32, ctx)
        logit = pr.sb("m_logit", [P, G], F32, ctx)
        gate = pr.sb("m_gate", [P, G], F32, ctx)
        msg = pr.sb("m_msg", [P, G, D], F32, ctx)
        top = pr.sb("m_top", [P, G // 2 * P], F32, ctx)
        w2 = pr.sb("m_w2", [P, H2], F32, ctx)
        b2 = pr.sb("m_b2", [P, 1], F32, ctx)
        row_ps = pr.ps("m_row_ps", [P, G * P], ctx)
        head_ps = pr.ps("m_head_ps", [P, G * H2], ctx)
        sum_ps = pr.ps("m_sum_ps", [P, 512], ctx)
        msgT_ps = pr.ps("m_msgT_ps", [P, 512], ctx)
        top_ps = pr.ps("m_top_ps", [P, 512], ctx)
        c = {n: pr.count("s_" + n) for n in ("rowed", "same", "spread", "scored", "turned", "peaked", "back",
                                             "weighed", "valued", "summed", "dve", "act", "edge_w")}
        with nc.Block() as block:
            @block.sync
            def _(sp):
                sp.dma_start(w2[:, :], We2.rearrange("k a -> a k").to_broadcast([P, H2])).then_inc(c["edge_w"].sem, 16)
                sp.dma_start(b2[:, :], be2.unsqueeze(0).to_broadcast([P, 1])).then_inc(c["edge_w"].sem, 16)
                io.sync(sp)

            @block.gpsimd
            def _(gp):
                io.gather(gp)

            @block.vector
            def _(v):
                def compare(i, k):
                    g = S * i + k
                    io.wait_loaded(v, i, k)
                    v.wait_ge(c["rowed"].sem, g + c["rowed"].at(1))
                    v.tensor_tensor(same[k % 2][:, :, :], row_ps[:, :].rearrange("p (t e) -> p t e", t=G),
                                    slots["seg"][k][:, :].unsqueeze(2).to_broadcast([P, G, P]), ALU.is_equal)\
                        .then_inc(c["same"].sem, 1)

                v.wait_ge(c["edge_w"].sem, c["edge_w"].at(32))
                compare(0, 0)
                for i, k, after in groups(v):
                    g = S * i + k
                    ch = Chain(v, c["dve"], 2, g)
                    rows = io.rows[k]
                    io.wait_loaded(v, i, k)
                    io.wait_gathered(v, i, k)
                    v.wait_ge(c["spread"].sem, g + c["spread"].at(1))
                    ch.link(v.tensor_tensor(hidden[:, :, :], rows[:, :, 0:H2],
                                            head_ps[:, :].rearrange("p (t w) -> p t w", t=G), ALU.add))
                    ch.link(v.scalar_tensor_tensor(out=hidden[:, :, :], in0=hidden[:, :, :], scalar=0.0,
                                                   in1=w2[:, :].unsqueeze(1).to_broadcast([P, G, H2]), op0=ALU.max, op1=ALU.mult))
                    v.tensor_reduce(logit[:, :], hidden[:, :, :], AX, ALU.add).then_inc(c["scored"].sem, 1)
                    v.wait_ge(io.ready.sem, g + io.ready.at(1))
                    if after:
                        compare(*after)
                    v.wait_ge(c["weighed"].sem, g + c["weighed"].at(1))
                    v.tensor_tensor(msg[:, :, :], rows[:, :, H2:H2 + D], gate[:, :].unsqueeze(2).to_broadcast([P, G, D]),
                                    ALU.mult).then_inc(c["valued"].sem, 1)
                    v.wait_ge(c["turned"].sem, g + c["turned"].at(1))
                    v.tensor_tensor_scan(top[:, :], slots["fk"][k][:, :, :].rearrange("p j e -> p (j e)"), msgT_ps[:, :],
                                         -BIG, ALU.add, ALU.max).then_inc(c["peaked"].sem, 1)
                    ch.close()

            @block.tensor
            def _(pe):
                def lay_out(i, k):
                    g = S * i + k
                    io.wait_loaded(pe, i, k)
                    for t in range(G):
                        ins = pe.transpose(row_ps[:, t * P:(t + 1) * P], slots["seg"][k][:, t:t + 1].to_broadcast([P, P]), C.ident[:, :])
                    ins.then_inc(c["rowed"].sem, 1)

                def spread(i, k):
                    g = S * i + k
                    pe.wait_ge(c["same"].sem, g + c["same"].at(1))
                    for t in range(G):
                        ins = pe.matmul(head_ps[:, t * H2:(t + 1) * H2], same[k % 2][:, t, :], slots["heads"][k][:, t, :], start=True, stop=True)
                    ins.then_inc(c["spread"].sem, 1)

                lay_out(0, 0)
                spread(0, 0)
                for i, k, after in groups(pe):
                    g = S * i + k
                    if after:
                        lay_out(*after)
                    pe.wait_ge(c["valued"].sem, g + c["valued"].at(1))
                    pe.wait_ge(io.ready.sem, g + io.ready.at(1))
                    for j in range(G // 2):
                        ins = pe.transpose(msgT_ps[:, j * P:(j + 1) * P], msg[:, 2 * j:2 * j + 2, :].rearrange("p t d -> p (t d)"), C.ident[:, :])
                    ins.then_inc(c["turned"].sem, 1)
                    if after:
                        spread(*after)
                    for t in range(G):
                        ins = pe.matmul(sum_ps[:, t * D:(t + 1) * D], same[k % 2][:, t, :], msg[:, t, :], start=True, stop=True)
                    ins.then_inc(c["summed"].sem, 1)
                    pe.wait_ge(c["peaked"].sem, g + c["peaked"].at(1))
                    for j in range(G // 2):
                        ins = pe.transpose(top_ps[:, j * P:(j + 1) * P], top[:, j * P:(j + 1) * P], C.ident[:, :])
                    ins.then_inc(c["back"].sem, 1)

            @block.scalar
            def _(act):
                act.wait_ge(c["edge_w"].sem, c["edge_w"].at(32))
                act.sem_inc(io.ready.sem, 1)
                for i, k, after in groups(act):
                    g = S * i + k
                    act.wait_ge(c["scored"].sem, g + c["scored"].at(1))
                    act.activation(gate[:, :], logit[:, :], ACT.Sigmoid, bias=b2[:, :]).then_inc(c["weighed"].sem, 1)
                    io.wait_out_free(act, g)
                    act.wait_ge(c["summed"].sem, g + c["summed"].at(1))
                    act.activation(io.out[k][:, :, 0:D], sum_ps[:, :].rearrange("p (t d) -> p t d", t=G), ACT.Copy).then_inc(c["act"].sem, 1)
                    act.wait_ge(c["back"].sem, g + c["back"].at(1))
                    act.activation(io.out[k][:, :, D:H2], top_ps[:, :].rearrange("p (t d) -> p t d", t=G), ACT.Copy).then_inc(c["act"].sem, 1)
                    act.wait_ge(c["act"].sem, g * 2 + c["act"].at(2))
                    act.sem_inc(io.ready.sem, 1)
                    act.sem_inc(io.done.sem, 1)
        io.passed()
        for n in ("rowed", "same", "spread", "scored", "turned", "peaked", "back", "weighed", "valued", "summed"):
            c[n].passed(NGRP)
        c["act"].passed(2 * NGRP)
        c["dve"].passed(2 * NGRP)
        c["edge_w"].passed(32)


def gcn_edges(pr, C, table, part):
    nc = pr.nc
    with ExitStack() as ctx:
        io = EdgeIO(pr, "g", ctx, common_loads(C.src_col_i, C.dst_col), table, D, part, D)
        slots = io.slot
        same = [pr.sb(f"g_same{k}", [P, G, P], F32, ctx) for k in range(S)]
        row_ps = pr.ps("g_row_ps", [P, G * P], ctx)
        sum_ps = pr.ps("g_sum_ps", [P, 512], ctx)
        c = {n: pr.count("s_" + n) for n in ("rowed", "same", "summed", "act")}
        with nc.Block() as block:
            @block.sync
            def _(sp):
                io.sync(sp)

            @block.gpsimd
            def _(gp):
                io.gather(gp)

            @block.vector
            def _(v):
                for i, k, after in groups(v):
                    g = S * i + k
                    io.wait_loaded(v, i, k)
                    v.wait_ge(c["rowed"].sem, g + c["rowed"].at(1))
                    v.tensor_tensor(same[k][:, :, :], row_ps[:, :].rearrange("p (t e) -> p t e", t=G),
                                    slots["seg"][k][:, :].unsqueeze(2).to_broadcast([P, G, P]), ALU.is_equal)\
                        .then_inc(c["same"].sem, 1)

            @block.tensor
            def _(pe):
                for i, k, after in groups(pe):
                    g = S * i + k
                    io.wait_loaded(pe, i, k)
                    for t in range(G):
                        ins = pe.transpose(row_ps[:, t * P:(t + 1) * P], slots["seg"][k][:, t:t + 1].to_broadcast([P, P]), C.ident[:, :])
                    ins.then_inc(c["rowed"].sem, 1)
                    pe.wait_ge(c["same"].sem, g + c["same"].at(1))
                    io.wait_gathered(pe, i, k)
                    pe.wait_ge(io.ready.sem, g + io.ready.at(1))
                    for t in range(G):
                        ins = pe.matmul(sum_ps[:, t * D:(t + 1) * D], same[k][:, t, :], io.rows[k][:, t, :], start=True, stop=True)
                    ins.then_inc(c["summed"].sem, 1)

            @block.scalar
            def _(act):
                act.sem_inc(io.ready.sem, 1)
                for i, k, after in groups(act):
                    g = S * i + k
                    io.wait_out_free(act, g)
                    act.wait_ge(c["summed"].sem, g + c["summed"].at(1))
                    act.activation(io.out[k][:, :, :], sum_ps[:, :].rearrange("p (t d) -> p t d", t=G), ACT.Copy).then_inc(c["act"].sem, 1)
                    act.wait_ge(c["act"].sem, g + c["act"].at(1))
                    act.sem_inc(io.ready.sem, 1)
                    act.sem_inc(io.done.sem, 1)
        io.passed()
        for n in ("rowed", "same", "summed", "act"):
            c[n].passed(NGRP)


def carry(pr, C, kind, part, carry_dram, keep, H=0):
    nc = pr.nc
    soft = kind == "softmax"
    W = {"sum": D, "sum_max": 2 * D, "softmax": D + H}[kind]
    with ExitStack() as ctx:
        t_rows = pr.sb("c_rows", [RB, NB, W + H], F32, ctx)
        wide = pr.sb("c_wide", [RB, NB, W], F32, ctx)
        n = [pr.sb(f"c_buf{j}", [P, ET], F32, ctx) for j in range(6 if soft else 3)]
        back = pr.sb("c_back", [RB, NB, 2 * W if soft else W], F32, ctx)
        ps = [pr.ps(f"c_ps{j}", [P, 2048], ctx) for j in range(2)]
        ld, dv, tr, ex, st = (pr.count("c_" + x) for x in ("loaded", "dve", "turned", "exp", "stored"))
        marks = {}
        with nc.Block() as block:
            @block.sync
            def _(sp):
                sp.dma_start(t_rows[:, :, :], part.rearrange("(b r e) w -> r b e w", r=RB, e=P)[:, :, P - 1, :]).then_inc(ld.sem, 16)

            @block.vector
            def _(v):
                ch = Chain(v, dv)
                v.wait_ge(ld.sem, ld.at(16))
                if soft:
                    ch.link(v.tensor_copy(wide[:, :, 0:D].rearrange("r b (h d) -> r b h d", h=H),
                                          t_rows[:, :, W:W + H].unsqueeze(3).to_broadcast([RB, NB, H, D // H])))
                    ch.link(v.tensor_copy(wide[:, :, D:W], t_rows[:, :, W:W + H]))
                marks["wide"] = ch.n
                v.wait_ge(tr.sem, tr.at(1))
                val, pen = n[0], n[1]
                ch.link(v.tensor_scalar(pen[:, :], keep[:, :], BIG, -BIG, ALU.mult, ALU.add))
                ch.link(v.tensor_copy(by_bank(val[0:W, :]), blocks(ps[0])[0:W]))
                if kind == "sum":
                    ch.link(v.tensor_tensor_scan(n[2][0:W, :], keep[0:W, :], val[0:W, :], 0.0, ALU.mult, ALU.add))
                elif kind == "sum_max":
                    ch.link(v.tensor_tensor_scan(n[2][0:D, :], keep[0:D, :], val[0:D, :], 0.0, ALU.mult, ALU.add))
                    ch.link(v.tensor_tensor_scan(n[2][D:W, :], pen[D:W, :], val[D:W, :], -BIG, ALU.add, ALU.max))
                else:
                    top, peak, ratio = n[2], n[3], n[4]
                    ch.link(v.tensor_copy(by_bank(top[0:W, :]), blocks(ps[1])[0:W]))
                    ch.link(v.tensor_tensor_scan(peak[0:W, :], pen[0:W, :], top[0:W, :], -BIG, ALU.add, ALU.max))
                    ch.link(v.memset(ratio[0:W, 0:1], 0.0))
                    ch.link(v.tensor_tensor(ratio[0:W, 1:ET], peak[0:W, 0:ET - 1], peak[0:W, 1:ET], ALU.subtract))
                    ch.link(v.tensor_scalar(ratio[0:W, :], ratio[0:W, :], 0.0, None, ALU.min))
                    ch.link(v.tensor_tensor(top[0:W, :], top[0:W, :], peak[0:W, :], ALU.subtract))
                    marks["exp"] = ch.n
                    v.wait_ge(ex.sem, ex.at(2))
                    ch.link(v.tensor_tensor(ratio[0:W, :], ratio[0:W, :], keep[0:W, :], ALU.mult))
                    ch.link(v.tensor_tensor(val[0:W, :], val[0:W, :], top[0:W, :], ALU.mult))
                    ch.link(v.tensor_tensor_scan(n[5][0:W, :], ratio[0:W, :], val[0:W, :], 0.0, ALU.mult, ALU.add))
                marks["scanned"] = ch.n
                v.wait_ge(tr.sem, tr.at(2))
                for j in range(2 if soft else 1):
                    ch.link(v.tensor_copy(back[:, :, j * W:(j + 1) * W], ps[j][0:RB, :].rearrange("r (b w) -> r b w", b=NB)[:, :, 0:W]))
                marks["back"] = ch.n

            @block.tensor
            def _(pe):
                pe.wait_ge(ld.sem, ld.at(16))
                if soft:
                    pe.wait_ge(dv.sem, dv.at(marks["wide"]))
                for j in range(2 if soft else 1):
                    for b in range(NB):
                        ins = pe.transpose(ps[j][0:W, block_at(b):block_at(b) + RB], t_rows[:, b, 0:W] if j == 0 else wide[:, b, :],
                                           C.ident[0:RB, 0:RB])
                ins.then_inc(tr.sem, 1)
                pe.wait_ge(dv.sem, dv.at(marks["scanned"]))
                res = (n[5], n[3]) if soft else (n[2],)
                for j, r in enumerate(res):
                    for b in range(NB):
                        ins = pe.transpose(ps[j][0:RB, b * P:b * P + W], r[0:W, b * RB:(b + 1) * RB], C.ident[0:W, 0:W])
                ins.then_inc(tr.sem, 1)

            @block.scalar
            def _(act):
                if soft:
                    act.wait_ge(dv.sem, dv.at(marks["exp"]))
                    act.activation(n[4][0:W, :], n[4][0:W, :], ACT.Exp).then_inc(ex.sem, 1)
                    act.activation(n[2][0:W, :], n[2][0:W, :], ACT.Exp).then_inc(ex.sem, 1)
                act.wait_ge(dv.sem, dv.at(marks["back"]))
                act.dma_start(carry_dram.rearrange("(b r) w -> r b w", r=RB), back[:, :, :]).then_inc(st.sem, 16)
                act.wait_ge(st.sem, st.at(16))
        ld.passed(16)
        dv.passed(marks["back"])
        tr.passed(2)
        st.passed(16)
        if soft:
            ex.passed(2)


def node_results(pr, C, kind, part, carry_dram, ix, has, spans, result, H=0, eps=0.0):
    nc = pr.nc
    soft = kind == "softmax"
    W = {"sum": D, "sum_max": 2 * D, "softmax": D + H}[kind]
    PW, CW = W + H, 2 * W if soft else W
    with ExitStack() as ctx:
        index = [pr.sb(f"n_index{k}", [P, 2, NG], I32, ctx) for k in range(2)]
        own = [pr.sb(f"n_own{k}", [P, NG, PW], F32, ctx) for k in range(2)]
        old = [pr.sb(f"n_old{k}", [P, NG, CW], F32, ctx) for k in range(2)]
        pen = pr.sb("n_pen", [P, NG], F32, ctx)
        top = pr.sb("n_top", [P, NG, max(H, 1)], F32, ctx)
        dif = pr.sb("n_dif", [P, NG, 2, max(H, 1)], F32, ctx)
        mul = pr.sb("n_mul", [P, NG, 2, max(H, 1)], F32, ctx)
        acc = pr.sb("n_acc", [P, NG, W], F32, ctx)
        ld = [pr.count(f"n_loaded{k}") for k in range(2)]
        got = [pr.count(f"n_gathered{k}") for k in range(2)]
        done, dv, ask, ex, gate = (pr.count("n_" + x) for x in ("done", "dve", "asked", "exp", "gate"))
        per = 12 if soft else {"sum": 3, "sum_max": 5}[kind]
        with nc.Block() as block:
            @block.sync
            def _(sp):
                def load(g, k):
                    for q in range(2):
                        sp.dma_start(index[k][:, q, :], ix[1 + q][:, bass.ds(NG * g, NG)]).then_inc(ld[k].sem, 16)
                for k in range(2):
                    load(k, k)
                with sp.Fori(0, NNG // 2 - 1) as i:
                    for k in range(2):
                        sp.wait_ge(done.sem, 2 * i + done.at(k + 1))
                        load(2 * i + (k + 2), k)

            @block.gpsimd
            def _(gp):
                with gp.Fori(0, NNG // 2) as i:
                    for k in range(2):
                        gp.wait_ge(ld[k].sem, i * 32 + ld[k].at(32))
                        gp.sem_inc(gate.sem, 1)
                        for q, (rows, src) in enumerate(((own[k], part), (old[k], carry_dram))):
                            for t in range(NG):
                                gp.indirect_dma_start(rows[:, t, :], None, src,
                                                      bass.IndirectOffsetOnAxis(ap=index[k][:, q, t:t + 1], axis=0)).then_inc(got[k].sem, 16)

            @block.vector
            def _(v):
                with v.Fori(0, NNG // 2) as i:
                    for k in range(2):
                        g = 2 * i + k
                        ch = Chain(v, dv, per, g)
                        tiles = bass.ds(NG * g, NG)
                        over = lambda m, w: m[:, tiles].unsqueeze(2).to_broadcast([P, NG, w])
                        v.wait_ge(got[k].sem, i * (32 * NG) + got[k].at(32 * NG))
                        o, c = own[k], old[k]
                        if not soft:
                            ch.link(v.tensor_tensor(c[:, :, 0:D], c[:, :, 0:D], over(spans, D), ALU.mult))
                            ch.link(v.tensor_tensor(o[:, :, 0:D], o[:, :, 0:D], c[:, :, 0:D], ALU.add))
                            if kind == "sum_max":
                                ch.link(v.tensor_tensor(c[:, :, D:W], c[:, :, D:W], over(spans, D), ALU.mult))
                                ch.link(v.tensor_tensor(o[:, :, D:W], o[:, :, D:W], c[:, :, D:W], ALU.max))
                            ch.link(v.tensor_tensor(result[:, tiles, :], o[:, :, :], over(has, W), ALU.mult))
                        else:
                            ch.link(v.tensor_scalar(pen[:, :], spans[:, tiles], BIG, -BIG, ALU.mult, ALU.add))
                            cm = c[:, :, W + D:W + D + H]
                            ch.link(v.tensor_tensor(cm, cm, pen[:, :].unsqueeze(2).to_broadcast([P, NG, H]), ALU.add))
                            ch.link(v.tensor_tensor(top[:, :, :], o[:, :, W:W + H], cm, ALU.max))
                            ch.link(v.tensor_tensor(dif[:, :, 0, :], o[:, :, W:W + H], top[:, :, :], ALU.subtract))
                            ch.link(v.tensor_tensor(dif[:, :, 1, :], cm, top[:, :, :], ALU.subtract))
                            v.sem_inc(ask.sem, 1)
                            v.wait_ge(ex.sem, g + ex.at(1))
                            for q, rows in enumerate((o, c)):
                                v.tensor_tensor(rows[:, :, 0:D].rearrange("p t (h d) -> p t h d", h=H),
                                                rows[:, :, 0:D].rearrange("p t (h d) -> p t h d", h=H),
                                                mul[:, :, q, :].unsqueeze(3).to_broadcast([P, NG, H, D // H]), ALU.mult)
                                ch.link(v.tensor_tensor(rows[:, :, D:W], rows[:, :, D:W], mul[:, :, q, :], ALU.mult))
                            ch.link(v.tensor_tensor(acc[:, :, :], o[:, :, 0:W], c[:, :, 0:W], ALU.add))
                            ch.link(v.tensor_scalar(acc[:, :, D:W], acc[:, :, D:W], eps, None, ALU.add))
                            ch.link(v.reciprocal(acc[:, :, D:W], acc[:, :, D:W]))
                            ch.link(v.tensor_tensor(acc[:, :, D:W], acc[:, :, D:W], over(has, H), ALU.mult))
                            ch.link(v.tensor_tensor(result[:, tiles, :].rearrange("p t (h d) -> p t h d", h=H),
                                                    acc[:, :, 0:D].rearrange("p t (h d) -> p t h d", h=H),
                                                    acc[:, :, D:W].unsqueeze(3).to_broadcast([P, NG, H, D // H]), ALU.mult))
                        v.sem_inc(done.sem, 1)
                        ch.close()

            @block.scalar
            def _(act):
                if soft:
                    with act.Fori(0, NNG) as i:
                        act.wait_ge(ask.sem, i + ask.at(1))
                        act.activation(mul[:, :, :, :], dif[:, :, :, :], ACT.Exp).then_inc(ex.sem, 1)
        for k in range(2):
            ld[k].passed(32 * (NNG // 2))
            got[k].passed(32 * NG * (NNG // 2))
        done.passed(NNG)
        dv.passed(per * NNG)
        if soft:
            ask.passed(NNG)
            ex.passed(NNG)


def elementwise(pr, steps):
    dv = pr.count("ew_steps")
    with pr.nc.Block() as block:
        @block.vector
        def _(v):
            ch = Chain(v, dv)
            for step in steps:
                ch.link(step(v))
    dv.passed(len(steps))


def node_mlp(pr, C, msgs, h, Wn1, bn1, Wn2, bn2, result):
    nc = pr.nc
    with ExitStack() as ctx:
        w1m = pr.sb("nm_w1m", [P, P], F32, ctx)
        w1h = pr.sb("nm_w1h", [D, P], F32, ctx)
        w2 = pr.sb("nm_w2", [P, D], F32, ctx)
        b1 = pr.sb("nm_b1", [P, 1], F32, ctx)
        b2 = pr.sb("nm_b2", [P, D], F32, ctx)
        sm = pr.sb("nm_sm", [P, NG, P], F32, ctx)
        sh = pr.sb("nm_sh", [P, NG, D], F32, ctx)
        mT = pr.sb("nm_mT", [P, NG * P], F32, ctx)
        hT = pr.sb("nm_hT", [D, NG * P], F32, ctx)
        hid = pr.sb("nm_hid", [P, NG * P], F32, ctx)
        pm = pr.ps("nm_pm", [P, 1024], ctx)
        ph = pr.ps("nm_ph", [P, 1024], ctx)
        p1 = pr.ps("nm_p1", [P, 1024], ctx)
        p2 = pr.ps("nm_p2", [P, 512], ctx)
        ld, stg, tr, mv, l1, l1a, l2, fin = (pr.count("nm_" + x) for x in ("loaded", "staged", "turned", "moved", "first",
                                                                          "activated", "second", "finished"))
        with nc.Block() as block:
            @block.sync
            def _(sp):
                sp.dma_start(w1m[0:D, :], Wn1[D:2 * D, :]).then_inc(ld.sem, 16)
                sp.dma_start(w1m[D:P, :], Wn1[0:D, :]).then_inc(ld.sem, 16)
                sp.dma_start(w1h[:, :], Wn1[2 * D:3 * D, :]).then_inc(ld.sem, 16)
                sp.dma_start(w2[:, :], Wn2).then_inc(ld.sem, 16)
                with nc.allow_non_contiguous_dma(reason="a bias, a word a partition"):
                    sp.dma_start(b1[:, :], bn1.unsqueeze(1)).then_inc(ld.sem, 16)
                sp.dma_start(b2[:, :], bn2.unsqueeze(0).to_broadcast([P, D])).then_inc(ld.sem, 16)

            @block.vector
            def _(v):
                v.wait_ge(ld.sem, 96)
                with v.Fori(0, NNG) as i:
                    tiles = bass.ds(NG * i, NG)
                    v.tensor_copy(sm[:, :, :], msgs[:, tiles, :])
                    v.tensor_copy(sh[:, :, :], h[:, tiles, :]).then_inc(stg.sem, 1)
                    v.wait_ge(l2.sem, i + 1)
                    v.tensor_tensor(result[:, tiles, :], p2[:, 0:NG * D].rearrange("p (t d) -> p t d", t=NG),
                                    b2[:, :].unsqueeze(1).to_broadcast([P, NG, D]), ALU.add).then_inc(fin.sem, 1)

            @block.tensor
            def _(pe):
                pe.wait_ge(ld.sem, 96)
                with pe.Fori(0, NNG) as i:
                    pe.wait_ge(stg.sem, i + 1)
                    for t in range(NG):
                        pe.transpose(pm[:, t * P:(t + 1) * P], sm[:, t, :], C.ident[:, :])
                        ins = pe.transpose(ph[0:D, t * P:(t + 1) * P], sh[:, t, :], C.ident[:, :])
                    ins.then_inc(tr.sem, 1)
                    pe.wait_ge(mv.sem, i * 2 + 2)
                    for a, b in ((0, 512), (512, NG * P)):
                        pe.matmul(p1[:, a:b], w1m[:, :], mT[:, a:b], start=True, stop=False)
                        ins = pe.matmul(p1[:, a:b], w1h[:, :], hT[:, a:b], start=False, stop=True)
                    ins.then_inc(l1.sem, 1)
                    pe.wait_ge(l1a.sem, i + 1)
                    for t in range(NG):
                        ins = pe.matmul(p2[:, t * D:(t + 1) * D], hid[:, t * P:(t + 1) * P], w2[:, :], start=True, stop=True)
                    ins.then_inc(l2.sem, 1)

            @block.scalar
            def _(act):
                act.wait_ge(ld.sem, 96)
                with act.Fori(0, NNG) as i:
                    act.wait_ge(tr.sem, i + 1)
                    act.activation(mT[:, :], pm[:, 0:NG * P], ACT.Copy).then_inc(mv.sem, 1)
                    act.activation(hT[:, :], ph[0:D, 0:NG * P], ACT.Copy).then_inc(mv.sem, 1)
                    act.wait_ge(l1.sem, i + 1)
                    act.activation(hid[:, :], p1[:, 0:NG * P], ACT.Relu, bias=b1[:, :]).then_inc(l1a.sem, 1)


def gnn(nc, A, out):
    with ExitStack() as ctx:
        pr = Program(nc, ctx)

        class C:
            pass
        C.src, C.dst, C.edge_attr = A["src"], A["dst"], A["edge_attr_32"]
        C.pairs = pr.dram("pairs", (P, ET * 2))
        C.src_col_i = pr.dram("src_col_i", (P, ET), I32)
        C.src_col = pr.dram("src_col", (P, ET))
        C.dst_col = pr.dram("dst_col", (P, ET))
        C.fk_dst = pr.dram("fk_dst", (ET, P + 1))
        C.fk_src = pr.dram("fk_src", (ET, 8, P + 1))
        C.sorted_pairs = pr.dram("sorted_pairs", (NE, 2))
        C.dst_of_sorted = pr.dram("dst_of_sorted", (P, ET), I32)
        C.src_sorted_col = pr.dram("src_sorted_col", (P, ET))
        C.heads8, C.heads64, C.heads128 = (pr.dram(f"heads{w}", (NE, w)) for w in (8, 64, 128))
        C.ix_dst, C.ix_src = (pr.dram(n, (3, P, NT), I32) for n in ("ix_dst", "ix_src"))
        C.cnt_d, C.start_d, C.has_d, C.spans_d = (pr.sb(n + "_d", [P, NT]) for n in ("cnt", "start", "has", "spans"))
        C.cnt_s, C.start_s, C.has_s, C.spans_s = (pr.sb(n + "_s", [P, NT]) for n in ("cnt", "start", "has", "spans"))
        C.deg_scale = pr.sb("deg_scale", [P, NT])
        C.keep_d, C.keep_s = (pr.sb(n, [P, ET]) for n in ("keep_d", "keep_s"))
        C.first_d, C.first_s = (pr.sb(n, [RB, NB], I32) for n in ("first_d", "first_s"))
        constants(pr, C)
        zero_heads(pr, C)
        with ExitStack() as early:
            C.seg_sb = pr.sb("seg_sb", [P, ET], F32, early)
            C.lo_d, C.hi_d, C.lo_s, C.hi_s = (pr.sb(n, [P, ET], F32, early) for n in ("lo_d", "hi_d", "lo_s", "hi_s"))
            read_ids(pr, C)
            count_nodes(pr, C)
            sort_by_src(pr, C)
        read_sorted(pr, C)
        node_bounds(pr, C)
        tile_starts(pr, C)

        x, h, skip = (pr.sb(n, [P, NT, D]) for n in ("x", "h", "skip"))
        ld, st, sq = pr.count("x_loaded"), pr.count("y_stored"), pr.count("deg_rooted")
        with nc.Block() as block:
            @block.sync
            def _(sp):
                sp.dma_start(x[:, :, :], A["x"].rearrange("(t p) d -> p t d", p=P)).then_inc(ld.sem, 16)
                sp.wait_ge(ld.sem, 16)

            @block.vector
            def _(v):
                v.tensor_scalar(C.deg_scale[:, :], C.cnt_d[:, :], 1.0, None, ALU.max).then_inc(sq.sem, 1)
                v.wait_ge(sq.sem, 2)
                v.reciprocal(C.deg_scale[:, :], C.deg_scale[:, :]).then_inc(sq.sem, 1)
                v.wait_ge(sq.sem, 3)
                v.tensor_tensor(C.deg_scale[:, :], C.deg_scale[:, :], C.has_d[:, :], ALU.mult)

            @block.scalar
            def _(act):
                act.wait_ge(sq.sem, 1)
                act.activation(C.deg_scale[:, :], C.deg_scale[:, :], ACT.Sqrt).then_inc(sq.sem, 1)

        def add_to(dst, a, b):
            return lambda v: v.tensor_tensor(dst[:, :, :], a[:, :, :], b[:, :, :], ALU.add)

        layernorm_relu(pr, C, x, h)
        T0, S0 = pr.dram("T0", (NN, D + 8)), pr.dram("S0", (NN, 8))
        project(pr, C, h, [(A["L0_gnn_W"], 0)], [], [(T0, 0, 0, D + 8), (S0, 0, D + 8, 8)],
                heads=[(C.heads8, D + 8, 8, C.ix_src[0])], scores=(A["L0_gnn_dst_attn"], A["L0_gnn_src_attn"]))
        head_rows(pr, C, "s0", S0, None, 8, C.heads8, None, C.first_s)
        part0, carry0 = pr.dram("part0", (NE, D + 16)), pr.dram("carry0", (ET, 2 * (D + 8)))
        softmax_edges(pr, C, "a", 8, T0, C.src_sorted_col, C.dst_of_sorted, C.heads8,
                      C.fk_src.rearrange("t h c -> (t h) c"), part0)
        carry(pr, C, "softmax", part0, carry0, C.keep_s, 8)
        node_results(pr, C, "softmax", part0, carry0, C.ix_src, C.has_s, C.spans_s, h, 8)
        elementwise(pr, [add_to(x, x, h)])

        layernorm_relu(pr, C, x, h)
        T1, B1 = pr.dram("T1", (NN, 3 * D)), pr.dram("B1", (NN, 2 * D))
        We1 = A["L1_gnn_We1"]
        project(pr, C, h, [(We1[0:D, :], 0), (We1[D:2 * D, :], 2 * D)], [(A["L1_gnn_be1"], 2 * D)],
                [(T1, 0, 0, 2 * D), (T1, 2 * D, None, D), (B1, 0, 2 * D, 2 * D)],
                heads=[(C.heads128, 2 * D, 2 * D, C.ix_dst[0])])
        head_rows(pr, C, "b1", B1, None, 2 * D, C.heads128, None, C.first_d)
        part1, carry1 = pr.dram("part1", (NE, 2 * D)), pr.dram("carry1", (ET, 2 * D))
        mlp_edges(pr, C, T1, C.heads128, part1, A["L1_gnn_be2"], A["L1_gnn_We2"])
        carry(pr, C, "sum_max", part1, carry1, C.keep_d)
        with ExitStack() as l1:
            msgs = pr.sb("msgs", [P, NT, 2 * D], F32, l1)
            node_results(pr, C, "sum_max", part1, carry1, C.ix_dst, C.has_d, C.spans_d, msgs)
            node_mlp(pr, C, msgs, h, A["L1_gnn_Wn1"], A["L1_gnn_bn1"], A["L1_gnn_Wn2"], A["L1_gnn_bn2"], skip)
        elementwise(pr, [add_to(x, x, skip), add_to(x, x, h)])

        layernorm_relu(pr, C, x, h)
        part2, carry2 = pr.dram("part2", (NE, D + 2)), pr.dram("carry2", (ET, 2 * (D + 1)))
        for layer in ("1", "2"):
            w = {n: A["L2_gnn_" + n + layer] for n in ("Wq", "bq", "Wk", "bk", "Wv", "bv", "We", "Ws", "bs")}
            KV, Q = pr.dram("KV" + layer, (NN, 2 * D)), pr.dram("Q" + layer, (NN, D))
            project(pr, C, h, [(w["W" + n], D * j) for j, n in enumerate("qkvs")], [(w["b" + n], D * j) for j, n in enumerate("qkvs")],
                    [(KV, 0, D, 2 * D), (Q, 0, 0, D)], heads=[(C.heads64, 0, D, C.ix_dst[0])], keep=(skip, 3 * D))
            head_rows(pr, C, "q", Q, None, D, C.heads64, None, C.first_d)
            softmax_edges(pr, C, "t" + layer, 1, KV, C.dst_col, C.src_col_i, C.heads64, C.fk_dst, part2, w["We"])
            carry(pr, C, "softmax", part2, carry2, C.keep_d, 1)
            node_results(pr, C, "softmax", part2, carry2, C.ix_dst, C.has_d, C.spans_d, h, 1, 1e-16)
            if layer == "1":
                elementwise(pr, [add_to(h, h, skip), lambda v: v.tensor_scalar(h[:, :, :], h[:, :, :], 0.0, None, ALU.max)])
            else:
                elementwise(pr, [add_to(x, x, h), add_to(x, x, skip)])

        layernorm_relu(pr, C, x, h)
        HN = pr.dram("HN", (NN, D))
        project(pr, C, h, [(A["L3_gnn_W"], 0)], [(A["L3_gnn_b"], 0)], [(HN, 0, 0, D)], row_scale=C.deg_scale)
        part3, carry3 = pr.dram("part3", (NE, D)), pr.dram("carry3", (ET, D))
        gcn_edges(pr, C, HN, part3)
        carry(pr, C, "sum", part3, carry3, C.keep_d)
        node_results(pr, C, "sum", part3, carry3, C.ix_dst, C.has_d, C.spans_d, h)
        wide = C.deg_scale[:, :].unsqueeze(2).to_broadcast([P, NT, D])
        elementwise(pr, [lambda v: v.tensor_tensor(h[:, :, :], h[:, :, :], wide, ALU.mult), add_to(x, x, h)])
        with nc.Block() as block:
            @block.sync
            def _(sp):
                full = N_NODES // P
                sp.dma_start(out[0:full * P, :].rearrange("(t p) d -> p t d", p=P), x[:, 0:full, :]).then_inc(st.sem, 16)
                sp.dma_start(out[full * P:N_NODES, :], x[0:N_NODES - full * P, full, :]).then_inc(st.sem, 16)
                sp.wait_ge(st.sem, 32)


def kernel(**inputs):
    import concourse.bacc as _bacc
    from concourse import mybir as _mybir
    from concourse.bass_utils import run_bass_kernel_spmd as _run

    nc = _bacc.Bacc("TRN2", target_bir_lowering=False, num_devices=1)
    laid = {k: np.asarray(v) for k, v in inputs.items()}
    for k in ("src", "dst"):
        laid[k] = np.pad(laid[k], (0, NE - N_EDGES), constant_values=NN - 1)
    laid["x"] = np.pad(laid["x"], ((0, NN - N_NODES), (0, 0)))
    laid["edge_attr_32"] = np.pad(laid["edge_attr_32"], ((0, NE - N_EDGES), (0, 0)))
    laid["L0_gnn_W"] = laid["L0_gnn_W"].T
    laid["L3_gnn_W"] = laid["L3_gnn_W"].T
    arrays, A = {}, {}
    for k, v in laid.items():
        arrays["in_" + k] = np.ascontiguousarray(v)
        A[k] = nc.dram_tensor("in_" + k, v.shape, _mybir.dt.from_np(v.dtype), kind="ExternalInput").ap()
    out = nc.dram_tensor("out0", (N_NODES, D), _mybir.dt.float32, kind="ExternalOutput").ap()
    gnn(nc, A, out)
    r = _run(nc, [arrays], core_ids=[0])
    return r.results[0]["out0"]
```

```python
import numpy as np
import concourse.bass as bass
from concourse import mybir
from concourse.alu_op_type import AluOpType as ALU
from contextlib import ExitStack

F32 = mybir.dt.float32
BF16 = mybir.dt.bfloat16
I32 = mybir.dt.int32
ACT = mybir.ActivationFunctionType
AX = mybir.AxisListType.X

P = 128
N_NODES = 12500
N_EDGES = 200000
NT = 98
NN = NT * P
ET = 1568
NE = ET * P
G = 8
NGRP = ET // G
S = 4
RB, NB = 98, 16
NG = 7
NNG = NT // NG
BIG = 3.0e38
EPS = 1e-5
D = 64


class Count:

    def __init__(self, sem):
        self.sem, self.base = sem, 0

    def at(self, n):
        return n + self.base

    def passed(self, n):
        self.base += n


class Chain:

    def __init__(self, eng, count, per=0, i=0):
        self.eng, self.count, self.per, self.i, self.n = eng, count, per, i, 0

    def link(self, ins):
        self.n += 1
        ins.then_inc(self.count.sem, 1)
        self.eng.wait_ge(self.count.sem, self.count.at(self.n) if self.per == 0 else self.i * self.per + self.count.at(self.n))

    def close(self):
        assert self.per == 0 or self.n == self.per, self.n


class Program:
    def __init__(self, nc, ctx):
        self.nc, self.ctx, self.counts, self.uses = nc, ctx, {}, {}

    def fresh(self, name):
        self.uses[name] = self.uses.get(name, 0) + 1
        return name if self.uses[name] == 1 else f"{name}_{self.uses[name]}"

    def count(self, name):
        if name not in self.counts:
            self.counts[name] = Count(self.ctx.enter_context(self.nc.semaphore(name)))
        return self.counts[name]

    def sb(self, name, shape, dt=F32, ctx=None):
        return (ctx or self.ctx).enter_context(self.nc.sbuf_tensor(self.fresh(name), shape, dt))

    def ps(self, name, shape, ctx, dt=F32):
        return ctx.enter_context(self.nc.psum_tensor(self.fresh(name), shape, dt))

    def dram(self, name, shape, dt=F32):
        return self.nc.dram_tensor(name, shape, dt, kind="Internal").ap()


def constants(pr, C):
    nc = pr.nc
    s = pr.count("const_made")
    C.ident = pr.sb("ident", [P, P])
    C.before = pr.sb("before", [P, P])
    C.iota8 = pr.sb("iota8", [P, P, G], BF16)
    C.ones = pr.sb("ones", [P, P])
    with nc.Block() as block:
        @block.gpsimd
        def _(gp):
            gp.memset(C.ident[:, :], 0.0).then_inc(s.sem, 1)
            gp.memset(C.ones[:, :], 1.0).then_inc(s.sem, 1)
            gp.memset(C.before[:, :], 1.0).then_inc(s.sem, 1)
            gp.iota(C.iota8[:, :, :], [[1, P], [0, G]], base=0, channel_multiplier=0,
                    allow_small_or_imprecise_dtypes=True).then_inc(s.sem, 1)
            gp.wait_ge(s.sem, 4)
            gp.affine_select(out=C.ident[:, :], in_=C.ident[:, :], compare_op=ALU.not_equal, fill=1.0, base=0,
                             pattern=[[-1, P]], channel_multiplier=1).then_inc(s.sem, 1)
            gp.affine_select(out=C.before[:, :], in_=C.before[:, :], compare_op=ALU.is_gt, fill=0.0, base=0,
                             pattern=[[1, P]], channel_multiplier=-1).then_inc(s.sem, 1)
            gp.wait_ge(s.sem, 6)


def zero_heads(pr, zeros, buffers):
    nc = pr.nc
    made, done = pr.count("zeros_made"), pr.count("zeros_written")
    with nc.Block() as block:
        @block.vector
        def _(v):
            v.memset(zeros[:, :], 0.0).then_inc(made.sem, 1)

        @block.scalar
        def _(act):
            act.wait_ge(made.sem, made.at(1))
            for buf in buffers:
                w = buf.shape[1]
                q = -(-w * (NE // P) // zeros.shape[1])
                while (NE // P) % q:
                    q += 1
                flat = buf.rearrange("(q p r) w -> q p (r w)", p=P, q=q)
                for j in range(q):
                    act.dma_start(flat[j], zeros[:, 0:flat.shape[2]]).then_inc(done.sem, 16)
                    done.passed(16)
    made.passed(1)


def zeros_written(pr):
    done = pr.count("zeros_written")
    with pr.nc.Block() as block:
        @block.sync
        def _(sp):
            sp.wait_ge(done.sem, done.at(0))


def block_at(b):
    return (b // 4) * 512 + (b % 4) * RB


def blocks(ps):
    return ps[:, :].rearrange("p (k c) -> p k c", k=4)[:, :, 0:4 * RB]


def by_bank(ap):
    return ap.rearrange("p (k c) -> p k c", k=4)


def read_ids(pr, C):
    nc = pr.nc
    with ExitStack() as ctx:
        raw = [pr.sb(f"ids_raw{j}", [RB, NB, P], I32, ctx) for j in range(2)]
        rowf = [pr.sb(f"ids_rowf{j}", [RB, NB, P], F32, ctx) for j in range(2)]
        fk = pr.sb("ids_fk", [RB, NB, P + 1], F32, ctx)
        colf = pr.sb("ids_colf", [P, ET], F32, ctx)
        coli = pr.sb("ids_coli", [P, ET], I32, ctx)
        digit = pr.sb("ids_digit", [P, ET], I32, ctx)
        ps = [pr.ps(f"ids_ps{j}", [P, 2048], ctx) for j in range(2)]
        ld, cv, tr, dv, st = (pr.count(n) for n in ("ids_loaded", "ids_converted", "ids_turned", "ids_dve", "ids_stored"))
        ready = {}
        with nc.Block() as block:
            @block.sync
            def _(sp):
                for j, a in enumerate((C.dst, C.src)):
                    sp.dma_start(raw[j][:, :, :], a.rearrange("(b r c) -> r b c", r=RB, c=P)).then_inc(ld.sem, 16)

            @block.vector
            def _(v):
                ch = Chain(v, dv)
                v.wait_ge(ld.sem, 32)
                for j in range(2):
                    v.tensor_copy(rowf[j][:, :, :], raw[j][:, :, :]).then_inc(cv.sem, 1)
                v.wait_ge(cv.sem, 2)
                ch.link(v.memset(fk[:, :, :], -BIG))
                ch.link(v.tensor_tensor(fk[:, :, 1:P], rowf[0][:, :, 1:P], rowf[0][:, :, 0:P - 1], ALU.not_equal))
                ch.link(v.tensor_scalar(fk[:, :, 1:P], fk[:, :, 1:P], -BIG, None, ALU.mult))
                ready["fk"] = ch.n
                for j, (lo, hi) in enumerate(((C.lo_d, C.hi_d), (C.lo_s, C.hi_s))):
                    v.wait_ge(tr.sem, j + 1)
                    dest = C.seg_sb if j == 0 else colf
                    ch.link(v.tensor_copy(by_bank(dest[:, :]), blocks(ps[j])))
                    ch.link(v.tensor_copy(coli[:, :], dest[:, :]))
                    ch.link(v.tensor_scalar(digit[:, :], coli[:, :], P - 1, None, ALU.bitwise_and))
                    ch.link(v.tensor_copy(lo[:, :], digit[:, :]))
                    ch.link(v.tensor_scalar(digit[:, :], coli[:, :], 7, None, ALU.arith_shift_right))
                    ch.link(v.tensor_copy(hi[:, :], digit[:, :]))
                ready["all"] = ch.n

            @block.tensor
            def _(pe):
                pe.wait_ge(cv.sem, 2)
                for j in range(2):
                    for b in range(NB):
                        ins = pe.transpose(ps[j][:, block_at(b):block_at(b) + RB], rowf[j][:, b, :], C.ident[0:RB, 0:RB])
                    ins.then_inc(tr.sem, 1)

            @block.scalar
            def _(act):
                act.wait_ge(dv.sem, ready["fk"])
                act.dma_start(C.fk_dst.rearrange("(b r) c -> r b c", r=RB), fk[:, :, :]).then_inc(st.sem, 16)
                act.wait_ge(dv.sem, ready["all"])
                act.dma_start(C.src_col_i, coli[:, :]).then_inc(st.sem, 16)
                act.dma_start(C.dst_col, C.seg_sb[:, :]).then_inc(st.sem, 16)
                act.dma_start(C.src_col, colf[:, :]).then_inc(st.sem, 16)
                act.wait_ge(st.sem, 64)


def one_hot(v, iota8, out, digit, g):
    n = out.shape[1]
    return v.tensor_tensor(out[:, :, :], iota8[:, 0:n, :], digit[:, bass.ds(G * g, G)].unsqueeze(1).to_broadcast([P, n, G]),
                           ALU.is_equal)


def count_nodes(pr, C):
    nc = pr.nc
    with ExitStack() as ctx:
        low = [[pr.sb(f"hist_low{j}{k}", [P, P, G], BF16, ctx) for k in range(2)] for j in range(2)]
        high = [[pr.sb(f"hist_high{j}{k}", [P, NT, G], BF16, ctx) for k in range(2)] for j in range(2)]
        zero = pr.sb("hist_zero", [P, P], BF16, ctx)
        tot = pr.sb("hist_tot", [P, NT], F32, ctx)
        run = pr.sb("hist_run", [P, NT], F32, ctx)
        hist = [pr.ps(f"hist_ps{j}", [P, 512], ctx) for j in range(2)]
        pre = pr.ps("hist_pre", [P, 512], ctx)
        zr, onehot, used, summed, copied, dv = (pr.count(n) for n in (
            "hist_zero", "hist_onehot", "hist_used", "hist_summed", "hist_copied", "hist_dve"))
        digits = ((C.lo_d, C.hi_d), (C.lo_s, C.hi_s))
        with nc.Block() as block:
            @block.vector
            def _(v):
                v.memset(zero[:, :], 0.0).then_inc(zr.sem, 1)
                with v.Fori(0, NGRP // 2) as i:
                    for k in range(2):
                        g = 2 * i + k
                        v.wait_ge(used.sem, g + 1)
                        for j, (lo, hi) in enumerate(digits):
                            one_hot(v, C.iota8, low[j][k], lo, g)
                            ins = one_hot(v, C.iota8, high[j][k], hi, g)
                        ins.then_inc(onehot.sem, 1)
                ch = Chain(v, dv)
                v.wait_ge(summed.sem, 1)
                for j, (cnt, start) in enumerate(((C.cnt_d, C.start_d), (C.cnt_s, C.start_s))):
                    ch.link(v.tensor_copy(cnt[:, :], hist[j][:, 0:NT]))
                    v.sem_inc(copied.sem, 1)
                    v.wait_ge(summed.sem, j + 2)
                    ch.link(v.tensor_copy(tot[:, :], pre[:, NT:2 * NT]))
                    ch.link(v.tensor_tensor_scan(run[:, :], C.ones[:, 0:NT], tot[:, :], 0.0, ALU.mult, ALU.add))
                    ch.link(v.tensor_tensor(run[:, :], run[:, :], tot[:, :], ALU.subtract))
                    ch.link(v.tensor_tensor(start[:, :], pre[:, 0:NT], run[:, :], ALU.add))

            @block.tensor
            def _(pe):
                pe.wait_ge(zr.sem, 1)
                pe.sem_inc(used.sem, 2)
                for j in range(2):
                    pe.matmul(hist[j][:, 0:NT], zero[:, :], zero[:, 0:NT], start=True, stop=False, skip_group_check=True)
                with pe.Fori(0, NGRP // 2) as i:
                    for k in range(2):
                        pe.wait_ge(onehot.sem, 2 * i + (k + 1))
                        for j in range(2):
                            for t in range(G):
                                ins = pe.matmul(hist[j][:, 0:NT], low[j][k][:, :, t], high[j][k][:, :, t],
                                                start=False, stop=False, skip_group_check=True)
                        ins.then_inc(used.sem, 1)
                for j in range(2):
                    ins = pe.matmul(hist[j][:, 0:NT], zero[:, :], zero[:, 0:NT], start=False, stop=True, skip_group_check=True)
                ins.then_inc(summed.sem, 1)
                for j, cnt in enumerate((C.cnt_d, C.cnt_s)):
                    pe.wait_ge(dv.sem, 1 + 5 * j)
                    pe.matmul(pre[:, 0:NT], C.before[:, :], cnt[:, :], start=True, stop=True)
                    pe.matmul(pre[:, NT:2 * NT], C.ones[:, :], cnt[:, :], start=True, stop=True).then_inc(summed.sem, 1)


def sort_by_src(pr, C):
    nc = pr.nc
    W = D + 8
    B = 4
    with ExitStack() as ctx:
        sb, pscope = (lambda n, s, d=F32: pr.sb("rank_" + n, s, d, ctx)), (lambda n, s, d=F32: pr.ps("rank_" + n, s, ctx, d))
        src = [sb(f"src{k}", [P, G]) for k in range(S)]
        dst = [sb(f"dst{k}", [P, G]) for k in range(S)]
        heads = [sb(f"heads{k}", [P, G, W]) for k in range(S)]
        row = [sb(f"row{k}", [P, G, W + 1]) for k in range(S)]
        place = [sb(f"place{k}", [P, G], I32) for k in range(S)]
        low = [sb(f"low{k}", [P, P, G], BF16) for k in range(2)]
        high = [sb(f"high{k}", [P, NT, G], BF16) for k in range(2)]
        lowT = [sb(f"lowT{k}", [P, G, P]) for k in range(2)]
        identb, ident128, halfb, onesb = (sb(n, [P, P], BF16) for n in ("identb", "ident128", "halfb", "onesb"))
        sofar = [sb(f"sofar{n}", [P, B, NT]) for n in range(2)]
        earlier = [sb(f"earlier{k}", [P, G, P], BF16) for k in range(2)]
        same = sb("same", [P, G, P])
        picked = sb("picked", [P, G, NT])
        base = sb("base", [P, G])
        row_ps = pscope("row_ps", [P, 1024])
        lowT_ps = pscope("lowT_ps", [P, 1024], BF16)
        total = pscope("total", [P, 512])
        pick_ps = pscope("pick_ps", [P, 1024])
        spread_ps = pscope("spread_ps", [P, 1024])
        spreads, _, spread_at = banked(spread_ps, W)
        RANK = 448
        const, onehot, lowed, turned, snap, counted, picks, rowed, masked, rowed_d, same_d, spread, filled, dv, placed = (
            pr.count("rank_" + n) for n in ("const", "onehot", "lowed", "turned", "snap", "counted", "picks", "rowed", "masked",
                                            "rowed_dst", "same_dst", "spread", "filled", "dve", "placed"))
        gate = pr.count("e_gate")
        picked_b, pe_gate = pr.count("rank_batch_picked"), pr.count("pe_gate")
        load, scattered = ([pr.count(f"e_{n}{k}") for k in range(S)] for n in ("loaded", "gathered"))
        with nc.Block() as block:
            @block.sync
            def _(sp):
                def load_group(g, k):
                    sp.dma_start(src[k][:, :], C.src_col[:, bass.ds(G * g, G)]).then_inc(load[k].sem, 16)
                    sp.dma_start(dst[k][:, :], C.dst_col[:, bass.ds(G * g, G)]).then_inc(load[k].sem, 16)
                    sp.dma_start(heads[k][:, :, :], tile_rows(C.heads72)(g)).then_inc(load[k].sem, 16)

                for k in range(S):
                    load_group(k, k)
                for i, k, after in groups(sp):
                    if not isinstance(i, int):
                        sp.wait_ge(scattered[k].sem, i * (16 * G) + 16 * G)
                        load_group(S * i + (k + S), k)

            @block.gpsimd
            def _(gp):
                for i, k, after in groups(gp):
                    g = S * i + k
                    gp.wait_ge(placed.sem, g + 1)
                    gp.wait_ge(filled.sem, g * 2 + 2)
                    gp.sem_inc(gate.sem, 1)
                    for t in range(G):
                        gp.indirect_dma_start(C.sorted_rows, bass.IndirectOffsetOnAxis(ap=place[k][:, t:t + 1], axis=0),
                                              row[k][:, t, :], None).then_inc(scattered[k].sem, 16)
                for k in range(S):
                    gp.wait_ge(scattered[k].sem, (NGRP // S) * 16 * G)

            @block.vector
            def _(v):
                def digits(i, k):
                    g = S * i + k
                    one_hot(v, C.iota8, low[k % 2], C.lo_s, g)
                    one_hot(v, C.iota8, high[k % 2], C.hi_s, g).then_inc(onehot.sem, 1)

                def mask(i, k):
                    g = S * i + k
                    v.wait_ge(load[k].sem, i * 48 + 48)
                    v.wait_ge(rowed.sem, g + 1)
                    v.tensor_tensor(earlier[k % 2][:, :, :], row_ps[:, :].rearrange("p (t e) -> p t e", t=G),
                                    src[k][:, :].unsqueeze(2).to_broadcast([P, G, P]), ALU.is_equal).then_inc(masked.sem, 1)

                v.tensor_copy(identb[:, :], C.ident[:, :])
                v.tensor_scalar(ident128[:, :], C.ident[:, :], float(P), None, ALU.mult)
                v.memset(onesb[:, :], 1.0)
                v.tensor_scalar(halfb[:, :], C.before[:, :], -0.5, 0.5, ALU.mult, ALU.add).then_inc(const.sem, 1)
                digits(0, 0)
                for i, k, after in groups(v):
                    g = S * i + k
                    ch = Chain(v, dv, 2, g)
                    mask(i, k)
                    if after:
                        digits(*after)
                    v.wait_ge(rowed_d.sem, g + 1)
                    v.tensor_tensor(same[:, :, :], row_ps[:, :].rearrange("p (t e) -> p t e", t=G),
                                    dst[k][:, :].unsqueeze(2).to_broadcast([P, G, P]), ALU.is_equal).then_inc(same_d.sem, 1)
                    v.wait_ge(picks.sem, g + 1)
                    ins = None
                    for b in range(G // B):
                        ins = v.tensor_tensor(picked[:, b * B:(b + 1) * B, :],
                                              pick_ps[:, b * 512:b * 512 + B * NT].rearrange("p (t c) -> p t c", t=B),
                                              high[k % 2][:, :, b * B:(b + 1) * B].rearrange("p c t -> p t c"), ALU.mult)
                    ch.link(ins)
                    ch.link(v.tensor_reduce(base[:, :], picked[:, :, :], AX, ALU.add))
                    v.tensor_tensor(place[k][:, :], base[:, :], pick_ps[:, RANK:RANK + G], ALU.add).then_inc(placed.sem, 1)
                    v.wait_ge(placed.sem, g + 1)
                    ch.close()

            @block.tensor
            def _(pe):
                def lay_ids(i, k, lo, hi, mask):
                    g = S * i + k
                    for t in range(G):
                        at = slice(t * P, (t + 1) * P)
                        col = bass.ds(G * g + t, 1)
                        pe.matmul(row_ps[:, at], lo[:, col].to_broadcast([P, P]), identb[:, :], start=True, stop=False)
                        ins = pe.matmul(row_ps[:, at], hi[:, col].to_broadcast([P, P]), ident128[:, :], start=False, stop=not mask)
                        if mask:
                            ins = pe.matmul(row_ps[:, at], identb[:, :], halfb[:, :], start=False, stop=True)
                    return ins

                def turn_low(i, k):
                    g = S * i + k
                    pe.wait_ge(onehot.sem, g + 1)
                    for t in range(G):
                        ins = pe.transpose(lowT_ps[:, t * P:(t + 1) * P], low[k % 2][:, :, t], identb[:, :])
                    ins.then_inc(lowed.sem, 1)

                def count_tile(k, t, regions):
                    n = regions.stop - regions.start
                    return pe.matmul(total[:, regions.start * NT:regions.stop * NT], low[k % 2][:, :, t],
                                     high[k % 2][:, :, t].unsqueeze(1).to_broadcast([P, n, NT]), start=False, stop=True,
                                     skip_group_check=True)

                def count_before(k, b):
                    for r in range(B - 1):
                        ins = count_tile(k, b * B + r, slice(r + 1, B))
                    ins.then_inc(counted.sem, 1)

                pe.wait_ge(const.sem, 1)
                pe.matmul(total[:, 0:B * NT], C.ident[:, :], C.start_s[:, :].unsqueeze(1).to_broadcast([P, B, NT]),
                          start=True, stop=True, skip_group_check=True)
                turn_low(0, 0)
                count_before(0, 0)
                lay_ids(0, 0, C.lo_s, C.hi_s, True).then_inc(rowed.sem, 1)
                for i, k, after in groups(pe):
                    g = S * i + k

                    def batch(b):
                        pe.wait_ge(snap.sem, g * 2 + (b + 1))
                        for r in range(B):
                            count_tile(k, b * B + r, slice(0, r + 1))
                        if b == 0:
                            count_before(k, 1)
                        elif after:
                            pe.wait_ge(onehot.sem, g + 2)
                            count_before(after[1], 0)
                        if b == 0:
                            pe.wait_ge(turned.sem, g + 1)
                        for r in range(B):
                            at = b * 512 + r * NT
                            ins = pe.matmul(pick_ps[:, at:at + NT], lowT[k % 2][:, b * B + r, :], sofar[b][:, r, :], start=True, stop=True)
                        ins.then_inc(picked_b.sem, 1)

                    batch(0)
                    pe.wait_ge(masked.sem, g + 1)
                    lay_ids(i, k, C.lo_d, C.hi_d, False).then_inc(rowed_d.sem, 1)
                    batch(1)
                    for t in range(G):
                        ins = pe.matmul(pick_ps[:, RANK + t:RANK + t + 1], earlier[k % 2][:, t, :], onesb[:, 0:1], start=True, stop=True)
                    ins.then_inc(picks.sem, 1)
                    if after:
                        turn_low(*after)
                    pe.wait_ge(same_d.sem, g + 1)
                    for t in range(G):
                        ins = pe.matmul(spread_ps[:, spread_at(t):spread_at(t) + W], same[:, t, :], heads[k][:, t, :], start=True, stop=True)
                    ins.then_inc(spread.sem, 1)
                    if after:
                        lay_ids(*after, C.lo_s, C.hi_s, True).then_inc(rowed.sem, 1)
                        pe.wait_ge(placed.sem, g + 1)
                        pe.sem_inc(pe_gate.sem, 1)

            @block.scalar
            def _(act):
                def move_low(i, k):
                    g = S * i + k
                    act.wait_ge(lowed.sem, g + 1)
                    act.activation(lowT[k % 2][:, :, :].rearrange("p t e -> p (t e)"), lowT_ps[:, :], ACT.Copy).then_inc(turned.sem, 1)

                def copy_counts(n, b):
                    act.wait_ge(counted.sem, n)
                    act.activation(sofar[b][:, :, :].rearrange("p t c -> p (t c)"), total[:, 0:B * NT], ACT.Copy).then_inc(snap.sem, 1)

                copy_counts(1, 0)
                move_low(0, 0)
                for i, k, after in groups(act):
                    g = S * i + k
                    copy_counts(g * 2 + 2, 1)
                    if after:
                        act.wait_ge(picked_b.sem, g * 2 + 1)
                        copy_counts(g * 2 + 3, 0)
                        move_low(*after)
                    act.wait_ge(load[k].sem, i * 48 + 48)
                    act.activation(row[k][:, :, W:W + 1], src[k][:, :].unsqueeze(2), ACT.Copy).then_inc(filled.sem, 1)
                    act.wait_ge(spread.sem, g + 1)
                    act.activation(row[k][:, :, 0:W].rearrange("p (a b) w -> p a b w", a=2),
                                   spreads.rearrange("p a (b w) -> p a b w", w=W), ACT.Copy).then_inc(filled.sem, 1)
        for k in range(S):
            load[k].passed(48 * (NGRP // S))
            scattered[k].passed(16 * G * (NGRP // S))


def sorted_segments(pr, C):
    nc = pr.nc
    with ExitStack() as ctx:
        ends = pr.sb("srt_ends", [RB, 2, NB], F32, ctx)
        ld, st = pr.count("srt_loaded"), pr.count("srt_stored")
        with nc.Block() as block:
            @block.sync
            def _(sp):
                view = C.sorted_rows.rearrange("(b r e) w -> r b e w", r=RB, e=P)
                with nc.allow_non_contiguous_dma(reason="one word of each tile"):
                    for j, e in enumerate((0, P - 1)):
                        sp.dma_start(ends[:, j, :], view[:, :, e, D + 8]).then_inc(ld.sem, 16)
                    sp.wait_ge(ld.sem, 32)
                    for j in range(2):
                        sp.dma_start(C.src_ends[j].rearrange("(b r) -> r b", r=RB), ends[:, j, :]).then_inc(st.sem, 16)
                sp.wait_ge(st.sem, 32)


def node_bounds(pr, C):
    nc = pr.nc
    with ExitStack() as ctx:
        f = [pr.sb(f"nb_f{j}", [P, NT], F32, ctx) for j in range(4)]
        n = [pr.sb(f"nb_i{j}", [P, NT], I32, ctx) for j in range(4)]
        out_i = [pr.sb(f"nb_out{j}", [P, NT], I32, ctx) for j in range(6)]
        dv, st = pr.count("bounds_dve"), pr.count("bounds_stored")
        with nc.Block() as block:
            @block.vector
            def _(v):
                ch = Chain(v, dv)
                for j, (cnt, start, has, spans) in enumerate(((C.cnt_d, C.start_d, C.has_d, C.spans_d),
                                                              (C.cnt_s, C.start_s, C.has_s, C.spans_s))):
                    ch.link(v.tensor_scalar(has[:, :], cnt[:, :], 0.5, None, ALU.is_gt))
                    ch.link(v.tensor_tensor(f[0][:, :], start[:, :], cnt[:, :], ALU.add))
                    ch.link(v.tensor_scalar(f[0][:, :], f[0][:, :], -1.0, 0.0, ALU.add, ALU.max))
                    ch.link(v.tensor_copy(out_i[3 * j + 1][:, :], f[0][:, :]))
                    ch.link(v.tensor_scalar(n[0][:, :], out_i[3 * j + 1][:, :], 7, None, ALU.arith_shift_right))
                    ch.link(v.tensor_copy(f[1][:, :], n[0][:, :]))
                    ch.link(v.tensor_copy(n[1][:, :], start[:, :]))
                    ch.link(v.tensor_scalar(n[2][:, :], n[1][:, :], 7, None, ALU.arith_shift_right))
                    ch.link(v.tensor_copy(f[2][:, :], n[2][:, :]))
                    ch.link(v.tensor_tensor(spans[:, :], f[1][:, :], f[2][:, :], ALU.is_gt))
                    ch.link(v.tensor_tensor(spans[:, :], spans[:, :], has[:, :], ALU.mult))
                    ch.link(v.tensor_scalar(f[1][:, :], f[1][:, :], -1.0, 0.0, ALU.add, ALU.max))
                    ch.link(v.tensor_copy(out_i[3 * j + 2][:, :], f[1][:, :]))
                    ch.link(v.tensor_scalar(f[3][:, :], has[:, :], -float(NE), float(NE), ALU.mult, ALU.add))
                    ch.link(v.tensor_tensor(f[3][:, :], f[3][:, :], start[:, :], ALU.add))
                    ch.link(v.tensor_copy(out_i[3 * j][:, :], f[3][:, :]))

            @block.sync
            def _(sp):
                sp.wait_ge(dv.sem, 32)
                for j, rows in enumerate((C.ix_dst, C.ix_src)):
                    for q in range(3):
                        sp.dma_start(rows[q], out_i[3 * j + q][:, :]).then_inc(st.sem, 16)
                sp.wait_ge(st.sem, 96)


def tile_starts(pr, C, order):
    nc = pr.nc
    head, tail, keep, idx = ((C.dst_col[0], C.dst_col[P - 1:P, :], C.keep_d, C.first_d),
                             (C.src_ends[0], C.src_ends[1:2, :], C.keep_s, C.first_s))[order]
    with ExitStack() as ctx:
        last = pr.sb("ts_last", [P, ET], F32, ctx)
        first = pr.sb("ts_first", [RB, NB], F32, ctx)
        ld = pr.count("starts_loaded")
        with nc.Block() as block:
            @block.sync
            def _(sp):
                sp.dma_start(last[:, :], tail.to_broadcast([P, ET])).then_inc(ld.sem, 16)
                with nc.allow_non_contiguous_dma(reason="one word of each tile"):
                    sp.dma_start(first[:, :], head.rearrange("(b r) -> r b", r=RB)).then_inc(ld.sem, 16)

            @block.vector
            def _(v):
                v.wait_ge(ld.sem, ld.at(32))
                v.memset(keep[:, 0:1], 0.0)
                v.tensor_tensor(keep[:, 1:ET], last[:, 1:ET], last[:, 0:ET - 1], ALU.is_equal)
                v.tensor_copy(idx[:, :], first[:, :])
        ld.passed(32)


def head_rows(pr, C, table, width, heads, first):
    nc = pr.nc
    with ExitStack() as ctx:
        rows = pr.sb("hr_rows", [RB, NB * width], F32, ctx)
        got, put = pr.count("hr_gathered"), pr.count("hr_written")
        with nc.Block() as block:
            @block.gpsimd
            def _(gp):
                for b in range(NB):
                    gp.indirect_dma_start(rows[:, b * width:(b + 1) * width], None, table,
                                          bass.IndirectOffsetOnAxis(ap=first[:, b:b + 1], axis=0)).then_inc(got.sem, 16)

            @block.sync
            def _(sp):
                sp.wait_ge(got.sem, got.at(16 * NB))
                sp.dma_start(heads.rearrange("(b r e) w -> r b e w", r=RB, e=P)[:, :, 0, :],
                             rows[:, :].rearrange("r (b w) -> r b w", w=width)).then_inc(put.sem, 16)
                sp.wait_ge(put.sem, put.at(16))
        got.passed(16 * NB)
        put.passed(16)


def layernorm_relu(pr, C, x, h):
    nc = pr.nc
    with ExitStack() as ctx:
        big = pr.sb("ln_big", [P, NT, D], F32, ctx)
        mean = pr.sb("ln_mean", [P, NT], F32, ctx)
        var = pr.sb("ln_var", [P, NT], F32, ctx)
        std = pr.sb("ln_std", [P, NT], F32, ctx)
        dv, sq = pr.count("ln_dve"), pr.count("ln_rooted")
        with nc.Block() as block:
            @block.vector
            def _(v):
                ch = Chain(v, dv)
                wide = lambda a: a[:, :].unsqueeze(2).to_broadcast([P, NT, D])
                ch.link(v.tensor_reduce(mean[:, :], x[:, :, :], AX, ALU.add))
                ch.link(v.tensor_scalar(mean[:, :], mean[:, :], 1.0 / D, None, ALU.mult))
                ch.link(v.tensor_tensor(h[:, :, :], x[:, :, :], wide(mean), ALU.subtract))
                ch.link(v.tensor_tensor(big[:, :, :], h[:, :, :], h[:, :, :], ALU.mult))
                ch.link(v.tensor_reduce(var[:, :], big[:, :, :], AX, ALU.add))
                ch.link(v.tensor_scalar(var[:, :], var[:, :], 1.0 / D, EPS, ALU.mult, ALU.add))
                v.wait_ge(sq.sem, sq.at(1))
                ch.link(v.reciprocal(std[:, :], std[:, :]))
                ch.link(v.tensor_tensor(h[:, :, :], h[:, :, :], wide(std), ALU.mult))
                ch.link(v.tensor_scalar(h[:, :, :], h[:, :, :], 0.0, None, ALU.max))

            @block.scalar
            def _(act):
                act.wait_ge(dv.sem, dv.at(6))
                act.activation(std[:, :], var[:, :], ACT.Sqrt).then_inc(sq.sem, 1)
        dv.passed(9)
        sq.passed(1)


def project(pr, C, h, weights, bias, tables, heads=(), keep=None, row_scale=None, scores=None):
    nc = pr.nc
    width = max(c + w.shape[1] for w, c in weights)
    total = width + (16 if scores else 0)
    room = max([total] + [c + w for _, c, w, _ in heads])
    pitch = 512 // (4 if width <= P else 2)
    K, LAG = 7, 3
    with ExitStack() as ctx:
        w_sb = pr.sb("pj_w", [D + 1, width], F32, ctx)
        att = pr.sb("pj_att", [P, 2, D], F32, ctx)
        stage = [pr.sb(f"pj_stage{k}", [P, NG, D], F32, ctx) for k in range(K)]
        hT = pr.sb("pj_hT", [D + 1, NG * P], F32, ctx)
        res = [pr.sb(f"pj_res{k}", [P, NG, room], F32, ctx) for k in range(K)]
        tmp = pr.sb("pj_tmp", [P, NG, 2, D], F32, ctx)
        idx_all = pr.sb("pj_idx_all", [P, max(len(heads), 1), NT], I32, ctx)
        idx = [pr.sb(f"pj_idx{k}", [P, max(len(heads), 1), NG], I32, ctx) for k in range(K)]
        trp = pr.ps("pj_trp", [P, 1024], ctx)
        acc = pr.ps("pj_acc", [P, 4 * 512], ctx)
        ld, ini, staged, turned, moved, made, products, scored, gate, pe_gate, free = (
            pr.count("pj_" + n) for n in ("loaded", "rows_set", "staged", "turned", "moved", "made", "products", "scored",
                                          "gate", "pe_gate", "free"))
        stored, scat = ([pr.count(f"pj_{n}{k}") for k in range(K)] for n in ("stored", "scattered"))
        nload = 16 * (len(weights) + len(bias) + len(heads) + (2 if scores else 0))
        nstore, nscat = 16 * len(tables), 16 * NG * len(heads)
        with nc.Block() as block:
            @block.sync
            def _(sp):
                for w, c in weights:
                    sp.dma_start(w_sb[0:D, c:c + w.shape[1]], w).then_inc(ld.sem, 16)
                sp.wait_ge(ini.sem, ini.at(2))
                for b, c in bias:
                    sp.dma_start(w_sb[D:D + 1, c:c + b.shape[0]], b.unsqueeze(0)).then_inc(ld.sem, 16)
                if scores:
                    for j, a in enumerate(scores):
                        sp.dma_start(att[:, j, :], a.rearrange("a h d -> a (h d)").to_broadcast([P, D])).then_inc(ld.sem, 16)

                for j, hd in enumerate(heads):
                    sp.dma_start(idx_all[:, j, :], hd[3]).then_inc(ld.sem, 16)

                def store(i, k):
                    g = K * i + k
                    sp.wait_ge(scored.sem, g + scored.at(1))
                    for tab, at, c, wd in tables:
                        src = stage[k][:, :, :] if c is None else res[k][:, :, c:c + wd]
                        sp.dma_start(tab.rearrange("(t p) w -> p t w", p=P)[:, bass.ds(NG * g, NG), at:at + wd], src)\
                            .then_inc(stored[k].sem, 16)

                def release(i, k):
                    sp.wait_ge(stored[k].sem, i * nstore + stored[k].at(nstore))
                    if heads:
                        sp.wait_ge(scat[k].sem, i * nscat + scat[k].at(nscat))
                    sp.sem_inc(free.sem, 1)

                with sp.Fori(0, NNG // K) as i:
                    for k in range(K):
                        store(i, k)
                        if k >= LAG:
                            release(i, k - LAG)
                    for k in range(K - LAG, K):
                        release(i, k)

            @block.gpsimd
            def _(gp):
                if heads:
                    with gp.Fori(0, NNG // K) as i:
                        for k in range(K):
                            gp.wait_ge(scored.sem, K * i + scored.at(k + 1))
                            gp.sem_inc(gate.sem, 1)
                            for j, (buf, c, wd, _) in enumerate(heads):
                                for t in range(NG):
                                    gp.indirect_dma_start(buf, bass.IndirectOffsetOnAxis(ap=idx[k][:, j, t:t + 1], axis=0),
                                                          res[k][:, t, c:c + wd], None,
                                                          bounds_check=NE - 1, oob_is_err=False).then_inc(scat[k].sem, 16)

            @block.vector
            def _(v):
                if room > total:
                    for k in range(K):
                        v.memset(res[k][:, :, total:room], 0.0)
                v.memset(hT[D:D + 1, :], 1.0).then_inc(ini.sem, 1)
                v.memset(w_sb[D:D + 1, :], 0.0).then_inc(ini.sem, 1)
                v.sem_inc(free.sem, K)
                if heads:
                    v.wait_ge(ld.sem, ld.at(nload))

                def set_out(i, k):
                    g = K * i + k
                    tiles = bass.ds(NG * g, NG)
                    v.wait_ge(free.sem, g + free.at(1))
                    if heads:
                        v.tensor_copy(idx[k][:, :, :], idx_all[:, :, tiles])
                    v.tensor_copy(stage[k][:, :, :], h[:, tiles, :]).then_inc(staged.sem, 1)

                with v.Fori(0, NNG // K) as i:
                    set_out(i, 0)
                    for k in range(K):
                        g = K * i + k
                        tiles = bass.ds(NG * g, NG)
                        if k + 1 < K:
                            set_out(i, k + 1)
                        v.wait_ge(made.sem, g + made.at(1))
                        if scores:
                            v.wait_ge(ld.sem, ld.at(nload))
                            for j in range(2):
                                v.tensor_tensor(tmp[:, :, j, :], res[k][:, :, 0:D], att[:, j, :].unsqueeze(1).to_broadcast([P, NG, D]),
                                                ALU.mult).then_inc(products.sem, 1)
                            v.wait_ge(products.sem, g * 2 + products.at(2))
                            for j in range(2):
                                ins = v.tensor_reduce(res[k][:, :, D + 8 * j:D + 8 * j + 8],
                                                      tmp[:, :, j, :].rearrange("p t (h d) -> p t h d", h=8), AX, ALU.add)
                            ins.then_inc(scored.sem, 1)
                            v.wait_ge(scored.sem, g + scored.at(1))
                        elif row_scale is not None:
                            v.tensor_tensor(res[k][:, :, 0:D], res[k][:, :, 0:D], row_scale[:, tiles].unsqueeze(2).to_broadcast([P, NG, D]),
                                            ALU.mult).then_inc(scored.sem, 1)
                        elif keep is not None:
                            v.tensor_copy(keep[0][:, tiles, :], res[k][:, :, keep[1]:keep[1] + D]).then_inc(scored.sem, 1)
                        else:
                            v.sem_inc(scored.sem, 1)

            @block.tensor
            def _(pe):
                pe.wait_ge(ld.sem, ld.at(nload))
                pe.wait_ge(ini.sem, ini.at(2))
                with pe.Fori(0, NNG // K) as i:
                    for k in range(K):
                        g = K * i + k
                        pe.wait_ge(staged.sem, g + staged.at(1))
                        pe.sem_inc(pe_gate.sem, 1)
                        for t in range(NG):
                            ins = pe.transpose(trp[0:D, t * P:(t + 1) * P], stage[k][:, t, :], C.ident[:, :])
                        ins.then_inc(turned.sem, 1)
                        pe.wait_ge(moved.sem, g + moved.at(1))
                        for t in range(NG):
                            ins = pe.matmul(acc[:, t * pitch:t * pitch + width], hT[:, t * P:(t + 1) * P], w_sb[:, :], start=True, stop=True)
                        ins.then_inc(turned.sem, 1)

            @block.scalar
            def _(act):
                act.wait_ge(ini.sem, ini.at(2))
                with act.Fori(0, NNG // K) as i:
                    for k in range(K):
                        g = K * i + k
                        act.wait_ge(turned.sem, g * 2 + turned.at(1))
                        act.activation(hT[0:D, :], trp[0:D, 0:NG * P], ACT.Copy).then_inc(moved.sem, 1)
                        act.wait_ge(turned.sem, g * 2 + turned.at(2))
                        act.activation(res[k][:, :, 0:width], acc[:, 0:NG * pitch].rearrange("p (t c) -> p t c", t=NG)[:, :, 0:width],
                                       ACT.Copy).then_inc(made.sem, 1)
        ld.passed(nload)
        ini.passed(2)
        for c in (staged, moved, made, scored):
            c.passed(NNG)
        turned.passed(2 * NNG)
        free.passed(NNG + K)
        for k in range(K):
            stored[k].passed(nstore * (NNG // K))
            scat[k].passed(nscat * (NNG // K))
        if scores:
            products.passed(2 * NNG)



def groups(eng):
    with eng.Fori(0, NGRP // S - 1) as i:
        for k in range(S):
            yield i, k, (i + (k + 1) // S, (k + 1) % S)
    i = NGRP // S - 1
    for k in range(S):
        yield i, k, (i, k + 1) if k + 1 < S else None


class EdgeIO:

    def __init__(self, pr, tag, ctx, loads, table, width, part, part_width, S=S):
        self.table, self.part, self.S = table, part, S
        self.slot = {n: [pr.sb(f"{tag}_{n}{k}", s, t, ctx) for k in range(S)] for n, s, t, _ in loads}
        self.loads = {n: f for n, _, _, f in loads}
        self.rows = self.slot["rows"] if table is None else [pr.sb(f"{tag}_rows{k}", [P, G, width], F32, ctx) for k in range(S)]
        self.out = [pr.sb(f"{tag}_out{k}", [P, G, part_width], F32, ctx) for k in range(S)]
        self.loaded = [pr.count(f"e_loaded{k}") for k in range(S)]
        self.gathered = [pr.count(f"e_gathered{k}") for k in range(S)]
        self.stored = [pr.count(f"e_stored{k}") for k in range(S)]
        self.done, self.free, self.gate = pr.count("e_done"), pr.count("e_out_free"), pr.count("e_gate")
        self.ready = pr.count("e_ready")
        self.ready_begins = 0 if table is None else 1
        self.per_load = 16 * sum(len(f) for f in self.loads.values())

    def sync(self, sp, used=None):
        view = self.part.rearrange("(t p) w -> p t w", p=P)
        S = self.S

        def load_group(g, k):
            for n, parts in self.loads.items():
                for part, source in parts:
                    sp.dma_start(part(self.slot[n][k]), source(g)).then_inc(self.loaded[k].sem, 16)

        def free_slot(i, k):
            sp.wait_ge(self.stored[k].sem, i * 16 + self.stored[k].at(16))
            sp.sem_inc(self.free.sem, 1)

        def step(i, k, more, first=False):
            g = S * i + k
            if used:
                sp.wait_ge(used.sem, g + used.at(1))
                if more:
                    load_group(g + S, k)
            sp.wait_ge(self.done.sem, g + self.done.at(1))
            if more and not used:
                load_group(g + S, k)
            sp.dma_start(view[:, bass.ds(G * g, G), :], self.out[k][:, :, :]).then_inc(self.stored[k].sem, 16)
            if k:
                free_slot(i, k - 1)
            elif not first:
                free_slot(i - 1, S - 1)

        for k in range(S):
            load_group(k, k)
        sp.sem_inc(self.free.sem, S)
        for k in range(S):
            step(0, k, True, first=True)
        with sp.Fori(1, NGRP // S - 1) as i:
            for k in range(S):
                step(i, k, True)
        for k in range(S):
            step(NGRP // S - 1, k, False)
        free_slot(NGRP // S - 1, S - 1)

    def gather(self, gp):
        index = next(iter(self.slot))
        for i, k, after in groups(gp):
            self.wait_loaded(gp, i, k)
            gp.sem_inc(self.gate.sem, 1)
            for t in range(G):
                gp.indirect_dma_start(self.rows[k][:, t, :], None, self.table,
                                      bass.IndirectOffsetOnAxis(ap=self.slot[index][k][:, t:t + 1], axis=0))\
                    .then_inc(self.gathered[k].sem, 16)

    def wait_loaded(self, eng, i, k):
        eng.wait_ge(self.loaded[k].sem, i * self.per_load + self.loaded[k].at(self.per_load))

    def wait_gathered(self, eng, i, k):
        if self.table is not None:
            eng.wait_ge(self.gathered[k].sem, i * (16 * G) + self.gathered[k].at(16 * G))

    def wait_out_free(self, eng, g):
        eng.wait_ge(self.free.sem, g + self.free.at(1))

    def passed(self):
        S = self.S
        for k in range(S):
            self.loaded[k].passed(self.per_load * (NGRP // S))
            self.gathered[k].passed(16 * G * (NGRP // S) if self.table is not None else 0)
            self.stored[k].passed(16 * (NGRP // S))
        self.done.passed(NGRP)
        self.free.passed(NGRP + S)
        self.ready.passed(self.ready_begins + NGRP if self.ready_begins else 0)


def whole(a):
    return a[:, :]


def whole3(a):
    return a[:, :, :]


def tile_rows(rows):
    view = rows.rearrange("(t p) w -> p t w", p=P)
    return lambda g: view[:, bass.ds(G * g, G), :]


def common_loads(index_col, seg_col):
    return [("index", [P, G], I32, [(whole, lambda g: index_col[:, bass.ds(G * g, G)])]),
            ("seg", [P, G], F32, [(whole, lambda g: seg_col[:, bass.ds(G * g, G)])])]


def banked(ps, w):
    if G * w <= 512:
        return ps[:, 0:G * w].rearrange("p (a c) -> p a c", a=1), 1, lambda t: t * w
    return ps[:, :].rearrange("p (a c) -> p a c", a=2)[:, :, 0:4 * w], 2, lambda t: (t // 4) * 512 + (t % 4) * w


def ahead(S, i, k, n):
    j = (i + (k + n) // S, (k + n) % S)
    return None if isinstance(i, int) and j[0] >= NGRP // S else j


def before(S, i, k):
    if k:
        return i, k - 1
    return None if isinstance(i, int) and i == 0 else (i - 1, S - 1)


def stepped(eng, S):
    for k in range(S):
        yield 0, k
    with eng.Fori(1, NGRP // S - 1) as i:
        for k in range(S):
            yield i, k
    for k in range(S):
        yield NGRP // S - 1, k


def gat_edges(pr, C, heads, part):
    nc = pr.nc
    H = 8
    W = D + H
    NF = G * H
    S = 7

    def flip(k):
        return 2 if k == S - 1 else k % 2

    with ExitStack() as ctx:
        loads = [("rows", [P, G, W + 1], F32, [(whole3, tile_rows(C.sorted_rows))]),
                 ("heads", [P, G, H], F32, [(whole3, tile_rows(heads))])]
        io = EdgeIO(pr, "a", ctx, loads, None, None, part, W + H, S)
        slots = io.slot

        def seg_of(k):
            return slots["rows"][k][:, :, W]

        seg_part = [[pr.sb(f"a_seg_part{k}{q}", [P, G], BF16, ctx) for q in range(2)] for k in range(S)]
        head_part = [pr.sb(f"a_head_part{k}", [P, G, 3, H], BF16, ctx) for k in range(S)]
        head_rest = pr.sb("a_head_rest", [P, G, H], F32, ctx)
        wide_seg = [pr.sb(f"a_wide_seg{k}", [P, G, H], F32, ctx) for k in range(S)]
        turned_seg = [pr.sb(f"a_turned_seg{k}", [NF, P], F32, ctx) for k in range(3)]
        penalty = pr.sb("a_penalty", [NF, P + 1], F32, ctx)
        same = [pr.sb(f"a_same{k}", [P, G, P], BF16, ctx) for k in range(S)]
        score, leaky, shifted, weight = (pr.sb("a_" + n, [P, G, H], F32, ctx) for n in ("score", "leaky", "shifted", "weight"))
        fwd, bwd = (pr.sb("a_" + n, [NF, P], F32, ctx) for n in ("fwd", "bwd"))
        identb = pr.sb("a_identb", [P, P], BF16, ctx)
        vals = [pr.sb(f"a_vals{k}", [P, G, W], F32, ctx) for k in range(3)]
        vals_part = [[pr.sb(f"a_vals_part{k}{q}", [P, G, W], BF16, ctx) for q in range(3)] for k in range(3)]
        vals_rest = pr.sb("a_vals_rest", [P, G, W], F32, ctx)
        row_ps = pr.ps("a_row_ps", [P, G * P], ctx)
        turn_ps, back_ps, head_ps, seg_ps = (pr.ps(f"a_{n}_ps", [P, 512], ctx) for n in ("turn", "back", "head", "seg"))
        sum_ps = pr.ps("a_sum_ps", [P, 1024], ctx)
        sums, _, sum_at = banked(sum_ps, W)
        names = ("rowed", "same", "spread", "scored", "turned", "peaked", "back", "shifted", "weighed", "valued", "summed",
                 "seg_turned", "seg_moved", "peaks_moved", "scanned", "scoring", "penalty_set", "out_moved",
                 "identb", "prepared", "preparing", "part0", "rest", "part1", "part2", "out_done")
        c = {n: pr.count(("s_" if n in names[:11] else "a_") + n) for n in names}
        pe_gate = pr.count("pe_gate")
        with nc.Block() as block:
            @block.sync
            def _(sp):
                io.sync(sp, used=c["valued"])

            @block.gpsimd
            def _(gp):
                def prepare(i, k):
                    ch = Chain(gp, c["preparing"], 3, S * i + k)

                    def link(ins):
                        ch.link(ins)
                        gp.sem_inc(io.gate.sem, 1)

                    seg, head, part = seg_of(k), slots["heads"][k], head_part[k]
                    io.wait_loaded(gp, i, k)
                    gp.sem_inc(io.gate.sem, 1)
                    gp.tensor_copy(wide_seg[k][:, :, :], seg.unsqueeze(2).to_broadcast([P, G, H]))
                    gp.tensor_copy(seg_part[k][0][:, :], seg)
                    link(gp.tensor_copy(part[:, :, 0, :], head[:, :, :]))
                    gp.tensor_tensor(seg_part[k][1][:, :], seg, seg_part[k][0][:, :], ALU.subtract)
                    link(gp.tensor_tensor(head_rest[:, :, :], head[:, :, :], part[:, :, 0, :], ALU.subtract))
                    link(gp.tensor_copy(part[:, :, 1, :], head_rest[:, :, :]))
                    gp.tensor_tensor(part[:, :, 2, :], head_rest[:, :, :], part[:, :, 1, :], ALU.subtract)\
                        .then_inc(c["prepared"].sem, 1)
                    ch.close()

                gp.sem_inc(c["part2"].sem, 2)
                for k in range(4):
                    prepare(0, k)
                for i, k in stepped(gp, S):
                    g = S * i + k
                    if ahead(S, i, k, 4):
                        prepare(*ahead(S, i, k, 4))
                    gp.wait_ge(c["part0"].sem, g + 1)
                    gp.sem_inc(io.gate.sem, 1)
                    gp.tensor_tensor(vals_rest[:, :, :], vals[flip(k)][:, :, :], vals_part[flip(k)][0][:, :, :], ALU.subtract)\
                        .then_inc(c["rest"].sem, 1)
                    gp.wait_ge(c["part1"].sem, g + 1)
                    gp.sem_inc(io.gate.sem, 1)
                    gp.tensor_tensor(vals_part[flip(k)][2][:, :, :], vals_rest[:, :, :], vals_part[flip(k)][1][:, :, :], ALU.subtract)\
                        .then_inc(c["part2"].sem, 1)
                    gp.wait_ge(c["part2"].sem, g + 3)
                    gp.sem_inc(io.gate.sem, 1)

            @block.vector
            def _(v):
                def compare(i, k):
                    g = S * i + k
                    io.wait_loaded(v, i, k)
                    v.wait_ge(c["rowed"].sem, g + 1)
                    v.tensor_tensor(same[k][:, :, :], row_ps[:, :].rearrange("p (t e) -> p t e", t=G),
                                    seg_of(k).unsqueeze(2).to_broadcast([P, G, P]), ALU.is_equal).then_inc(c["same"].sem, 1)

                def scores(i, k):
                    g = S * i + k
                    ch = Chain(v, c["scoring"], 4, g)
                    turned = turned_seg[flip(k)]
                    v.wait_ge(c["seg_moved"].sem, g + 1)
                    ch.link(v.tensor_tensor(penalty[:, 1:P], turned[:, 1:P], turned[:, 0:P - 1], ALU.not_equal))
                    ch.link(v.tensor_scalar(penalty[:, 1:P], penalty[:, 1:P], -BIG, None, ALU.mult))
                    io.wait_loaded(v, i, k)
                    v.wait_ge(c["spread"].sem, g + 1)
                    ch.link(v.tensor_reduce(score[:, :, :], head_ps[:, 0:3 * NF].rearrange("p (t q h) -> p t h q", t=G, q=3),
                                            AX, ALU.add))
                    ch.link(v.tensor_tensor(score[:, :, :], slots["rows"][k][:, :, D:W], score[:, :, :], ALU.add))
                    v.scalar_tensor_tensor(out=leaky[:, :, :], in0=score[:, :, :], scalar=0.2, in1=score[:, :, :],
                                           op0=ALU.mult, op1=ALU.max).then_inc(c["scored"].sem, 1)
                    ch.close()

                v.tensor_copy(identb[:, :], C.ident[:, :]).then_inc(c["identb"].sem, 1)
                v.memset(penalty[:, :], -BIG).then_inc(c["penalty_set"].sem, 1)
                v.wait_ge(c["penalty_set"].sem, 1)
                compare(0, 0)
                scores(0, 0)
                compare(0, 1)
                for i, k in stepped(v, S):
                    g = S * i + k
                    rows = slots["rows"][k]
                    ch = Chain(v, c["scanned"], 1, g)
                    v.wait_ge(c["turned"].sem, g + 1)
                    v.tensor_tensor_scan(fwd[:, :], penalty[:, 0:P], turn_ps[0:NF, 0:P], -BIG, ALU.add, ALU.max)
                    ch.link(v.tensor_tensor_scan(bwd[:, ::-1], penalty[:, 1:P + 1][:, ::-1], turn_ps[0:NF, 0:P][:, ::-1], -BIG,
                                                 ALU.add, ALU.max))
                    v.tensor_tensor(fwd[:, :], fwd[:, :], bwd[:, :], ALU.max).then_inc(c["peaked"].sem, 1)
                    if ahead(S, i, k, 2):
                        v.wait_ge(c["out_done"].sem, g + 1)
                        compare(*ahead(S, i, k, 2))
                    v.wait_ge(c["back"].sem, g + 1)
                    v.tensor_tensor(shifted[:, :, :], leaky[:, :, :],
                                    back_ps[:, 0:NF].rearrange("p (t h) -> p t h", t=G), ALU.subtract)\
                        .then_inc(c["shifted"].sem, 1)
                    if ahead(S, i, k, 1):
                        scores(*ahead(S, i, k, 1))
                    v.wait_ge(c["weighed"].sem, g + 1)
                    v.wait_ge(c["part2"].sem, g + 1)
                    val = vals[flip(k)]
                    v.tensor_copy(val[:, :, D:W], weight[:, :, :])
                    v.tensor_tensor(val[:, :, 0:D].rearrange("p t (h d) -> p t h d", h=H),
                                    rows[:, :, 0:D].rearrange("p t (h d) -> p t h d", h=H),
                                    weight[:, :, :].unsqueeze(3).to_broadcast([P, G, H, D // H]), ALU.mult)\
                        .then_inc(c["valued"].sem, 1)
                    v.wait_ge(c["valued"].sem, g + 1)

            @block.tensor
            def _(pe):
                def lay_out(i, k):
                    pe.wait_ge(c["prepared"].sem, S * i + k + 1)
                    pe.sem_inc(pe_gate.sem, 1)
                    for t in range(G):
                        for q in range(2):
                            ins = pe.matmul(row_ps[:, t * P:(t + 1) * P], seg_part[k][q][:, t:t + 1].to_broadcast([P, P]),
                                            identb[:, :], start=q == 0, stop=q == 1)
                    ins.then_inc(c["rowed"].sem, 1)

                def turn_segments(i, k):
                    pe.wait_ge(c["prepared"].sem, S * i + k + 1)
                    pe.sem_inc(pe_gate.sem, 1)
                    pe.transpose(seg_ps[0:NF, 0:P], wide_seg[k][:, :, :].rearrange("p t h -> p (t h)"), C.ident[:, :])\
                        .then_inc(c["seg_turned"].sem, 1)

                def spread(i, k):
                    pe.wait_ge(c["same"].sem, S * i + k + 1)
                    for t in range(G):
                        ins = pe.matmul(head_ps[:, t * 3 * H:(t + 1) * 3 * H], same[k][:, t, :],
                                        head_part[k][:, t, :, :].rearrange("p q h -> p (q h)"), start=True, stop=True)
                    ins.then_inc(c["spread"].sem, 1)

                def turn_scores(i, k):
                    pe.wait_ge(c["scored"].sem, S * i + k + 1)
                    pe.sem_inc(pe_gate.sem, 1)
                    pe.transpose(turn_ps[0:NF, 0:P], leaky[:, :, :].rearrange("p t h -> p (t h)"), C.ident[:, :])\
                        .then_inc(c["turned"].sem, 1)

                def sum_up(i, k):
                    g = S * i + k
                    pe.wait_ge(c["part2"].sem, g + 3)
                    pe.wait_ge(c["out_done"].sem, g + 2)
                    pe.sem_inc(pe_gate.sem, 1)
                    for t in range(G):
                        for q in range(3):
                            ins = pe.matmul(sum_ps[:, sum_at(t):sum_at(t) + W], same[k][:, t, :], vals_part[flip(k)][q][:, t, :],
                                            start=q == 0, stop=q == 2)
                    ins.then_inc(c["summed"].sem, 1)

                pe.wait_ge(c["identb"].sem, 1)
                lay_out(0, 0)
                turn_segments(0, 0)
                spread(0, 0)
                lay_out(0, 1)
                turn_scores(0, 0)
                turn_segments(0, 1)
                spread(0, 1)
                lay_out(0, 2)
                for i, k in stepped(pe, S):
                    g = S * i + k
                    pe.wait_ge(c["peaked"].sem, g + 1)
                    pe.wait_ge(c["peaks_moved"].sem, g + 1)
                    pe.sem_inc(pe_gate.sem, 1)
                    pe.transpose(back_ps[:, 0:NF], fwd[:, :], C.ident[0:NF, 0:NF]).then_inc(c["back"].sem, 1)
                    if before(S, i, k):
                        sum_up(*before(S, i, k))
                    if ahead(S, i, k, 3):
                        pe.wait_ge(c["same"].sem, g + 3)
                        lay_out(*ahead(S, i, k, 3))
                    if ahead(S, i, k, 1):
                        turn_scores(*ahead(S, i, k, 1))
                    if ahead(S, i, k, 2):
                        turn_segments(*ahead(S, i, k, 2))
                        spread(*ahead(S, i, k, 2))
                sum_up(NGRP // S - 1, S - 1)

            @block.scalar
            def _(act):
                def move_segments(i, k):
                    act.wait_ge(c["seg_turned"].sem, S * i + k + 1)
                    act.activation(turned_seg[flip(k)][:, :], seg_ps[0:NF, 0:P], ACT.Copy).then_inc(c["seg_moved"].sem, 1)

                def move_sums(i, k):
                    g = S * i + k
                    act.wait_ge(c["summed"].sem, g + 1)
                    act.activation(io.out[k][:, :, 0:W].rearrange("p (a b) w -> p a b w", a=sums.shape[1]),
                                   sums.rearrange("p a (b w) -> p a b w", w=W), ACT.Copy).then_inc(c["out_moved"].sem, 1)
                    act.wait_ge(c["out_moved"].sem, g + 1)
                    act.sem_inc(c["out_done"].sem, 1)
                    act.sem_inc(io.done.sem, 1)

                act.sem_inc(c["out_done"].sem, 2)
                act.sem_inc(c["peaks_moved"].sem, 1)
                move_segments(0, 0)
                move_segments(0, 1)
                for i, k in stepped(act, S):
                    g = S * i + k
                    act.wait_ge(c["shifted"].sem, g + 1)
                    act.activation(weight[:, :, :], shifted[:, :, :], ACT.Exp).then_inc(c["weighed"].sem, 1)
                    io.wait_out_free(act, g)
                    act.activation(io.out[k][:, :, W:W + H], back_ps[:, 0:NF].rearrange("p (t h) -> p t h", t=G), ACT.Copy)\
                        .then_inc(c["peaks_moved"].sem, 1)
                    act.wait_ge(c["valued"].sem, g + 1)
                    act.activation(vals_part[flip(k)][0][:, :, :], vals[flip(k)][:, :, :], ACT.Copy).then_inc(c["part0"].sem, 1)
                    if before(S, i, k):
                        move_sums(*before(S, i, k))
                    act.wait_ge(c["rest"].sem, g + 1)
                    act.activation(vals_part[flip(k)][1][:, :, :], vals_rest[:, :, :], ACT.Copy).then_inc(c["part1"].sem, 1)
                    if ahead(S, i, k, 2):
                        move_segments(*ahead(S, i, k, 2))
                move_sums(NGRP // S - 1, S - 1)
        io.passed()
        for n in names[:11]:
            c[n].passed(NGRP)


def softmax_edges(pr, C, tag, table, seg_col, index_col, heads, part, edge_w):
    nc = pr.nc
    H = 1
    HW = D
    W = D + H
    NF = G
    with ExitStack() as ctx:
        loads = common_loads(index_col, seg_col) + [
            ("heads", [P, G, HW], F32, [(whole3, tile_rows(heads))]),
            ("fk", [NF, P + 1], F32, [(whole, lambda g: C.fk_dst[bass.ds(NF * g, NF), :])]),
            ("attr", [P, G, 32], F32, [(whole3, tile_rows(C.edge_attr))]),
        ]
        io = EdgeIO(pr, tag, ctx, loads, table, 2 * D, part, W + H)
        slots = io.slot

        def seg_of(k):
            return slots["seg"][k][:, :]

        same = [pr.sb(f"{tag}_same{k}", [P, G, P], F32, ctx) for k in range(2)]
        leaky = pr.sb(f"{tag}_leaky", [P, G, H], F32, ctx)
        fwd = pr.sb(f"{tag}_fwd", [NF, P], F32, ctx)
        bwd = pr.sb(f"{tag}_bwd", [NF, P], F32, ctx)
        shifted = pr.sb(f"{tag}_shifted", [P, G, H], F32, ctx)
        vals = pr.sb(f"{tag}_vals", [P, G, W], F32, ctx)
        weight = pr.sb(f"{tag}_weight", [P, G, H], F32, ctx)
        row_ps = pr.ps(f"{tag}_row_ps", [P, G * P], ctx)
        small = pr.ps(f"{tag}_small", [P, 512], ctx)
        head_ps = pr.ps(f"{tag}_head_ps", [P, 512], ctx)
        sum_ps = pr.ps(f"{tag}_sum_ps", [P, 1024], ctx)
        ew = pr.sb(f"{tag}_ew", [P, 4, D], F32, ctx)
        attrT = pr.sb(f"{tag}_attrT", [P, 2, P], F32, ctx)
        both = pr.sb(f"{tag}_both", [P, G, 2, D], F32, ctx)
        prod = pr.sb(f"{tag}_prod", [P, G, D], F32, ctx)
        attr_ps = pr.ps(f"{tag}_attr_ps", [P, 512], ctx)
        edge_ps = pr.ps(f"{tag}_edge_ps", [P, 512], ctx)
        sums, _, sum_at = banked(sum_ps, W)
        c = {n: pr.count("s_" + n) for n in ("rowed", "same", "spread", "scored", "turned", "peaked", "back", "shifted",
                                             "weighed", "valued", "summed", "dve", "act", "edge_w", "attr_turned",
                                             "attr_moved", "edged", "ew_loaded")}
        pe_gate = pr.count("pe_gate")
        dper = 3
        with nc.Block() as block:
            @block.sync
            def _(sp):
                sp.wait_ge(c["edge_w"].sem, c["edge_w"].at(1))
                for q in range(4):
                    sp.dma_start(ew[32 * q:32 * q + 32, q, :], edge_w).then_inc(c["ew_loaded"].sem, 16)
                io.sync(sp)

            @block.gpsimd
            def _(gp):
                io.gather(gp)
            @block.vector
            def _(v):
                v.memset(ew[:, :, :], 0.0).then_inc(c["edge_w"].sem, 1)

                def compare(i, k):
                    g = S * i + k
                    io.wait_loaded(v, i, k)
                    v.wait_ge(c["rowed"].sem, g + c["rowed"].at(1))
                    v.tensor_tensor(same[k % 2][:, :, :], row_ps[:, :].rearrange("p (t e) -> p t e", t=G),
                                    seg_of(k).unsqueeze(2).to_broadcast([P, G, P]), ALU.is_equal)\
                        .then_inc(c["same"].sem, 1)

                compare(0, 0)
                for i, k, after in groups(v):
                    g = S * i + k
                    ch = Chain(v, c["dve"], dper, g)
                    rows, fks = io.rows[k], slots["fk"][k]
                    io.wait_loaded(v, i, k)
                    io.wait_gathered(v, i, k)
                    v.wait_ge(c["edged"].sem, g + c["edged"].at(1))
                    ch.link(v.tensor_tensor(both[:, :, :, :], rows[:, :, :].rearrange("p t (j d) -> p t j d", j=2),
                                            edge_ps[:, :].rearrange("p (t d) -> p t d", t=G).unsqueeze(2)
                                            .to_broadcast([P, G, 2, D]), ALU.add))
                    v.wait_ge(c["spread"].sem, g + c["spread"].at(1))
                    ch.link(v.scalar_tensor_tensor(out=prod[:, :, :], in0=both[:, :, 0, :], scalar=float(D) ** -0.5,
                                                   in1=head_ps[:, :].rearrange("p (t d) -> p t d", t=G),
                                                   op0=ALU.mult, op1=ALU.mult))
                    v.tensor_reduce(leaky[:, :, :], prod[:, :, :], AX, ALU.add).then_inc(c["scored"].sem, 1)
                    v.wait_ge(io.ready.sem, g + io.ready.at(1))
                    if after:
                        compare(*after)
                    v.wait_ge(c["turned"].sem, g + c["turned"].at(1))
                    v.tensor_tensor_scan(fwd[:, :], fks[:, 0:P], small[0:NF, 0:P], -BIG, ALU.add, ALU.max)
                    ch.link(v.tensor_tensor_scan(bwd[:, ::-1], fks[:, 1:P + 1][:, ::-1], small[0:NF, 0:P][:, ::-1], -BIG,
                                                 ALU.add, ALU.max))
                    v.tensor_tensor(fwd[:, :], fwd[:, :], bwd[:, :], ALU.max).then_inc(c["peaked"].sem, 1)
                    v.wait_ge(c["back"].sem, g + c["back"].at(1))
                    v.tensor_tensor(shifted[:, :, :], leaky[:, :, :],
                                    small[:, P:P + G * H].rearrange("p (t h) -> p t h", t=G), ALU.subtract)\
                        .then_inc(c["shifted"].sem, 1)
                    v.wait_ge(c["weighed"].sem, g + c["weighed"].at(1))
                    v.tensor_copy(vals[:, :, D:D + H], weight[:, :, :])
                    ins = v.tensor_tensor(vals[:, :, 0:D], both[:, :, 1, :], weight[:, :, :].to_broadcast([P, G, D]), ALU.mult)
                    ins.then_inc(c["valued"].sem, 1)
                    v.wait_ge(c["valued"].sem, g + c["valued"].at(1))
                    ch.close()

            @block.tensor
            def _(pe):
                pe.wait_ge(c["ew_loaded"].sem, c["ew_loaded"].at(64))

                def lay_out(i, k):
                    g = S * i + k
                    io.wait_loaded(pe, i, k)
                    for t in range(G):
                        ins = pe.transpose(row_ps[:, t * P:(t + 1) * P], seg_of(k)[:, t:t + 1].to_broadcast([P, P]), C.ident[:, :])
                    ins.then_inc(c["rowed"].sem, 1)

                def features(i, k):
                    g = S * i + k
                    for q in range(2):
                        ins = pe.transpose(attr_ps[:, q * P:(q + 1) * P],
                                           slots["attr"][k][:, 4 * q:4 * q + 4, :].rearrange("p t c -> p (t c)"), C.ident[:, :])
                    ins.then_inc(c["attr_turned"].sem, 1)
                    pe.wait_ge(c["attr_moved"].sem, g + c["attr_moved"].at(1))
                    for q in range(2):
                        ins = pe.matmul(edge_ps[:, q * 256:(q + 1) * 256], attrT[:, q, :], ew[:, :, :].rearrange("p q d -> p (q d)"),
                                        start=True, stop=True)
                    ins.then_inc(c["edged"].sem, 1)

                def turn_segments(i, k):
                    pe.wait_ge(c["widened"].sem, S * i + k + c["widened"].at(1))
                    pe.sem_inc(pe_gate.sem, 1)
                    pe.transpose(seg_ps[0:NF, 0:P], wide_seg[k][:, :, :].rearrange("p t h -> p (t h)"), C.ident[:, :])\
                        .then_inc(c["attr_turned"].sem, 1)

                def spread(i, k):
                    g = S * i + k
                    pe.wait_ge(c["same"].sem, g + c["same"].at(1))
                    for t in range(G):
                        ins = pe.matmul(head_ps[:, t * HW:(t + 1) * HW], same[k % 2][:, t, :], slots["heads"][k][:, t, :], start=True, stop=True)
                    ins.then_inc(c["spread"].sem, 1)

                lay_out(0, 0)
                features(0, 0)
                spread(0, 0)
                for i, k, after in groups(pe):
                    g = S * i + k
                    if after:
                        lay_out(*after)
                    pe.wait_ge(c["scored"].sem, g + c["scored"].at(1))
                    pe.wait_ge(io.ready.sem, g + io.ready.at(1))
                    pe.sem_inc(pe_gate.sem, 1)
                    pe.transpose(small[0:NF, 0:P], leaky[:, :, :].rearrange("p t h -> p (t h)"), C.ident[:, :]).then_inc(c["turned"].sem, 1)
                    if after:
                        features(*after)
                    pe.wait_ge(c["peaked"].sem, g + c["peaked"].at(1))
                    pe.sem_inc(pe_gate.sem, 1)
                    pe.transpose(small[:, P:P + NF], fwd[:, :], C.ident[0:NF, 0:NF]).then_inc(c["back"].sem, 1)
                    if after:
                        spread(*after)
                    pe.wait_ge(c["valued"].sem, g + c["valued"].at(1))
                    for t in range(G):
                        ins = pe.matmul(sum_ps[:, sum_at(t):sum_at(t) + W], same[k % 2][:, t, :], vals[:, t, :], start=True, stop=True)
                    ins.then_inc(c["summed"].sem, 1)

            @block.scalar
            def _(act):
                def move_features(i, k):
                    g = S * i + k
                    act.wait_ge(c["attr_turned"].sem, g + c["attr_turned"].at(1))
                    ins = act.activation(attrT[:, :, :].rearrange("p q e -> p (q e)"), attr_ps[:, 0:2 * P], ACT.Copy)
                    ins.then_inc(c["attr_moved"].sem, 1)

                act.sem_inc(io.ready.sem, 1)
                move_features(0, 0)
                for i, k, after in groups(act):
                    g = S * i + k
                    if after:
                        move_features(*after)
                    act.wait_ge(c["shifted"].sem, g + c["shifted"].at(1))
                    act.activation(weight[:, :, :], shifted[:, :, :], ACT.Exp).then_inc(c["weighed"].sem, 1)
                    io.wait_out_free(act, g)
                    act.activation(io.out[k][:, :, W:W + H], small[:, P:P + NF].rearrange("p (t h) -> p t h", t=G), ACT.Copy)\
                        .then_inc(c["act"].sem, 1)
                    act.wait_ge(c["summed"].sem, g + c["summed"].at(1))
                    act.activation(io.out[k][:, :, 0:W].rearrange("p (a b) w -> p a b w", a=sums.shape[1]),
                                   sums.rearrange("p a (b w) -> p a b w", w=W), ACT.Copy).then_inc(c["act"].sem, 1)
                    act.wait_ge(c["act"].sem, g * 2 + c["act"].at(2))
                    act.sem_inc(io.ready.sem, 1)
                    act.sem_inc(io.done.sem, 1)
        io.passed()
        for n in ("rowed", "same", "spread", "scored", "turned", "peaked", "back", "shifted", "weighed", "valued", "summed"):
            c[n].passed(NGRP)
        c["act"].passed(2 * NGRP)
        c["dve"].passed(dper * NGRP)
        c["edge_w"].passed(1)
        c["attr_turned"].passed(NGRP)
        c["attr_moved"].passed(NGRP)
        c["ew_loaded"].passed(64)
        c["edged"].passed(NGRP)


def mlp_edges(pr, C, table, heads, part, be2, We2):
    nc = pr.nc
    H2 = 2 * D
    tag = "m"
    with ExitStack() as ctx:
        def fk_of(par):
            view = C.fk_dst.rearrange("(g j two) c -> g two j c", two=2, j=G // 2)
            return lambda g: view[bass.ds(g, 1), par, :, 0:P].to_broadcast([D, G // 2, P])

        loads = common_loads(C.src_col_i, C.dst_col) + [
            ("heads", [P, G, H2], F32, [(whole3, tile_rows(heads))]),
            ("fk", [P, G // 2, P], F32, [(lambda a: a[0:D, :, :], fk_of(0)), (lambda a: a[D:P, :, :], fk_of(1))]),
        ]
        io = EdgeIO(pr, tag, ctx, loads, table, H2 + D, part, H2)
        slots = io.slot
        same = [pr.sb(f"m_same{k}", [P, G, P], F32, ctx) for k in range(2)]
        hidden = pr.sb("m_hidden", [P, G, H2], F32, ctx)
        logit = pr.sb("m_logit", [P, G], F32, ctx)
        gate = pr.sb("m_gate", [P, G], F32, ctx)
        msg = pr.sb("m_msg", [P, G, D], F32, ctx)
        top = pr.sb("m_top", [P, G // 2 * P], F32, ctx)
        w2 = pr.sb("m_w2", [P, H2], F32, ctx)
        b2 = pr.sb("m_b2", [P, 1], F32, ctx)
        row_ps = pr.ps("m_row_ps", [P, G * P], ctx)
        head_ps = pr.ps("m_head_ps", [P, G * H2], ctx)
        sum_ps = pr.ps("m_sum_ps", [P, 512], ctx)
        msgT_ps = pr.ps("m_msgT_ps", [P, 512], ctx)
        top_ps = pr.ps("m_top_ps", [P, 512], ctx)
        c = {n: pr.count("s_" + n) for n in ("rowed", "same", "spread", "scored", "turned", "peaked", "back",
                                             "weighed", "valued", "summed", "dve", "act", "edge_w")}
        with nc.Block() as block:
            @block.sync
            def _(sp):
                sp.dma_start(w2[:, :], We2.rearrange("k a -> a k").to_broadcast([P, H2])).then_inc(c["edge_w"].sem, 16)
                sp.dma_start(b2[:, :], be2.unsqueeze(0).to_broadcast([P, 1])).then_inc(c["edge_w"].sem, 16)
                io.sync(sp)

            @block.gpsimd
            def _(gp):
                io.gather(gp)

            @block.vector
            def _(v):
                def compare(i, k):
                    g = S * i + k
                    io.wait_loaded(v, i, k)
                    v.wait_ge(c["rowed"].sem, g + c["rowed"].at(1))
                    v.tensor_tensor(same[k % 2][:, :, :], row_ps[:, :].rearrange("p (t e) -> p t e", t=G),
                                    slots["seg"][k][:, :].unsqueeze(2).to_broadcast([P, G, P]), ALU.is_equal)\
                        .then_inc(c["same"].sem, 1)

                v.wait_ge(c["edge_w"].sem, c["edge_w"].at(32))
                compare(0, 0)
                for i, k, after in groups(v):
                    g = S * i + k
                    ch = Chain(v, c["dve"], 2, g)
                    rows = io.rows[k]
                    io.wait_loaded(v, i, k)
                    io.wait_gathered(v, i, k)
                    v.wait_ge(c["spread"].sem, g + c["spread"].at(1))
                    ch.link(v.tensor_tensor(hidden[:, :, :], rows[:, :, 0:H2],
                                            head_ps[:, :].rearrange("p (t w) -> p t w", t=G), ALU.add))
                    ch.link(v.scalar_tensor_tensor(out=hidden[:, :, :], in0=hidden[:, :, :], scalar=0.0,
                                                   in1=w2[:, :].unsqueeze(1).to_broadcast([P, G, H2]), op0=ALU.max, op1=ALU.mult))
                    v.tensor_reduce(logit[:, :], hidden[:, :, :], AX, ALU.add).then_inc(c["scored"].sem, 1)
                    v.wait_ge(io.ready.sem, g + io.ready.at(1))
                    if after:
                        compare(*after)
                    v.wait_ge(c["weighed"].sem, g + c["weighed"].at(1))
                    v.tensor_tensor(msg[:, :, :], rows[:, :, H2:H2 + D], gate[:, :].unsqueeze(2).to_broadcast([P, G, D]),
                                    ALU.mult).then_inc(c["valued"].sem, 1)
                    v.wait_ge(c["turned"].sem, g + c["turned"].at(1))
                    v.tensor_tensor_scan(top[:, :], slots["fk"][k][:, :, :].rearrange("p j e -> p (j e)"), msgT_ps[:, :],
                                         -BIG, ALU.add, ALU.max).then_inc(c["peaked"].sem, 1)
                    ch.close()

            @block.tensor
            def _(pe):
                def lay_out(i, k):
                    g = S * i + k
                    io.wait_loaded(pe, i, k)
                    for t in range(G):
                        ins = pe.transpose(row_ps[:, t * P:(t + 1) * P], slots["seg"][k][:, t:t + 1].to_broadcast([P, P]), C.ident[:, :])
                    ins.then_inc(c["rowed"].sem, 1)

                def spread(i, k):
                    g = S * i + k
                    pe.wait_ge(c["same"].sem, g + c["same"].at(1))
                    for t in range(G):
                        ins = pe.matmul(head_ps[:, t * H2:(t + 1) * H2], same[k % 2][:, t, :], slots["heads"][k][:, t, :], start=True, stop=True)
                    ins.then_inc(c["spread"].sem, 1)

                lay_out(0, 0)
                spread(0, 0)
                for i, k, after in groups(pe):
                    g = S * i + k
                    if after:
                        lay_out(*after)
                    pe.wait_ge(c["valued"].sem, g + c["valued"].at(1))
                    pe.wait_ge(io.ready.sem, g + io.ready.at(1))
                    for j in range(G // 2):
                        ins = pe.transpose(msgT_ps[:, j * P:(j + 1) * P], msg[:, 2 * j:2 * j + 2, :].rearrange("p t d -> p (t d)"), C.ident[:, :])
                    ins.then_inc(c["turned"].sem, 1)
                    if after:
                        spread(*after)
                    for t in range(G):
                        ins = pe.matmul(sum_ps[:, t * D:(t + 1) * D], same[k % 2][:, t, :], msg[:, t, :], start=True, stop=True)
                    ins.then_inc(c["summed"].sem, 1)
                    pe.wait_ge(c["peaked"].sem, g + c["peaked"].at(1))
                    for j in range(G // 2):
                        ins = pe.transpose(top_ps[:, j * P:(j + 1) * P], top[:, j * P:(j + 1) * P], C.ident[:, :])
                    ins.then_inc(c["back"].sem, 1)

            @block.scalar
            def _(act):
                act.wait_ge(c["edge_w"].sem, c["edge_w"].at(32))
                act.sem_inc(io.ready.sem, 1)
                for i, k, after in groups(act):
                    g = S * i + k
                    act.wait_ge(c["scored"].sem, g + c["scored"].at(1))
                    act.activation(gate[:, :], logit[:, :], ACT.Sigmoid, bias=b2[:, :]).then_inc(c["weighed"].sem, 1)
                    io.wait_out_free(act, g)
                    act.wait_ge(c["summed"].sem, g + c["summed"].at(1))
                    act.activation(io.out[k][:, :, 0:D], sum_ps[:, :].rearrange("p (t d) -> p t d", t=G), ACT.Copy).then_inc(c["act"].sem, 1)
                    act.wait_ge(c["back"].sem, g + c["back"].at(1))
                    act.activation(io.out[k][:, :, D:H2], top_ps[:, :].rearrange("p (t d) -> p t d", t=G), ACT.Copy).then_inc(c["act"].sem, 1)
                    act.wait_ge(c["act"].sem, g * 2 + c["act"].at(2))
                    act.sem_inc(io.ready.sem, 1)
                    act.sem_inc(io.done.sem, 1)
        io.passed()
        for n in ("rowed", "same", "spread", "scored", "turned", "peaked", "back", "weighed", "valued", "summed"):
            c[n].passed(NGRP)
        c["act"].passed(2 * NGRP)
        c["dve"].passed(2 * NGRP)
        c["edge_w"].passed(32)


def gcn_edges(pr, C, table, part):
    nc = pr.nc
    with ExitStack() as ctx:
        io = EdgeIO(pr, "g", ctx, common_loads(C.src_col_i, C.dst_col), table, D, part, D)
        slots = io.slot
        same = [pr.sb(f"g_same{k}", [P, G, P], F32, ctx) for k in range(S)]
        row_ps = pr.ps("g_row_ps", [P, G * P], ctx)
        sum_ps = pr.ps("g_sum_ps", [P, 512], ctx)
        c = {n: pr.count("s_" + n) for n in ("rowed", "same", "summed", "act")}
        with nc.Block() as block:
            @block.sync
            def _(sp):
                io.sync(sp)

            @block.gpsimd
            def _(gp):
                io.gather(gp)

            @block.vector
            def _(v):
                for i, k, after in groups(v):
                    g = S * i + k
                    io.wait_loaded(v, i, k)
                    v.wait_ge(c["rowed"].sem, g + c["rowed"].at(1))
                    v.tensor_tensor(same[k][:, :, :], row_ps[:, :].rearrange("p (t e) -> p t e", t=G),
                                    slots["seg"][k][:, :].unsqueeze(2).to_broadcast([P, G, P]), ALU.is_equal)\
                        .then_inc(c["same"].sem, 1)

            @block.tensor
            def _(pe):
                for i, k, after in groups(pe):
                    g = S * i + k
                    io.wait_loaded(pe, i, k)
                    for t in range(G):
                        ins = pe.transpose(row_ps[:, t * P:(t + 1) * P], slots["seg"][k][:, t:t + 1].to_broadcast([P, P]), C.ident[:, :])
                    ins.then_inc(c["rowed"].sem, 1)
                    pe.wait_ge(c["same"].sem, g + c["same"].at(1))
                    io.wait_gathered(pe, i, k)
                    pe.wait_ge(io.ready.sem, g + io.ready.at(1))
                    for t in range(G):
                        ins = pe.matmul(sum_ps[:, t * D:(t + 1) * D], same[k][:, t, :], io.rows[k][:, t, :], start=True, stop=True)
                    ins.then_inc(c["summed"].sem, 1)

            @block.scalar
            def _(act):
                act.sem_inc(io.ready.sem, 1)
                for i, k, after in groups(act):
                    g = S * i + k
                    io.wait_out_free(act, g)
                    act.wait_ge(c["summed"].sem, g + c["summed"].at(1))
                    act.activation(io.out[k][:, :, :], sum_ps[:, :].rearrange("p (t d) -> p t d", t=G), ACT.Copy).then_inc(c["act"].sem, 1)
                    act.wait_ge(c["act"].sem, g + c["act"].at(1))
                    act.sem_inc(io.ready.sem, 1)
                    act.sem_inc(io.done.sem, 1)
        io.passed()
        for n in ("rowed", "same", "summed", "act"):
            c[n].passed(NGRP)


def carry(pr, C, kind, part, carry_dram, keep, H=0):
    nc = pr.nc
    soft = kind == "softmax"
    W = {"sum": D, "sum_max": 2 * D, "softmax": D + H}[kind]
    with ExitStack() as ctx:
        t_rows = pr.sb("c_rows", [RB, NB, W + H], F32, ctx)
        wide = pr.sb("c_wide", [RB, NB, W], F32, ctx)
        n = [pr.sb(f"c_buf{j}", [P, ET], F32, ctx) for j in range(6 if soft else 3)]
        back = pr.sb("c_back", [RB, NB, 2 * W if soft else W], F32, ctx)
        ps = [pr.ps(f"c_ps{j}", [P, 2048], ctx) for j in range(2)]
        ld, dv, tr, ex, st = (pr.count("c_" + x) for x in ("loaded", "dve", "turned", "exp", "stored"))
        marks = {}
        with nc.Block() as block:
            @block.sync
            def _(sp):
                sp.dma_start(t_rows[:, :, :], part.rearrange("(b r e) w -> r b e w", r=RB, e=P)[:, :, P - 1, :]).then_inc(ld.sem, 16)

            @block.vector
            def _(v):
                ch = Chain(v, dv)
                v.wait_ge(ld.sem, ld.at(16))
                if soft:
                    ch.link(v.tensor_copy(wide[:, :, 0:D].rearrange("r b (h d) -> r b h d", h=H),
                                          t_rows[:, :, W:W + H].unsqueeze(3).to_broadcast([RB, NB, H, D // H])))
                    ch.link(v.tensor_copy(wide[:, :, D:W], t_rows[:, :, W:W + H]))
                marks["wide"] = ch.n
                v.wait_ge(tr.sem, tr.at(1))
                val, pen = n[0], n[1]
                ch.link(v.tensor_scalar(pen[:, :], keep[:, :], BIG, -BIG, ALU.mult, ALU.add))
                ch.link(v.tensor_copy(by_bank(val[0:W, :]), blocks(ps[0])[0:W]))
                if kind == "sum":
                    ch.link(v.tensor_tensor_scan(n[2][0:W, :], keep[0:W, :], val[0:W, :], 0.0, ALU.mult, ALU.add))
                elif kind == "sum_max":
                    ch.link(v.tensor_tensor_scan(n[2][0:D, :], keep[0:D, :], val[0:D, :], 0.0, ALU.mult, ALU.add))
                    ch.link(v.tensor_tensor_scan(n[2][D:W, :], pen[D:W, :], val[D:W, :], -BIG, ALU.add, ALU.max))
                else:
                    top, peak, ratio = n[2], n[3], n[4]
                    ch.link(v.tensor_copy(by_bank(top[0:W, :]), blocks(ps[1])[0:W]))
                    ch.link(v.tensor_tensor_scan(peak[0:W, :], pen[0:W, :], top[0:W, :], -BIG, ALU.add, ALU.max))
                    ch.link(v.memset(ratio[0:W, 0:1], 0.0))
                    ch.link(v.tensor_tensor(ratio[0:W, 1:ET], peak[0:W, 0:ET - 1], peak[0:W, 1:ET], ALU.subtract))
                    ch.link(v.tensor_scalar(ratio[0:W, :], ratio[0:W, :], 0.0, None, ALU.min))
                    ch.link(v.tensor_tensor(top[0:W, :], top[0:W, :], peak[0:W, :], ALU.subtract))
                    marks["exp"] = ch.n
                    v.wait_ge(ex.sem, ex.at(2))
                    ch.link(v.tensor_tensor(ratio[0:W, :], ratio[0:W, :], keep[0:W, :], ALU.mult))
                    ch.link(v.tensor_tensor(val[0:W, :], val[0:W, :], top[0:W, :], ALU.mult))
                    ch.link(v.tensor_tensor_scan(n[5][0:W, :], ratio[0:W, :], val[0:W, :], 0.0, ALU.mult, ALU.add))
                marks["scanned"] = ch.n
                v.wait_ge(tr.sem, tr.at(2))
                for j in range(2 if soft else 1):
                    ch.link(v.tensor_copy(back[:, :, j * W:(j + 1) * W], ps[j][0:RB, :].rearrange("r (b w) -> r b w", b=NB)[:, :, 0:W]))
                marks["back"] = ch.n

            @block.tensor
            def _(pe):
                pe.wait_ge(ld.sem, ld.at(16))
                if soft:
                    pe.wait_ge(dv.sem, dv.at(marks["wide"]))
                for j in range(2 if soft else 1):
                    for b in range(NB):
                        ins = pe.transpose(ps[j][0:W, block_at(b):block_at(b) + RB], t_rows[:, b, 0:W] if j == 0 else wide[:, b, :],
                                           C.ident[0:RB, 0:RB])
                ins.then_inc(tr.sem, 1)
                pe.wait_ge(dv.sem, dv.at(marks["scanned"]))
                res = (n[5], n[3]) if soft else (n[2],)
                for j, r in enumerate(res):
                    for b in range(NB):
                        ins = pe.transpose(ps[j][0:RB, b * P:b * P + W], r[0:W, b * RB:(b + 1) * RB], C.ident[0:W, 0:W])
                ins.then_inc(tr.sem, 1)

            @block.scalar
            def _(act):
                if soft:
                    act.wait_ge(dv.sem, dv.at(marks["exp"]))
                    act.activation(n[4][0:W, :], n[4][0:W, :], ACT.Exp).then_inc(ex.sem, 1)
                    act.activation(n[2][0:W, :], n[2][0:W, :], ACT.Exp).then_inc(ex.sem, 1)
                act.wait_ge(dv.sem, dv.at(marks["back"]))
                act.dma_start(carry_dram.rearrange("(b r) w -> r b w", r=RB), back[:, :, :]).then_inc(st.sem, 16)
                act.wait_ge(st.sem, st.at(16))
        ld.passed(16)
        dv.passed(marks["back"])
        tr.passed(2)
        st.passed(16)
        if soft:
            ex.passed(2)


def node_results(pr, C, kind, part, carry_dram, ix, has, spans, result, H=0, eps=0.0):
    nc = pr.nc
    soft = kind == "softmax"
    W = {"sum": D, "sum_max": 2 * D, "softmax": D + H}[kind]
    PW, CW = W + H, 2 * W if soft else W
    with ExitStack() as ctx:
        index = [pr.sb(f"n_index{k}", [P, 2, NG], I32, ctx) for k in range(2)]
        own = [pr.sb(f"n_own{k}", [P, NG, PW], F32, ctx) for k in range(2)]
        old = [pr.sb(f"n_old{k}", [P, NG, CW], F32, ctx) for k in range(2)]
        pen = pr.sb("n_pen", [P, NG], F32, ctx)
        top = pr.sb("n_top", [P, NG, max(H, 1)], F32, ctx)
        dif = pr.sb("n_dif", [P, NG, 2, max(H, 1)], F32, ctx)
        mul = pr.sb("n_mul", [P, NG, 2, max(H, 1)], F32, ctx)
        acc = pr.sb("n_acc", [P, NG, W], F32, ctx)
        ld = [pr.count(f"n_loaded{k}") for k in range(2)]
        got = [pr.count(f"n_gathered{k}") for k in range(2)]
        done, dv, ask, ex, gate = (pr.count("n_" + x) for x in ("done", "dve", "asked", "exp", "gate"))
        per = 12 if soft else {"sum": 3, "sum_max": 5}[kind]
        with nc.Block() as block:
            @block.sync
            def _(sp):
                def load(g, k):
                    for q in range(2):
                        sp.dma_start(index[k][:, q, :], ix[1 + q][:, bass.ds(NG * g, NG)]).then_inc(ld[k].sem, 16)
                for k in range(2):
                    load(k, k)
                with sp.Fori(0, NNG // 2 - 1) as i:
                    for k in range(2):
                        sp.wait_ge(done.sem, 2 * i + done.at(k + 1))
                        load(2 * i + (k + 2), k)

            @block.gpsimd
            def _(gp):
                with gp.Fori(0, NNG // 2) as i:
                    for k in range(2):
                        gp.wait_ge(ld[k].sem, i * 32 + ld[k].at(32))
                        gp.sem_inc(gate.sem, 1)
                        for q, (rows, src) in enumerate(((own[k], part), (old[k], carry_dram))):
                            for t in range(NG):
                                gp.indirect_dma_start(rows[:, t, :], None, src,
                                                      bass.IndirectOffsetOnAxis(ap=index[k][:, q, t:t + 1], axis=0)).then_inc(got[k].sem, 16)

            @block.vector
            def _(v):
                with v.Fori(0, NNG // 2) as i:
                    for k in range(2):
                        g = 2 * i + k
                        ch = Chain(v, dv, per, g)
                        tiles = bass.ds(NG * g, NG)
                        over = lambda m, w: m[:, tiles].unsqueeze(2).to_broadcast([P, NG, w])
                        v.wait_ge(got[k].sem, i * (32 * NG) + got[k].at(32 * NG))
                        o, c = own[k], old[k]
                        if not soft:
                            ch.link(v.tensor_tensor(c[:, :, 0:D], c[:, :, 0:D], over(spans, D), ALU.mult))
                            ch.link(v.tensor_tensor(o[:, :, 0:D], o[:, :, 0:D], c[:, :, 0:D], ALU.add))
                            if kind == "sum_max":
                                ch.link(v.tensor_tensor(c[:, :, D:W], c[:, :, D:W], over(spans, D), ALU.mult))
                                ch.link(v.tensor_tensor(o[:, :, D:W], o[:, :, D:W], c[:, :, D:W], ALU.max))
                            ch.link(v.tensor_tensor(result[:, tiles, :], o[:, :, :], over(has, W), ALU.mult))
                        else:
                            ch.link(v.tensor_scalar(pen[:, :], spans[:, tiles], BIG, -BIG, ALU.mult, ALU.add))
                            cm = c[:, :, W + D:W + D + H]
                            ch.link(v.tensor_tensor(cm, cm, pen[:, :].unsqueeze(2).to_broadcast([P, NG, H]), ALU.add))
                            ch.link(v.tensor_tensor(top[:, :, :], o[:, :, W:W + H], cm, ALU.max))
                            ch.link(v.tensor_tensor(dif[:, :, 0, :], o[:, :, W:W + H], top[:, :, :], ALU.subtract))
                            ch.link(v.tensor_tensor(dif[:, :, 1, :], cm, top[:, :, :], ALU.subtract))
                            v.sem_inc(ask.sem, 1)
                            v.wait_ge(ex.sem, g + ex.at(1))
                            for q, rows in enumerate((o, c)):
                                v.tensor_tensor(rows[:, :, 0:D].rearrange("p t (h d) -> p t h d", h=H),
                                                rows[:, :, 0:D].rearrange("p t (h d) -> p t h d", h=H),
                                                mul[:, :, q, :].unsqueeze(3).to_broadcast([P, NG, H, D // H]), ALU.mult)
                                ch.link(v.tensor_tensor(rows[:, :, D:W], rows[:, :, D:W], mul[:, :, q, :], ALU.mult))
                            ch.link(v.tensor_tensor(acc[:, :, :], o[:, :, 0:W], c[:, :, 0:W], ALU.add))
                            ch.link(v.tensor_scalar(acc[:, :, D:W], acc[:, :, D:W], eps, None, ALU.add))
                            ch.link(v.reciprocal(acc[:, :, D:W], acc[:, :, D:W]))
                            ch.link(v.tensor_tensor(acc[:, :, D:W], acc[:, :, D:W], over(has, H), ALU.mult))
                            ch.link(v.tensor_tensor(result[:, tiles, :].rearrange("p t (h d) -> p t h d", h=H),
                                                    acc[:, :, 0:D].rearrange("p t (h d) -> p t h d", h=H),
                                                    acc[:, :, D:W].unsqueeze(3).to_broadcast([P, NG, H, D // H]), ALU.mult))
                        v.sem_inc(done.sem, 1)
                        ch.close()

            @block.scalar
            def _(act):
                if soft:
                    with act.Fori(0, NNG) as i:
                        act.wait_ge(ask.sem, i + ask.at(1))
                        act.activation(mul[:, :, :, :], dif[:, :, :, :], ACT.Exp).then_inc(ex.sem, 1)
        for k in range(2):
            ld[k].passed(32 * (NNG // 2))
            got[k].passed(32 * NG * (NNG // 2))
        done.passed(NNG)
        dv.passed(per * NNG)
        if soft:
            ask.passed(NNG)
            ex.passed(NNG)


def elementwise(pr, steps):
    dv = pr.count("ew_steps")
    with pr.nc.Block() as block:
        @block.vector
        def _(v):
            ch = Chain(v, dv)
            for step in steps:
                ch.link(step(v))
    dv.passed(len(steps))


def node_mlp(pr, C, msgs, h, Wn1, bn1, Wn2, bn2, result):
    nc = pr.nc
    with ExitStack() as ctx:
        w1m = pr.sb("nm_w1m", [P, P], F32, ctx)
        w1h = pr.sb("nm_w1h", [D, P], F32, ctx)
        w2 = pr.sb("nm_w2", [P, D], F32, ctx)
        b1 = pr.sb("nm_b1", [P, 1], F32, ctx)
        b2 = pr.sb("nm_b2", [P, D], F32, ctx)
        sm = pr.sb("nm_sm", [P, NG, P], F32, ctx)
        sh = pr.sb("nm_sh", [P, NG, D], F32, ctx)
        mT = pr.sb("nm_mT", [P, NG * P], F32, ctx)
        hT = pr.sb("nm_hT", [D, NG * P], F32, ctx)
        hid = pr.sb("nm_hid", [P, NG * P], F32, ctx)
        pm = pr.ps("nm_pm", [P, 1024], ctx)
        ph = pr.ps("nm_ph", [P, 1024], ctx)
        p1 = pr.ps("nm_p1", [P, 1024], ctx)
        p2 = pr.ps("nm_p2", [P, 512], ctx)
        ld, stg, tr, mv, l1, l1a, l2, fin = (pr.count("nm_" + x) for x in ("loaded", "staged", "turned", "moved", "first",
                                                                          "activated", "second", "finished"))
        with nc.Block() as block:
            @block.sync
            def _(sp):
                sp.dma_start(w1m[0:D, :], Wn1[D:2 * D, :]).then_inc(ld.sem, 16)
                sp.dma_start(w1m[D:P, :], Wn1[0:D, :]).then_inc(ld.sem, 16)
                sp.dma_start(w1h[:, :], Wn1[2 * D:3 * D, :]).then_inc(ld.sem, 16)
                sp.dma_start(w2[:, :], Wn2).then_inc(ld.sem, 16)
                with nc.allow_non_contiguous_dma(reason="a bias, a word a partition"):
                    sp.dma_start(b1[:, :], bn1.unsqueeze(1)).then_inc(ld.sem, 16)
                sp.dma_start(b2[:, :], bn2.unsqueeze(0).to_broadcast([P, D])).then_inc(ld.sem, 16)

            @block.vector
            def _(v):
                v.wait_ge(ld.sem, 96)
                with v.Fori(0, NNG) as i:
                    tiles = bass.ds(NG * i, NG)
                    v.tensor_copy(sm[:, :, :], msgs[:, tiles, :])
                    v.tensor_copy(sh[:, :, :], h[:, tiles, :]).then_inc(stg.sem, 1)
                    v.wait_ge(l2.sem, i + 1)
                    v.tensor_tensor(result[:, tiles, :], p2[:, 0:NG * D].rearrange("p (t d) -> p t d", t=NG),
                                    b2[:, :].unsqueeze(1).to_broadcast([P, NG, D]), ALU.add).then_inc(fin.sem, 1)

            @block.tensor
            def _(pe):
                pe.wait_ge(ld.sem, 96)
                with pe.Fori(0, NNG) as i:
                    pe.wait_ge(stg.sem, i + 1)
                    for t in range(NG):
                        pe.transpose(pm[:, t * P:(t + 1) * P], sm[:, t, :], C.ident[:, :])
                        ins = pe.transpose(ph[0:D, t * P:(t + 1) * P], sh[:, t, :], C.ident[:, :])
                    ins.then_inc(tr.sem, 1)
                    pe.wait_ge(mv.sem, i * 2 + 2)
                    for a, b in ((0, 512), (512, NG * P)):
                        pe.matmul(p1[:, a:b], w1m[:, :], mT[:, a:b], start=True, stop=False)
                        ins = pe.matmul(p1[:, a:b], w1h[:, :], hT[:, a:b], start=False, stop=True)
                    ins.then_inc(l1.sem, 1)
                    pe.wait_ge(l1a.sem, i + 1)
                    for t in range(NG):
                        ins = pe.matmul(p2[:, t * D:(t + 1) * D], hid[:, t * P:(t + 1) * P], w2[:, :], start=True, stop=True)
                    ins.then_inc(l2.sem, 1)

            @block.scalar
            def _(act):
                act.wait_ge(ld.sem, 96)
                with act.Fori(0, NNG) as i:
                    act.wait_ge(tr.sem, i + 1)
                    act.activation(mT[:, :], pm[:, 0:NG * P], ACT.Copy).then_inc(mv.sem, 1)
                    act.activation(hT[:, :], ph[0:D, 0:NG * P], ACT.Copy).then_inc(mv.sem, 1)
                    act.wait_ge(l1.sem, i + 1)
                    act.activation(hid[:, :], p1[:, 0:NG * P], ACT.Relu, bias=b1[:, :]).then_inc(l1a.sem, 1)


def load_nodes(pr, C, A, x):
    ld, sq = pr.count("x_loaded"), pr.count("deg_rooted")
    with pr.nc.Block() as block:
        @block.sync
        def _(sp):
            sp.dma_start(x[:, :, :], A["x"].rearrange("(t p) d -> p t d", p=P)).then_inc(ld.sem, 16)
            sp.wait_ge(ld.sem, 16)

        @block.vector
        def _(v):
            v.tensor_scalar(C.deg_scale[:, :], C.cnt_d[:, :], 1.0, None, ALU.max).then_inc(sq.sem, 1)
            v.wait_ge(sq.sem, 2)
            v.reciprocal(C.deg_scale[:, :], C.deg_scale[:, :]).then_inc(sq.sem, 1)
            v.wait_ge(sq.sem, 3)
            v.tensor_tensor(C.deg_scale[:, :], C.deg_scale[:, :], C.has_d[:, :], ALU.mult)

        @block.scalar
        def _(act):
            act.wait_ge(sq.sem, 1)
            act.activation(C.deg_scale[:, :], C.deg_scale[:, :], ACT.Sqrt).then_inc(sq.sem, 1)


def gnn(nc, A, out):
    with ExitStack() as ctx:
        pr = Program(nc, ctx)

        class C:
            pass
        C.src, C.dst, C.edge_attr = A["src"], A["dst"], A["edge_attr_32"]
        C.src_col_i = pr.dram("src_col_i", (P, ET), I32)
        C.src_col = pr.dram("src_col", (P, ET))
        C.dst_col = pr.dram("dst_col", (P, ET))
        C.fk_dst = pr.dram("fk_dst", (ET, P + 1))
        C.sorted_rows = pr.dram("sorted_rows", (NE, D + 9))
        C.src_ends = pr.dram("src_ends", (2, ET))
        C.heads8, C.heads128 = (pr.dram(f"heads{w}", (NE, w)) for w in (8, 2 * D))
        C.heads72, C.heads64 = C.heads128[:, 0:D + 8], C.heads128[:, 0:D]
        C.ix_dst, C.ix_src = (pr.dram(n, (3, P, NT), I32) for n in ("ix_dst", "ix_src"))
        C.cnt_d, C.start_d, C.has_d, C.spans_d = (pr.sb(n + "_d", [P, NT]) for n in ("cnt", "start", "has", "spans"))
        C.cnt_s, C.start_s, C.has_s, C.spans_s = (pr.sb(n + "_s", [P, NT]) for n in ("cnt", "start", "has", "spans"))
        C.deg_scale = pr.sb("deg_scale", [P, NT])
        C.keep_d, C.keep_s = (pr.sb(n, [P, ET]) for n in ("keep_d", "keep_s"))
        C.first_d, C.first_s = (pr.sb(n, [RB, NB], I32) for n in ("first_d", "first_s"))
        x, h = (pr.sb(n, [P, NT, D]) for n in ("x", "h"))
        T0, S0 = pr.dram("T0", (NN, D + 8)), pr.dram("S0", (NN, 8))
        constants(pr, C)
        with ExitStack() as early:
            C.lo_s, C.hi_s, C.lo_d, C.hi_d = (pr.sb(n, [P, ET], BF16, early) for n in ("lo_s", "hi_s", "lo_d", "hi_d"))
            with ExitStack() as filling:
                zeros = pr.sb("zeros", [P, 4096], F32, filling)
                C.seg_sb = pr.sb("seg_sb", [P, ET], F32, filling)
                read_ids(pr, C)
                zero_heads(pr, zeros, (C.heads8, C.heads128))
                count_nodes(pr, C)
                node_bounds(pr, C)
                zeros_written(pr)
            tile_starts(pr, C, 0)
            load_nodes(pr, C, A, x)
            layernorm_relu(pr, C, x, h)
            project(pr, C, h, [(A["L0_gnn_W"], 0)], [], [(T0, 0, 0, D + 8), (S0, 0, D + 8, 8)],
                    heads=[(C.heads128, 0, 2 * D, C.ix_dst[0]), (C.heads8, D + 8, 8, C.ix_src[0])],
                    scores=(A["L0_gnn_dst_attn"], A["L0_gnn_src_attn"]))
            head_rows(pr, C, T0, D + 8, C.heads72, C.first_d)
            sort_by_src(pr, C)
        sorted_segments(pr, C)
        tile_starts(pr, C, 1)
        st = pr.count("y_stored")

        def add_to(dst, a, b):
            return lambda v: v.tensor_tensor(dst[:, :, :], a[:, :, :], b[:, :, :], ALU.add)

        head_rows(pr, C, S0, 8, C.heads8, C.first_s)
        part0, carry0 = pr.dram("part0", (NE, D + 16)), pr.dram("carry0", (ET, 2 * (D + 8)))
        gat_edges(pr, C, C.heads8, part0)
        carry(pr, C, "softmax", part0, carry0, C.keep_s, 8)
        node_results(pr, C, "softmax", part0, carry0, C.ix_src, C.has_s, C.spans_s, h, 8)
        elementwise(pr, [add_to(x, x, h)])
        skip = pr.sb("skip", [P, NT, D])

        layernorm_relu(pr, C, x, h)
        T1, B1 = pr.dram("T1", (NN, 3 * D)), pr.dram("B1", (NN, 2 * D))
        We1 = A["L1_gnn_We1"]
        project(pr, C, h, [(We1[0:D, :], 0), (We1[D:2 * D, :], 2 * D)], [(A["L1_gnn_be1"], 2 * D)],
                [(T1, 0, 0, 2 * D), (T1, 2 * D, None, D), (B1, 0, 2 * D, 2 * D)],
                heads=[(C.heads128, 2 * D, 2 * D, C.ix_dst[0])])
        head_rows(pr, C, B1, 2 * D, C.heads128, C.first_d)
        part1, carry1 = pr.dram("part1", (NE, 2 * D)), pr.dram("carry1", (ET, 2 * D))
        mlp_edges(pr, C, T1, C.heads128, part1, A["L1_gnn_be2"], A["L1_gnn_We2"])
        carry(pr, C, "sum_max", part1, carry1, C.keep_d)
        with ExitStack() as l1:
            msgs = pr.sb("msgs", [P, NT, 2 * D], F32, l1)
            node_results(pr, C, "sum_max", part1, carry1, C.ix_dst, C.has_d, C.spans_d, msgs)
            node_mlp(pr, C, msgs, h, A["L1_gnn_Wn1"], A["L1_gnn_bn1"], A["L1_gnn_Wn2"], A["L1_gnn_bn2"], skip)
        elementwise(pr, [add_to(x, x, skip), add_to(x, x, h)])

        layernorm_relu(pr, C, x, h)
        part2, carry2 = pr.dram("part2", (NE, D + 2)), pr.dram("carry2", (ET, 2 * (D + 1)))
        for layer in ("1", "2"):
            w = {n: A["L2_gnn_" + n + layer] for n in ("Wq", "bq", "Wk", "bk", "Wv", "bv", "We", "Ws", "bs")}
            KV, Q = pr.dram("KV" + layer, (NN, 2 * D)), pr.dram("Q" + layer, (NN, D))
            project(pr, C, h, [(w["W" + n], D * j) for j, n in enumerate("qkvs")], [(w["b" + n], D * j) for j, n in enumerate("qkvs")],
                    [(KV, 0, D, 2 * D), (Q, 0, 0, D)], heads=[(C.heads128, 0, 2 * D, C.ix_dst[0])], keep=(skip, 3 * D))
            head_rows(pr, C, Q, D, C.heads64, C.first_d)
            softmax_edges(pr, C, "t" + layer, KV, C.dst_col, C.src_col_i, C.heads64, part2, w["We"])
            carry(pr, C, "softmax", part2, carry2, C.keep_d, 1)
            node_results(pr, C, "softmax", part2, carry2, C.ix_dst, C.has_d, C.spans_d, h, 1, 1e-16)
            if layer == "1":
                elementwise(pr, [add_to(h, h, skip), lambda v: v.tensor_scalar(h[:, :, :], h[:, :, :], 0.0, None, ALU.max)])
            else:
                elementwise(pr, [add_to(x, x, h), add_to(x, x, skip)])

        layernorm_relu(pr, C, x, h)
        HN = pr.dram("HN", (NN, D))
        project(pr, C, h, [(A["L3_gnn_W"], 0)], [(A["L3_gnn_b"], 0)], [(HN, 0, 0, D)], row_scale=C.deg_scale)
        part3, carry3 = pr.dram("part3", (NE, D)), pr.dram("carry3", (ET, D))
        gcn_edges(pr, C, HN, part3)
        carry(pr, C, "sum", part3, carry3, C.keep_d)
        node_results(pr, C, "sum", part3, carry3, C.ix_dst, C.has_d, C.spans_d, h)
        wide = C.deg_scale[:, :].unsqueeze(2).to_broadcast([P, NT, D])
        elementwise(pr, [lambda v: v.tensor_tensor(h[:, :, :], h[:, :, :], wide, ALU.mult), add_to(x, x, h)])
        with nc.Block() as block:
            @block.sync
            def _(sp):
                full = N_NODES // P
                sp.dma_start(out[0:full * P, :].rearrange("(t p) d -> p t d", p=P), x[:, 0:full, :]).then_inc(st.sem, 16)
                sp.dma_start(out[full * P:N_NODES, :], x[0:N_NODES - full * P, full, :]).then_inc(st.sem, 16)
                sp.wait_ge(st.sem, 32)


def kernel(**inputs):
    import concourse.bacc as _bacc
    from concourse import mybir as _mybir
    from concourse.bass_utils import run_bass_kernel_spmd as _run

    nc = _bacc.Bacc("TRN2", target_bir_lowering=False, num_devices=1)
    laid = {k: np.asarray(v) for k, v in inputs.items()}
    for k in ("src", "dst"):
        laid[k] = np.pad(laid[k], (0, NE - N_EDGES), constant_values=NN - 1)
    laid["x"] = np.pad(laid["x"], ((0, NN - N_NODES), (0, 0)))
    laid["edge_attr_32"] = np.pad(laid["edge_attr_32"], ((0, NE - N_EDGES), (0, 0)))
    laid["L0_gnn_W"] = laid["L0_gnn_W"].T
    laid["L3_gnn_W"] = laid["L3_gnn_W"].T
    arrays, A = {}, {}
    for k, v in laid.items():
        arrays["in_" + k] = np.ascontiguousarray(v)
        A[k] = nc.dram_tensor("in_" + k, v.shape, _mybir.dt.from_np(v.dtype), kind="ExternalInput").ap()
    out = nc.dram_tensor("out0", (N_NODES, D), _mybir.dt.float32, kind="ExternalOutput").ap()
    gnn(nc, A, out)
    r = _run(nc, [arrays], core_ids=[0])
    return r.results[0]["out0"]
```
